# Optimizing a Trainium2 kernel written in Bass

```python
import numpy as np
import jax
import jax.numpy as jnp

def _softmax(x, axis=-1):
    return jax.nn.softmax(x, axis=axis)

def _gelu(x):
    return jax.nn.gelu(x, approximate=True)

def _silu(x):
    return jax.nn.silu(x)

def _sigmoid(x):
    return jax.nn.sigmoid(x)

def _layernorm(x, axis=-1, eps=1e-05):
    m = jnp.mean(x, axis=axis, keepdims=True)
    v = jnp.var(x, axis=axis, keepdims=True)
    return (x - m) / jnp.sqrt(v + eps)

def _scatter_add(tgt, idx, src, axis=0):
    return tgt.at[idx].add(src)

def _segment_sum(src, seg, n):
    return jax.ops.segment_sum(src, seg, n)
kernel_name = 'mk_seq_postln_d1_jaxref_r8_4de9b0'

def setup_inputs(seed: int=0):
    np.random.seed(seed)
    _w = jnp.asarray

    def _L0_attn_setup():
        import jax, jax.numpy as jnp
        import numpy as np
        B, N, DIM = (4, 128, 128)
        HEADS, DH = (16, 64)
        INNER = HEADS * DH
        PROJ_H = max(16, DH // 8)
        TOP_K = 32
        TEMP = 1.0
        SCALE = DH ** (-0.5)
        LN_EPS = 1e-05

        def _soma_gate(token_feat, ln_g, ln_b, w1, b1, w2, b2):
            mu = token_feat.mean(axis=-1, keepdims=True)
            var = token_feat.var(axis=-1, keepdims=True)
            H = (token_feat - mu) * jax.lax.rsqrt(var + LN_EPS) * ln_g + ln_b
            h = jax.nn.gelu(H @ w1.T + b1, approximate=False)
            scores = (h @ w2.T + b2)[..., 0]
            scores = scores / (TEMP + 1e-12)
            topk_vals, topk_idx = jax.lax.top_k(scores, TOP_K)
            b_idx = jnp.arange(scores.shape[0])[:, None]
            scores = jnp.full_like(scores, -1000000000.0).at[b_idx, topk_idx].set(topk_vals)
            return jax.nn.sigmoid(scores)
        key = jax.random.key(seed)
        ks = jax.random.split(key, 9)
        s = 0.02
        return {'x': jax.random.normal(ks[0], (B, N, DIM), dtype=jnp.float32), 'w_qkv': jax.random.normal(ks[1], (3 * INNER, DIM), dtype=jnp.float32) * s, 'w_out': jax.random.normal(ks[2], (DIM, INNER), dtype=jnp.float32) * s, 'b_out': jnp.zeros((DIM,), dtype=jnp.float32), 'ln_g': jnp.ones((DH,), dtype=jnp.float32), 'ln_b': jnp.zeros((DH,), dtype=jnp.float32), 'w1': jax.random.normal(ks[3], (PROJ_H, DH), dtype=jnp.float32) * s, 'b1': jnp.zeros((PROJ_H,), dtype=jnp.float32), 'w2': jax.random.normal(ks[4], (1, PROJ_H), dtype=jnp.float32) * s, 'b2': jnp.zeros((1,), dtype=jnp.float32)}
    _L0_attn_in = _L0_attn_setup()

    def _L0_ffn_setup():
        import jax, jax.numpy as jnp
        import numpy as np
        EMB = 128
        HEADS = 16
        SEQ = 256
        LATENT = 64
        N_EXP = 8
        TOP_K = 2
        EXP_DIM = 256
        BATCH = 2
        EPS = 1e-06

        def _rmsnorm(x, g):
            return x * jax.lax.rsqrt(jnp.mean(x * x, axis=-1, keepdims=True) + EPS) * g

        def _mla(h, Wq, Wdkv, Wuk, Wuv, Wo):
            B, S, D = h.shape
            hd = D // HEADS
            q = (h @ Wq).reshape(B, S, HEADS, hd)
            c = h @ Wdkv
            k = (c @ Wuk).reshape(B, S, HEADS, hd)
            v = (c @ Wuv).reshape(B, S, HEADS, hd)
            scores = jnp.einsum('bqhd,bkhd->bhqk', q, k) / jnp.sqrt(jnp.asarray(hd, h.dtype))
            causal = jnp.tril(jnp.ones((S, S), bool))
            scores = jnp.where(causal, scores, jnp.asarray(-1000000000.0, h.dtype))
            a = jax.nn.softmax(scores, axis=-1)
            out = jnp.einsum('bhqk,bkhd->bqhd', a, v).reshape(B, S, D)
            return out @ Wo

        def _moe(h, gate_w, w1, w2):
            B, S, D = h.shape
            t = h.reshape(B * S, D)
            logits = t @ gate_w
            top_v, top_i = jax.lax.top_k(logits, TOP_K)
            gates = jax.nn.softmax(top_v, axis=-1)
            T = t.shape[0]
            combine = jnp.zeros((T, N_EXP), t.dtype).at[jnp.arange(T)[:, None], top_i].add(gates)
            hid = jax.nn.silu(jnp.einsum('td,edh->teh', t, w1))
            ye = jnp.einsum('teh,ehd->ted', hid, w2)
            out = jnp.einsum('te,ted->td', combine, ye)
            return out.reshape(B, S, D)
        key = jax.random.key(seed)
        ks = jax.random.split(key, 12)
        s = 0.02
        return {'x': jax.random.normal(ks[0], (BATCH, SEQ, EMB), jnp.float32), 'g1': jnp.ones((EMB,), jnp.float32), 'Wq': jax.random.normal(ks[1], (EMB, EMB), jnp.float32) * s, 'Wdkv': jax.random.normal(ks[2], (EMB, LATENT), jnp.float32) * s, 'Wuk': jax.random.normal(ks[3], (LATENT, EMB), jnp.float32) * s, 'Wuv': jax.random.normal(ks[4], (LATENT, EMB), jnp.float32) * s, 'Wo': jax.random.normal(ks[5], (EMB, EMB), jnp.float32) * s, 'g2': jnp.ones((EMB,), jnp.float32), 'gate_w': jax.random.normal(ks[6], (EMB, N_EXP), jnp.float32) * s, 'w1': jax.random.normal(ks[7], (N_EXP, EMB, EXP_DIM), jnp.float32) * s, 'w2': jax.random.normal(ks[8], (N_EXP, EXP_DIM, EMB), jnp.float32) * s}
    _L0_ffn_in = _L0_ffn_setup()
    _d = {'L0_attn_x': _L0_attn_in['x'], 'L0_attn_w_qkv': _L0_attn_in['w_qkv'], 'L0_attn_w_out': _L0_attn_in['w_out'], 'L0_attn_b_out': _L0_attn_in['b_out'], 'L0_attn_ln_g': _L0_attn_in['ln_g'], 'L0_attn_ln_b': _L0_attn_in['ln_b'], 'L0_attn_w1': _L0_attn_in['w1'], 'L0_attn_b1': _L0_attn_in['b1'], 'L0_attn_w2': _L0_attn_in['w2'], 'L0_attn_b2': _L0_attn_in['b2'], 'L0_ffn_g1': _L0_ffn_in['g1'], 'L0_ffn_Wq': _L0_ffn_in['Wq'], 'L0_ffn_Wdkv': _L0_ffn_in['Wdkv'], 'L0_ffn_Wuk': _L0_ffn_in['Wuk'], 'L0_ffn_Wuv': _L0_ffn_in['Wuv'], 'L0_ffn_Wo': _L0_ffn_in['Wo'], 'L0_ffn_g2': _L0_ffn_in['g2'], 'L0_ffn_gate_w': _L0_ffn_in['gate_w'], 'L0_ffn_w1': _L0_ffn_in['w1'], 'L0_ffn_w2': _L0_ffn_in['w2']}
    _x0 = _d['L0_attn_x']
    _d['L0_attn_x'] = jax.random.normal(jax.random.fold_in(jax.random.key(seed), 1), (8, 512, 128), dtype=_x0.dtype)
    del _x0
    return _d

def reference(L0_attn_x, L0_attn_w_qkv, L0_attn_w_out, L0_attn_b_out, L0_attn_ln_g, L0_attn_ln_b, L0_attn_w1, L0_attn_b1, L0_attn_w2, L0_attn_b2, L0_ffn_g1, L0_ffn_Wq, L0_ffn_Wdkv, L0_ffn_Wuk, L0_ffn_Wuv, L0_ffn_Wo, L0_ffn_g2, L0_ffn_gate_w, L0_ffn_w1, L0_ffn_w2):

    def _L0_attn_ref(x, w_qkv, w_out, b_out, ln_g, ln_b, w1, b1, w2, b2):
        import jax, jax.numpy as jnp
        import numpy as np
        B, N, DIM = (4, 128, 128)
        HEADS, DH = (16, 64)
        INNER = HEADS * DH
        PROJ_H = max(16, DH // 8)
        TOP_K = 32
        TEMP = 1.0
        SCALE = DH ** (-0.5)
        LN_EPS = 1e-05

        def _soma_gate(token_feat, ln_g, ln_b, w1, b1, w2, b2):
            mu = token_feat.mean(axis=-1, keepdims=True)
            var = token_feat.var(axis=-1, keepdims=True)
            H = (token_feat - mu) * jax.lax.rsqrt(var + LN_EPS) * ln_g + ln_b
            h = jax.nn.gelu(H @ w1.T + b1, approximate=False)
            scores = (h @ w2.T + b2)[..., 0]
            scores = scores / (TEMP + 1e-12)
            topk_vals, topk_idx = jax.lax.top_k(scores, TOP_K)
            b_idx = jnp.arange(scores.shape[0])[:, None]
            scores = jnp.full_like(scores, -1000000000.0).at[b_idx, topk_idx].set(topk_vals)
            return jax.nn.sigmoid(scores)
        Bx, Nx, _ = x.shape
        qkv = x @ w_qkv.T
        q, k, v = jnp.split(qkv, 3, axis=-1)
        to_heads = lambda t: t.reshape(Bx, Nx, HEADS, DH).transpose(0, 2, 1, 3)
        q, k, v = (to_heads(q), to_heads(k), to_heads(v))
        dots = jnp.einsum('bhid,bhjd->bhij', q, k) * SCALE
        q_mean = q.mean(axis=1)
        gate = _soma_gate(q_mean, ln_g, ln_b, w1, b1, w2, b2)
        dots = dots * (gate[:, None, :, None] * gate[:, None, None, :])
        attn = jax.nn.softmax(dots, axis=-1)
        out = jnp.einsum('bhij,bhjd->bhid', attn, v)
        out = out.transpose(0, 2, 1, 3).reshape(Bx, Nx, INNER)
        return out @ w_out.T + b_out

    def _L0_ffn_ref(x, g1, Wq, Wdkv, Wuk, Wuv, Wo, g2, gate_w, w1, w2):
        import jax, jax.numpy as jnp
        import numpy as np
        EMB = 128
        HEADS = 16
        SEQ = 256
        LATENT = 64
        N_EXP = 8
        TOP_K = 2
        EXP_DIM = 256
        BATCH = 2
        EPS = 1e-06

        def _rmsnorm(x, g):
            return x * jax.lax.rsqrt(jnp.mean(x * x, axis=-1, keepdims=True) + EPS) * g

        def _mla(h, Wq, Wdkv, Wuk, Wuv, Wo):
            B, S, D = h.shape
            hd = D // HEADS
            q = (h @ Wq).reshape(B, S, HEADS, hd)
            c = h @ Wdkv
            k = (c @ Wuk).reshape(B, S, HEADS, hd)
            v = (c @ Wuv).reshape(B, S, HEADS, hd)
            scores = jnp.einsum('bqhd,bkhd->bhqk', q, k) / jnp.sqrt(jnp.asarray(hd, h.dtype))
            causal = jnp.tril(jnp.ones((S, S), bool))
            scores = jnp.where(causal, scores, jnp.asarray(-1000000000.0, h.dtype))
            a = jax.nn.softmax(scores, axis=-1)
            out = jnp.einsum('bhqk,bkhd->bqhd', a, v).reshape(B, S, D)
            return out @ Wo

        def _moe(h, gate_w, w1, w2):
            B, S, D = h.shape
            t = h.reshape(B * S, D)
            logits = t @ gate_w
            top_v, top_i = jax.lax.top_k(logits, TOP_K)
            gates = jax.nn.softmax(top_v, axis=-1)
            T = t.shape[0]
            combine = jnp.zeros((T, N_EXP), t.dtype).at[jnp.arange(T)[:, None], top_i].add(gates)
            hid = jax.nn.silu(jnp.einsum('td,edh->teh', t, w1))
            ye = jnp.einsum('teh,ehd->ted', hid, w2)
            out = jnp.einsum('te,ted->td', combine, ye)
            return out.reshape(B, S, D)
        x = x + _mla(_rmsnorm(x, g1), Wq, Wdkv, Wuk, Wuv, Wo)
        x = x + _moe(_rmsnorm(x, g2), gate_w, w1, w2)
        return x
    x = L0_attn_x
    x = _layernorm(x + _L0_attn_ref(x, L0_attn_w_qkv, L0_attn_w_out, L0_attn_b_out, L0_attn_ln_g, L0_attn_ln_b, L0_attn_w1, L0_attn_b1, L0_attn_w2, L0_attn_b2), axis=-1)
    x = _layernorm(x + _L0_ffn_ref(x, L0_ffn_g1, L0_ffn_Wq, L0_ffn_Wdkv, L0_ffn_Wuk, L0_ffn_Wuv, L0_ffn_Wo, L0_ffn_g2, L0_ffn_gate_w, L0_ffn_w1, L0_ffn_w2), axis=-1)
    return x

_drawn_inputs = setup_inputs


def setup_inputs(seed=0):
    import zlib

    import numpy as np

    out = dict(_drawn_inputs(seed))
    spreads = {'L0_attn_b_out': (0.0, 0.1),
     'L0_attn_ln_g': (1.0, 0.6),
     'L0_attn_ln_b': (0.0, 0.8),
     'L0_attn_b1': (0.0, 0.8),
     'L0_ffn_g1': (1.0, 0.6),
     'L0_ffn_g2': (1.0, 0.6)}
    factors = {'L0_attn_w_qkv': 8.0,
     'L0_attn_w_out': 8.0,
     'L0_attn_w1': 8.0,
     'L0_attn_w2': 8.0,
     'L0_ffn_Wq': 8.0,
     'L0_ffn_Wdkv': 8.0,
     'L0_ffn_Wuk': 8.0,
     'L0_ffn_Wuv': 8.0,
     'L0_ffn_Wo': 8.0,
     'L0_ffn_gate_w': 4.802,
     'L0_ffn_w1': 4.219,
     'L0_ffn_w2': 4.203}
    for name, (base, spread) in spreads.items():
        noise = np.random.default_rng([zlib.crc32(name.encode()), seed]).standard_normal(out[name].shape)
        drawn = base * np.exp(spread * noise) if base else spread * noise
        out[name] = jnp.asarray(drawn.astype(out[name].dtype))
    for name, factor in factors.items():
        out[name] = (out[name] * factor).astype(out[name].dtype)
    return out
```

```python
from contextlib import ExitStack

import numpy as np

import concourse.bass as bass
from concourse import mybir

ALU = mybir.AluOpType
ACT = mybir.ActivationFunctionType
AX = mybir.AxisListType.X
F32 = mybir.dt.float32
F32R = mybir.dt.float32r
BF16 = mybir.dt.bfloat16
NEG_MAX = float(np.finfo(np.float32).min)
ds = bass.ds

B, T, D = 8, 512, 128
P = 128
C = T // P
NC = B * C
H, DH = 16, 64
INNER = H * DH
NI = INNER // P
TOPK = 32
HB = P // TOPK
NH = B // HB
GH = 16
GR0 = 32
LN_EPS = 1e-5
RMS_EPS = 1e-6
MH, MD = 16, 8
LAT = 64
NG = MH // 4
R = 32
SHIFT = 3 * MD
NE, EH = 8, 256
BIG = -1e30


class Chain:

    def __init__(self, eng, sem):
        self.eng, self.sem, self.n, self.base = eng, sem, 0, 0

    def __call__(self, ins):
        self.n += 1
        ins.then_inc(self.sem, 1)
        self.eng.wait_ge(self.sem, self.base + self.n)


def head_at(k):
    return 2 * (k % (H // 2)) + k // (H // 2)


def gated_attention(nc, keep, x, xT, wqkvT, woutT, b_out, ln_g, ln_b, w1gT, b1g, w2gT, b2g):
    X, ident, mhalf, r1 = keep["X"], keep["ident"], keep["mhalf"], keep["r1"]
    ctx = ExitStack()
    with ctx:
        def sb(name, shape, dt=F32):
            return ctx.enter_context(nc.sbuf_tensor(name, shape, dt))

        def sem(name):
            return ctx.enter_context(nc.semaphore(name))

        XT = sb("XT", [P, B * T])
        WQKV = sb("WQKV", [P, 3 * INNER])
        WOUT = sb("WOUT", [P, NI, D])
        Fc = sb("Fc", [P, 2, T])
        sq = sb("sq", [P, 2, T])
        var = sb("var", [64, B // 2, T])
        hid = sb("hid", [64, B // 2, T])
        wsum = sb("wsum", [P, DH])
        wmean = sb("wmean", [P, 2])
        Wc = sb("Wc", [P, DH])
        w1raw = sb("w1raw", [P, 64])
        w1g = sb("w1g", [P, 64])
        gcol = sb("gcol", [P, 1])
        bcol = sb("bcol", [P, 1])
        ones64 = sb("ones64", [P, 64])
        b1col = sb("b1col", [64, 1])
        cbias = sb("cbias", [64, 1])
        w2col = sb("w2col", [64, 1])
        w2sel = sb("w2sel", [64, B // 2, B])
        b2col = sb("b2col", [B, 1])
        bout = sb("bout", [1, D])
        ones8 = sb("ones8", [1, B])
        selb = sb("selb", [B, B, P])
        selh = sb("selh", [B, NH, P])
        rcol = sb("rcol", [P, 1])
        iota32 = sb("iota32", [P, TOPK])
        scores = sb("scores", [B, T])
        cur = sb("cur", [B, 2, T])
        top8 = sb("top8", [B, 8])
        gv = sb("gv", [B, T])
        ones512 = sb("ones512", [B, T])
        mask = sb("mask", [B, T])
        pos = sb("pos", [B, T])
        slot = sb("slot", [B, T])
        slotT = sb("slotT", [P, B, C])
        gT = sb("gT", [P, B, C])
        GR = sb("GR", [P, NC, 2 * TOPK + 1])
        SR = sb("SR", [P, NH, T])
        Xg = sb("Xg", [P, B * TOPK])
        Xc = sb("Xc", [P, B * TOPK])
        xm = sb("xm", [P, B])
        QK = sb("QK", [P, 2 * NI, B * TOPK])
        V = sb("V", [P, NH, INNER])
        S0 = sb("S0", [P, H, TOPK])
        mx = sb("mx", [P, 6, H])
        BD = sb("BD", [P, H, P])
        BDT = sb("BDT", [P, H, P])
        OT = sb("OT", [P, NI, P])
        vmT = sb("vmT", [P, NI, B])
        base = sb("base", [B, D])
        base_all = sb("base_all", [P, B, D])
        delta = sb("delta", [P, NH, D])
        st6 = sb("st6", [P, C, 6])
        mv = sb("mv", [P, NC, 2])
        rs = sb("rs", [P, NC])
        ve = sb("ve", [P, NC])
        y = XT[:, :].rearrange("p (i d) -> p i d", d=D)
        bank = [ctx.enter_context(nc.psum_tensor(f"a{i}", [P, 512], F32)) for i in range(8)]

        ld_gate, ld_zero, ld_x, ld_w = sem("ld_gate"), sem("ld_zero"), sem("ld_x"), sem("ld_w")
        ld_xT = [sem(f"ld_xT{j}") for j in range(4)]
        ld_wq = sem("ld_wq")
        zeroed, consts = sem("zeroed"), sem("consts")
        wc_ready, cb_ps = sem("wc_ready"), sem("cb_ps")
        f_ps, f_sb, g_ps, g_used, std_ready, hpre, gelu, sc_ps = (
            sem(n) for n in ("f_ps", "f_sb", "g_ps", "g_used", "std_ready", "hpre", "gelu", "sc_ps"))
        sc_sb, sig, slot_ready, slotT_ps, slotT_sb, sr_ps, sr_sb, gr_ready = (
            sem(n) for n in ("sc_sb", "sig", "slot_ready", "slotT_ps", "slotT_sb", "sr_ps", "sr_sb", "gr_ready"))
        xs_ps, xs_sb, qk_ps, q_sb, k_sb, v_ps, v_sb, vm_ps, vm_sb, base_ps, base_sb = (
            sem(n) for n in ("xs_ps", "xs_sb", "qk_ps", "q_sb", "k_sb", "v_ps", "v_sb", "vm_ps", "vm_sb", "base_ps", "base_sb"))
        s_ps, s_sb, s_shift, s_exp, em, bd_ready, bdT_ps, bdT_sb, o_ps, o_sb, dl_ps, dl_sb = (
            sem(n) for n in ("s_ps", "s_sb", "s_shift", "s_exp", "em", "bd_ready", "bdT_ps", "bdT_sb", "o_ps", "o_sb",
                             "dl_ps", "dl_sb"))
        xb_ready = sem("xb_ready")
        at_ps, y_ready, ve_ready, rstd_ready = (sem(n) for n in ("at_ps", "y_ready", "ve_ready", "rstd_ready"))
        ms_ready, r1_ready = sem("ms_ready"), sem("r1_ready")
        dve_own, pool_own, act_own = sem("dve_own"), sem("pool_own"), sem("act_own")

        block = ctx.enter_context(nc.Block())

        @block.sync
        def _(sp):
            sp.dma_start(WQKV[:, 0:INNER], wqkvT[:, 0:INNER]).then_inc(ld_wq, 16)
            sp.dma_start(gcol[0:DH, :], ln_g).then_inc(ld_gate, 16)
            sp.dma_start(gcol[DH:P, :], ln_g).then_inc(ld_gate, 16)
            sp.dma_start(bcol[0:DH, :], ln_b).then_inc(ld_gate, 16)
            sp.dma_start(bcol[DH:P, :], ln_b).then_inc(ld_gate, 16)
            sp.dma_start(b2col[:, :], b2g).then_inc(ld_gate, 16)
            sp.wait_ge(zeroed, 1)
            for k in range(2):
                sp.dma_start(w1raw[DH * k:DH * k + DH, GR0 * k:GR0 * k + GH], w1gT).then_inc(ld_zero, 16)
                sp.dma_start(b1col[GR0 * k:GR0 * k + GH, :], b1g).then_inc(ld_zero, 16)
                sp.dma_start(w2col[GR0 * k:GR0 * k + GH, :], w2gT).then_inc(ld_zero, 16)
            for j in range(4):
                sp.dma_start(XT[:, 2 * T * j:2 * T * (j + 1)], xT[:, 2 * T * j:2 * T * (j + 1)]).then_inc(ld_xT[j], 16)
            sp.dma_start(X[:, :, :], x).then_inc(ld_x, 16)
            sp.dma_start(WQKV[:, INNER:3 * INNER], wqkvT[:, INNER:3 * INNER]).then_inc(ld_w, 16)
            sp.dma_start(WOUT[:, :, :], woutT.rearrange("(c p) d -> p c d", p=P)).then_inc(ld_w, 16)
            sp.dma_start(bout[:, :], b_out).then_inc(ld_w, 16)

        @block.gpsimd
        def _(pool):
            own = Chain(pool, pool_own)
            own(pool.memset(w1raw[:, :], 0.0))
            own(pool.memset(b1col[:, :], 0.0))
            pool.memset(w2col[:, :], 0.0).then_inc(zeroed, 1)
            pool.wait_ge(zeroed, 1)
            own(pool.memset(ident[:, :], 0.0))
            own(pool.memset(ones64[:, :], 0.0))
            own(pool.memset(w2sel[:, :, :], 0.0))
            own(pool.memset(selb[:, :, :], 0.0))
            own(pool.memset(selh[:, :, :], 1.0))
            own(pool.memset(ones8[:, :], 1.0))
            own(pool.memset(ones512[:, :], 1.0))
            own(pool.memset(mhalf[:, :], -0.5))
            own(pool.memset(keep["tri"][:, :, :], 1.0))
            own(pool.memset(ones64[0:DH, 0:GH], 1.0 / DH))
            own(pool.memset(ones64[DH:P, GR0:GR0 + GH], 1.0 / DH))
            own(pool.affine_select(out=ident[:, :], in_=ident[:, :], compare_op=ALU.not_equal, fill=1.0, base=0,
                               pattern=[[-1, P]], channel_multiplier=1))
            own(pool.affine_select(out=selb[:, :, :], in_=selb[:, :, :], compare_op=ALU.not_equal, fill=1.0, base=0,
                               pattern=[[-1, B], [0, P]], channel_multiplier=1))
            own(pool.affine_select(out=selh[:, :, :], in_=selh[:, :, :], compare_op=ALU.is_ge, fill=0.0, base=0,
                                   pattern=[[1, NH * P]], channel_multiplier=-TOPK))
            own(pool.affine_select(out=selh[:, :, :], in_=selh[:, :, :], compare_op=ALU.is_ge, fill=0.0,
                               base=TOPK - 1, pattern=[[-1, NH * P]], channel_multiplier=TOPK))
            own(pool.iota(iota32[:, :], pattern=[[1, TOPK]], base=0, channel_multiplier=0,
                      allow_small_or_imprecise_dtypes=True))
            for a in range(HB):
                own(pool.iota(rcol[TOPK * a:TOPK * (a + 1), :], pattern=[[0, 1]], base=0, channel_multiplier=1,
                          allow_small_or_imprecise_dtypes=True))
            own(pool.affine_select(out=keep["tri"][:, :, :], in_=keep["tri"][:, :, :], compare_op=ALU.is_gt, fill=0.0,
                               base=0, pattern=[[1, NE], [-1, NE]], channel_multiplier=0))
            pool.memset(BD[:, :, :], 0.0).then_inc(consts, 1)
            pool.wait_ge(consts, 1)
            own(pool.memset(keep["identb"][:, :], 0.0))
            own(pool.memset(keep["maskb"][:, :], 0.0))
            own(pool.memset(keep["qpad"][:, :, :].bitcast(F32), 0.0))
            own(pool.affine_select(out=keep["identb"][:, :], in_=keep["identb"][:, :], compare_op=ALU.not_equal,
                               fill=1.0, base=0, pattern=[[-1, P]], channel_multiplier=1))
            own(pool.affine_select(out=keep["maskb"][:, :], in_=keep["maskb"][:, :], compare_op=ALU.is_ge,
                               fill=BIG, base=0, pattern=[[-1, P]], channel_multiplier=1))
            pool.wait_ge(ld_x, 16)
            pool.wait_ge(base_sb, 2)
            for b in range(B):
                ts = slice(C * b, C * b + C)
                pool.tensor_tensor(y[:, ts, :], X[:, ts, :], base_all[:, b, :].unsqueeze(1).broadcast_to([P, C, D]),
                                   ALU.add).then_inc(xb_ready, 1)
            for b in range(B):
                cs = slice(C * b, C * b + C)
                pool.wait_ge(ve_ready, b + 1)
                pool.tensor_tensor(rs[:, cs], ve[:, cs], mhalf[:, cs], ALU.pow).then_inc(rstd_ready, 1)
            pool.wait_ge(ms_ready, 1)
            pool.tensor_tensor(r1[:, :], ve[:, :], mhalf[:, :], ALU.pow).then_inc(r1_ready, 1)

        @block.tensor
        def _(pe):
            mm = nc.tensor.matmul
            pe.wait_ge(ld_gate, 16 * 5)
            pe.wait_ge(ld_zero, 16 * 6)
            mm(bank[7][0:64, 0:1], w1raw[:, :], bcol[:, :], start=True, stop=True).then_inc(cb_ps, 1)
            pe.wait_ge(wc_ready, 1)
            pe.wait_ge(consts, 1)

            def features(j):
                pe.wait_ge(ld_xT[j], 16)
                if j >= 2:
                    pe.wait_ge(f_sb, 2 * (j - 1))
                for k in range(2):
                    b = 2 * j + k
                    last = mm(bank[j % 2][DH * k:DH * k + DH, :], Wc[:, :], XT[:, T * b:T * b + T],
                              start=True, stop=True)
                last.then_inc(f_ps, 1)

            features(0)
            for j in range(B // 2):
                if j + 1 < B // 2:
                    features(j + 1)
                pe.wait_ge(f_sb, 2 * j + 2)
                mm(bank[2 + j][0:64, :], w1g[:, :], Fc[:, j % 2, :], start=True, stop=True)
                if j == 1:
                    pe.wait_ge(wc_ready, 2)
                if j >= 2:
                    pe.wait_ge(g_used, j - 1)
                mm(bank[6 + j % 2][0:64, :], ones64[:, :], sq[:, j % 2, :], start=True, stop=True).then_inc(g_ps, 1)
            for j in range(B // 2):
                pe.wait_ge(gelu, j + 1)
                last = mm(bank[0][0:B, :], w2sel[:, j, :], hid[:, j, :], start=(j == 0), stop=(j == B // 2 - 1))
            last.then_inc(sc_ps, 1)

            pe.wait_ge(slot_ready, 1)
            pe.wait_ge(sig, 1)
            for c in range(C):
                nc.tensor.transpose(bank[1][:, B * c:B * c + B], slot[:, P * c:P * c + P], ident[0:B, 0:B])
                last = nc.tensor.transpose(bank[1][:, 64 + B * c:64 + B * c + B], gv[:, P * c:P * c + P],
                                           ident[0:B, 0:B])
            last.then_inc(slotT_ps, 1)
            for n in range(NH):
                last = mm(bank[2 + n][:, :], selh[:, n, :], slot[:, :], start=True, stop=True)
            last.then_inc(sr_ps, 1)

            pe.wait_ge(ld_x, 16)
            pe.wait_ge(gr_ready, 1)
            for b in range(B):
                o = (2 * TOPK + 1) * (b % HB)
                for c in range(C):
                    last = mm(bank[4 + b // HB][:, o:o + 2 * TOPK + 1], X[:, C * b + c, :], GR[:, C * b + c, :],
                              start=(c == 0), stop=(c == C - 1))
            last.then_inc(xs_ps, 1)

            pe.wait_ge(xs_sb, 1)
            pe.wait_ge(ld_w, 48)
            pe.wait_ge(sr_sb, 1)
            for i in range(NI):
                if i >= 4:
                    pe.wait_ge(q_sb, i - 3)
                for k in range(2):
                    n = 2 * i + k
                    last = mm(bank[i % 4][:, 256 * k:256 * k + 256], WQKV[:, P * n:P * n + P], Xg[:, :],
                              start=True, stop=True)
                last.then_inc(qk_ps, 1)
            for n in range(NH):
                for k in range(2):
                    if n == 1:
                        pe.wait_ge(v_sb, k + 1)
                    mm(bank[6 + k][:, :], Xc[:, P * n:P * n + P],
                       WQKV[:, 2 * INNER + 512 * k:2 * INNER + 512 * k + 512], start=True, stop=True).then_inc(v_ps, 1)
            for i in range(NI):
                last = mm(bank[4][:, B * i:B * i + B], WQKV[:, 2 * INNER + P * i:2 * INNER + P * i + P], xm[:, :],
                          start=True, stop=True)
            last.then_inc(vm_ps, 1)
            pe.wait_ge(vm_sb, 1)
            for i in range(NI):
                mm(bank[5][0:B, 0:D], vmT[:, i, :], WOUT[:, i, :], start=(i == 0), stop=False)
            mm(bank[5][0:B, 0:D], ones8[:, :], bout[:, :], start=False, stop=True).then_inc(base_ps, 1)
            pe.wait_ge(base_sb, 1)
            for b in range(B):
                last = mm(bank[4 + b // 4][:, D * (b % 4):D * (b % 4) + D], selb[:, b, :], base[:, :],
                          start=True, stop=True)
            last.then_inc(base_ps, 1)

            pe.wait_ge(q_sb, NI // 2)
            pe.wait_ge(k_sb, NI // 2)
            pe.wait_ge(v_sb, 4)
            pe.wait_ge(base_sb, 2)
            for n in range(NH):
                for q in range(4):
                    if n:
                        pe.wait_ge(bdT_sb, 4)
                    for k in range(4):
                        h = head_at(4 * q + k)
                        rows = slice(DH * (h % 2), DH * (h % 2) + DH)
                        last = mm(bank[q][:, P * k:P * k + P], QK[rows, h // 2, P * n:P * n + P],
                                  QK[rows, NI + h // 2, P * n:P * n + P], start=True, stop=True)
                last.then_inc(s_ps, 1)
                pe.wait_ge(bd_ready, n + 1)
                for q in range(4):
                    for k in range(4):
                        last = nc.tensor.transpose(bank[q][:, P * k:P * k + P], BD[:, 4 * q + k, :], ident[:, :])
                    last.then_inc(bdT_ps, 1)
                pe.wait_ge(bdT_sb, 4 * n + 4)
                if n:
                    pe.wait_ge(o_sb, 2)
                for k in range(H):
                    h = head_at(k)
                    i = h // 2
                    rows = slice(DH * (h % 2), DH * (h % 2) + DH)
                    last = mm(bank[4 + i // 4][rows, P * (i % 4):P * (i % 4) + P], V[:, n, DH * h:DH * h + DH],
                              BDT[:, k, :], start=True, stop=True)
                last.then_inc(o_ps, 1)
                pe.wait_ge(o_sb, 2 * n + 2)
                for i in range(NI):
                    last = mm(bank[6][:, D * n:D * n + D], OT[:, i, :], WOUT[:, i, :], start=(i == 0),
                              stop=(i == NI - 1))
                last.then_inc(dl_ps, 1)
            pe.wait_ge(dl_sb, 2)
            for b in range(B):
                n, a = divmod(b, HB)
                rows = slice(TOPK * a, TOPK * a + TOPK)
                if b >= 4:
                    pe.wait_ge(y_ready, b - 3)
                for c in range(C):
                    last = mm(bank[b % 4][:, D * c:D * c + D], SR[rows, n, P * c:P * c + P], delta[rows, n, :],
                              start=True, stop=True, tile_position=(TOPK * a, 0))
                last.then_inc(at_ps, 1)

        @block.scalar
        def _(act):
            A = nc.scalar.activation
            own = Chain(act, act_own)
            for j in range(B // 2):
                act.wait_ge(f_ps, j + 1)
                if j >= 2:
                    act.wait_ge(g_ps, j - 1)
                A(Fc[:, j % 2, :], bank[j % 2][:, :], ACT.Copy).then_inc(f_sb, 1)
                A(sq[:, j % 2, :], bank[j % 2][:, :], ACT.Square).then_inc(f_sb, 1)
            act.wait_ge(g_used, 4)
            A(var[:, :, :], var[:, :, :], ACT.Sqrt).then_inc(std_ready, 1)
            for j in range(B // 2):
                act.wait_ge(hpre, j + 1)
                A(hid[:, j, :], hid[:, j, :], ACT.Gelu, bias=cbias[:, :]).then_inc(gelu, 1)
            act.wait_ge(sc_sb, 1)
            A(gv[:, :], scores[:, :], ACT.Sigmoid).then_inc(sig, 1)
            act.wait_ge(xs_ps, 1)
            for i in range(NI // 2, NI):
                act.wait_ge(qk_ps, i + 1)
                A(QK[:, 2 * i:2 * i + 2, :], bank[i % 4][:, :].rearrange("p (k t) -> p k t", k=2),
                  ACT.Copy).then_inc(k_sb, 1)
            for n in range(NH):
                for k in range(2):
                    act.wait_ge(v_ps, 2 * n + k + 1)
                    A(V[:, n, 512 * k:512 * k + 512], bank[6 + k][:, :], ACT.Copy).then_inc(v_sb, 1)
            for n in range(NH):
                act.wait_ge(s_shift, 2 * n + 1)
                A(mx[:, 1, :], mx[:, 0, :], ACT.Exp, scale=-1.0).then_inc(em, 1)
                act.wait_ge(s_shift, 2 * n + 2)
                A(S0[:, :, :], S0[:, :, :], ACT.Exp).then_inc(s_exp, 1)
                for q in range(4):
                    act.wait_ge(bdT_ps, 4 * n + q + 1)
                    if n and q == 0:
                        act.wait_ge(o_ps, 1)
                    A(BDT[:, 4 * q:4 * q + 4, :], bank[q][:, :].rearrange("p (k t) -> p k t", k=4),
                      ACT.Copy).then_inc(bdT_sb, 1)
                act.wait_ge(o_ps, n + 1)
                if n:
                    act.wait_ge(dl_ps, 1)
                for i in range(2):
                    A(OT[:, 4 * i:4 * i + 4, :], bank[4 + i][:, :].rearrange("p (k t) -> p k t", k=4),
                      ACT.Copy).then_inc(o_sb, 1)

        @block.vector
        def _(dve):
            V_ = nc.vector
            own = Chain(dve, dve_own)
            dve.wait_ge(ld_wq, 16)
            own(V_.tensor_reduce(wsum[:, :], WQKV[:, 0:INNER].rearrange("p (h e) -> p e h", h=H), AX, ALU.add))
            own(V_.tensor_reduce(wmean[:, 0:1], wsum[:, :], AX, ALU.add))
            own(V_.tensor_scalar(wmean[:, 1:2], wmean[:, 0:1], -1.0 / DH, None, ALU.mult))
            V_.tensor_scalar(Wc[:, :], wsum[:, :], wmean[:, 1:2], 1.0 / H, ALU.add, ALU.mult)
            dve.wait_ge(ld_gate, 16 * 5)
            dve.wait_ge(ld_zero, 16 * 6)
            dve.wait_ge(consts, 1)
            V_.tensor_scalar(w1g[:, :], w1raw[:, :], gcol[:, :], None, ALU.mult)
            V_.tensor_copy(w2sel[0:32, :, :].rearrange("p j b -> p (j b)")[:, 0:31:10],
                           w2col[0:32, :].broadcast_to([32, 4]))
            V_.tensor_copy(w2sel[32:64, :, :].rearrange("p j b -> p (j b)")[:, 1:32:10],
                           w2col[32:64, :].broadcast_to([32, 4])).then_inc(wc_ready, 1)
            dve.wait_ge(cb_ps, 1)
            V_.tensor_tensor(cbias[:, :], bank[7][0:64, 0:1], b1col[:, :], ALU.add).then_inc(wc_ready, 1)
            for j in range(B // 2):
                dve.wait_ge(g_ps, j + 1)
                V_.tensor_scalar(var[:, j, :], bank[6 + j % 2][0:64, :], LN_EPS, None, ALU.add).then_inc(g_used, 1)
            dve.wait_ge(std_ready, 1)
            own(V_.reciprocal(var[:, :, :], var[:, :, :]))
            for j in range(B // 2):
                V_.tensor_tensor(hid[:, j, :], bank[2 + j][0:64, :], var[:, j, :], ALU.mult).then_inc(hpre, 1)
            dve.wait_ge(sc_ps, 1)
            ins = V_.tensor_scalar(scores[:, :], bank[0][0:B, :], b2col[:, :], None, ALU.add)
            ins.then_inc(sc_sb, 1)
            dve.wait_ge(sc_sb, 1)
            src = scores[:, :]
            for i in range(TOPK // 8):
                own(V_.max(top8[:, :], src))
                own(V_.match_replace(cur[:, i % 2, :], top8[:, :], src, NEG_MAX))
                src = cur[:, i % 2, :]
            own(V_.tensor_tensor(mask[:, :], scores[:, :], src, ALU.is_gt))
            own(V_.tensor_tensor_scan(pos[:, :], ones512[:, :], mask[:, :], 0.0, ALU.mult, ALU.add))
            own(V_.tensor_tensor(pos[:, :], pos[:, :], mask[:, :], ALU.mult))
            V_.tensor_scalar(slot[:, :], pos[:, :], -1.0, None, ALU.add).then_inc(slot_ready, 1)
            dve.wait_ge(slotT_ps, 1)
            V_.tensor_copy(slotT[:, :, :], bank[1][:, 0:B * C].rearrange("p (c b) -> p b c", b=B))
            V_.tensor_copy(gT[:, :, :], bank[1][:, 64:64 + B * C].rearrange("p (c b) -> p b c", b=B)
                           ).then_inc(slotT_sb, 1)
            dve.wait_ge(slotT_sb, 1)
            s3 = slotT[:, :, :].rearrange("p b c -> p (b c)").unsqueeze(2).broadcast_to([P, NC, TOPK])
            g3 = gT[:, :, :].rearrange("p b c -> p (b c)").unsqueeze(2).broadcast_to([P, NC, TOPK])
            i3 = iota32[:, :].unsqueeze(1).broadcast_to([P, NC, TOPK])
            own(V_.tensor_tensor(GR[:, :, TOPK:2 * TOPK], s3, i3, ALU.is_equal))
            own(V_.tensor_tensor(GR[:, :, 0:TOPK], GR[:, :, TOPK:2 * TOPK], g3, ALU.mult))
            V_.tensor_scalar(GR[:, :, TOPK:2 * TOPK], GR[:, :, TOPK:2 * TOPK], -1.0 / T, None, ALU.add)
            V_.memset(GR[:, :, 2 * TOPK:], 1.0 / T).then_inc(gr_ready, 1)
            dve.wait_ge(sr_ps, 1)
            for n in range(NH):
                last = V_.tensor_scalar(SR[:, n, :], bank[2 + n][:, :], rcol[:, :], None, ALU.is_equal)
            last.then_inc(sr_sb, 1)
            dve.wait_ge(xs_ps, 1)
            for n in range(NH):
                v = bank[4 + n][:, 0:HB * (2 * TOPK + 1)].rearrange("p (b k) -> p b k", b=HB)
                o = slice(P * n, P * n + P)
                V_.tensor_copy(Xg[:, o].rearrange("p (b k) -> p b k", b=HB), v[:, :, 0:TOPK])
                V_.tensor_copy(Xc[:, o].rearrange("p (b k) -> p b k", b=HB), v[:, :, TOPK:2 * TOPK])
                last = V_.tensor_copy(xm[:, HB * n:HB * n + HB], v[:, :, 2 * TOPK])
            last.then_inc(xs_sb, 1)
            for i in range(NI // 2):
                dve.wait_ge(qk_ps, i + 1)
                V_.tensor_scalar(QK[:, 2 * i:2 * i + 2, :], bank[i % 4][:, :].rearrange("p (k t) -> p k t", k=2),
                                 DH ** -0.5, None, ALU.mult).then_inc(q_sb, 1)
            dve.wait_ge(vm_ps, 1)
            V_.tensor_copy(vmT[:, :, :], bank[4][:, 0:NI * B].rearrange("p (i b) -> p i b", b=B)).then_inc(vm_sb, 1)
            dve.wait_ge(base_ps, 1)
            V_.tensor_copy(base[:, :], bank[5][0:B, 0:D]).then_inc(base_sb, 1)
            dve.wait_ge(base_ps, 2)
            for n in range(2):
                last = V_.tensor_copy(base_all[:, 4 * n:4 * n + 4, :],
                                      bank[4 + n][:, :].rearrange("p (b d) -> p b d", b=4))
            last.then_inc(base_sb, 1)
            m, e_, s, r, u, neg = (mx[:, k, :] for k in range(6))
            for n in range(NH):
                dve.wait_ge(s_ps, n + 1)
                for q in range(4):
                    for a in range(HB):
                        rows = slice(TOPK * a, TOPK * a + TOPK)
                        last = V_.tensor_copy(S0[rows, 4 * q:4 * q + 4, :],
                                              bank[q][rows, :].rearrange("p (k t) -> p k t", k=4)[:, :, rows])
                own(last)
                own(V_.tensor_reduce(m, S0[:, :, :], AX, ALU.max))
                V_.tensor_scalar(m, m, 0.0, None, ALU.max).then_inc(s_shift, 1)
                dve.wait_ge(s_shift, 2 * n + 1)
                V_.tensor_tensor(S0[:, :, :], S0[:, :, :], m.unsqueeze(2).broadcast_to([P, H, TOPK]),
                                 ALU.subtract).then_inc(s_shift, 1)
                dve.wait_ge(em, n + 1)
                dve.wait_ge(s_exp, n + 1)
                own(V_.tensor_reduce(s, S0[:, :, :], AX, ALU.add))
                own(V_.scalar_tensor_tensor(out=s, in0=e_, scalar=float(T - TOPK), in1=s, op0=ALU.mult, op1=ALU.add))
                own(V_.reciprocal(r, s))
                V_.tensor_tensor(u, e_, r, ALU.mult)
                own(V_.tensor_tensor(S0[:, :, :], S0[:, :, :], r.unsqueeze(2).broadcast_to([P, H, TOPK]), ALU.mult))
                if n:
                    dve.wait_ge(bdT_ps, 4)
                for a in range(HB):
                    rows = slice(TOPK * a, TOPK * a + TOPK)
                    last = V_.tensor_tensor(BD[rows, :, rows], S0[rows, :, :],
                                            u[rows].unsqueeze(2).broadcast_to([TOPK, H, TOPK]), ALU.subtract)
                last.then_inc(bd_ready, 1)
                dve.wait_ge(dl_ps, n + 1)
                V_.tensor_copy(delta[:, n, :], bank[6][:, D * n:D * n + D]).then_inc(dl_sb, 1)

            def normalise(b):
                dve.wait_ge(rstd_ready, b + 1)
                for c in range(C):
                    i = C * b + c
                    last = V_.tensor_scalar(X[:, i, :], y[:, i, :], mv[:, i, 0:1], rs[:, i:i + 1],
                                            ALU.subtract, ALU.mult)
                return last

            for b in range(B):
                dve.wait_ge(at_ps, b + 1)
                dve.wait_ge(xb_ready, b + 1)
                V_.tensor_tensor(y[:, C * b:C * b + C, :], y[:, C * b:C * b + C, :],
                                 bank[b % 4][:, :].rearrange("p (c d) -> p c d", c=C), ALU.add).then_inc(y_ready, 1)
                dve.wait_ge(y_ready, b + 1)
                for c in range(C):
                    last = V_.bn_stats(st6[:, c, :], y[:, C * b + c, :])
                own(last)
                for c in range(C):
                    last = V_.bn_aggr(mv[:, C * b + c, :], st6[:, c, :])
                own(last)
                V_.tensor_scalar(ve[:, C * b:C * b + C], mv[:, C * b:C * b + C, 1], LN_EPS, None,
                                 ALU.add).then_inc(ve_ready, 1)
                if b:
                    normalise(b - 1)
            own(normalise(B - 1))
            own(V_.tensor_tensor(rs[:, :], rs[:, :], rs[:, :], ALU.mult))
            own(V_.tensor_tensor(rs[:, :], rs[:, :], mv[:, :, 1], ALU.mult))
            V_.tensor_scalar(ve[:, :], rs[:, :], RMS_EPS, None, ALU.add).then_inc(ms_ready, 1)
            dve.wait_ge(r1_ready, 1)


def causal_attention_and_experts(nc, keep, g1, Wq, WdkvT, Wuk, Wuv, Wo, g2, gate_w, w1, w2, out):
    X, ident, identb, maskb = keep["X"], keep["ident"], keep["identb"], keep["maskb"]
    qpad, r1, mhalf, tri = keep["qpad"], keep["r1"], keep["mhalf"], keep["tri"]
    ctx = ExitStack()
    with ctx:
        def sb(name, shape, dt=F32):
            return ctx.enter_context(nc.sbuf_tensor(name, shape, dt))

        def sem(name):
            return ctx.enter_context(nc.semaphore(name))

        wexp1 = sb("wexp1", [P, NE, EH])
        wexp2 = sb("wexp2", [P, NE, 2, D])
        wgate = sb("wgate", [P, NE])
        wqkv = sb("wqkv", [P, 3 * D])
        wo = sb("wo", [P, D])
        wd = sb("wd", [LAT, D])
        wu = sb("wu", [LAT, 2, D])
        g1c, g2c = sb("g1c", [P, 1]), sb("g2c", [P, 1])
        xr = sb("xr", [P, C, D])
        xrT = sb("xrT", [P, T])
        qs = sb("qs", [P, C, MH, R], F32R)
        ks = sb("ks", [P, C, MH, R], F32R)
        qT = sb("qT", [P, NG, T], F32R)
        kT = sb("kT", [P, NG, T], F32R)
        va = sb("va", [P, C, MH, R])
        negmax = sb("negmax", [P, C, MH])
        shift = sb("shift", [P, C, 4, 2, NG], F32R)
        shiftT = sb("shiftT", [4 * 2 * NG, T], F32R)
        prob = sb("prob", [P, 2, 4, T])
        oT = sb("oT", [P, NG, T])
        rden = sb("rden", [P, C, MH])
        attn = sb("attn", [P, C, D])
        attnT = sb("attnT", [P, T])
        x2 = sb("x2", [P, C, D])
        both_x = sb("both_x", [P, C, D])
        t = sb("t", [P, C, D])
        tT = sb("tT", [P, T])
        st2, mv2, ms2, r2 = sb("st2", [P, C, 6]), sb("mv2", [P, C, 2]), sb("ms2", [P, C]), sb("r2", [P, C])
        st3, mv3, ve3, rs3 = sb("st3", [P, C, 6]), sb("mv3", [P, C, 2]), sb("ve3", [P, C]), sb("rs3", [P, C])
        lg, ex = sb("lg", [P, C, NE]), sb("ex", [P, C, NE])
        before, equal = sb("before", [P, C, NE, NE]), sb("equal", [P, C, NE, NE])
        rank, top1 = sb("rank", [P, C, NE]), sb("top1", [P, C])
        wsum, wrec = sb("wsum2", [P, C]), sb("wrec", [P, C])
        comb = sb("comb", [P, C, NE])
        hid = sb("hid2", [P, 2, 2, T])
        acc = sb("acc", [P, C, D])
        outb = sb("outb", [P, C, D])
        psA = ctx.enter_context(nc.psum_tensor("psA", [P, 4, 512], F32))
        psH = ctx.enter_context(nc.psum_tensor("psH", [P, 2, 512], F32))
        psY = ctx.enter_context(nc.psum_tensor("psY", [P, 2, 512], F32))

        names = """ld_w ld_e const w_ps w_ready xr_ready xrT_ps xrT_sb qkv_ps hi_ready lo_ready stack_ps q_sb k_sb
            qpad_in s_ps max_ready shift_ready shiftT_ps shiftT_sb shift_in st_ps exp_ready masked pv_done oT_sb
            o_ps attn_ready attnT_ps attnT_sb wo_ps x2_ready both_ready ms2_ready r2_ready t_ready tT_ps tT_sb lg_ps lg_shift
            lg_exp comb_ready hid_ps hid_ready y_ps y_used ve3_ready rs3_ready out_ready out_done own_dve steps_dve steps_pool
            own_pool""".split()
        s = {n: sem(n) for n in names}

        def loop(eng, first, rest, last):
            first(0)
            with eng.Fori(1, B) as b:
                rest(b)
            last(B - 1)

        out_v = out.rearrange("b (c p) d -> p (b c) d", p=P)
        block = ctx.enter_context(nc.Block())

        @block.sync
        def _(sp):
            sp.dma_start(wd[:, :], WdkvT).then_inc(s["ld_w"], 16)
            sp.dma_start(wu[:, 0, :], Wuk).then_inc(s["ld_w"], 16)
            sp.dma_start(wu[:, 1, :], Wuv).then_inc(s["ld_w"], 16)
            sp.dma_start(g1c[:, :], g1).then_inc(s["ld_w"], 16)
            sp.dma_start(wqkv[:, 0:D], Wq).then_inc(s["ld_w"], 16)
            sp.dma_start(wo[:, :], Wo).then_inc(s["ld_w"], 16)
            sp.dma_start(g2c[:, :], g2).then_inc(s["ld_e"], 16)
            sp.dma_start(wgate[:, :], gate_w).then_inc(s["ld_e"], 16)
            sp.dma_start(wexp1[:, :, :], w1.rearrange("e d h -> d e h")).then_inc(s["ld_e"], 16)
            sp.dma_start(wexp2[:, :, :, :], w2.rearrange("e (k p) d -> p e k d", p=P)).then_inc(s["ld_e"], 16)

            def attention(b):
                sp.wait_ge(s["q_sb"], NG * b + NG)
                for a in range(4):
                    rows = slice(R * a, R * a + R)
                    sp.dma_start(qpad[rows, a:MH:4, :].bitcast(F32), qT[rows, :, :].bitcast(F32)).then_inc(s["qpad_in"], 16)
                sp.wait_ge(s["shiftT_sb"], b + 1)
                for a in range(4):
                    for j in range(2):
                        sp.dma_start(qpad[R * a + SHIFT + j:R * a + SHIFT + j + 1, a:MH:4, :].bitcast(F32),
                                     shiftT[8 * a + 4 * j:8 * a + 4 * j + 4, :].bitcast(F32)).then_inc(s["shift_in"], 16)

            def store(m):
                sp.wait_ge(s["out_ready"], m + 1)
                sp.dma_start(out_v[:, ds(C * m, C), :], outb[:, :, :]).then_inc(s["out_done"], 16)

            def both(b):
                attention(b)
                store(b - 1)

            loop(sp, attention, both, store)
            sp.wait_ge(s["out_done"], 16 * B + 16)

        @block.gpsimd
        def _(pool):
            own = Chain(pool, s["own_pool"])
            own(pool.memset(va[:, :, :, :], 0.0))
            own(pool.memset(va[:, :, :, MD:MD + 1], 1.0))
            own(pool.memset(qs[:, :, :, :].bitcast(F32), 0.0))
            own(pool.memset(ks[:, :, :, :].bitcast(F32), 0.0))
            pool.memset(ks[:, :, :, SHIFT:SHIFT + 2].bitcast(F32), 1.0).then_inc(s["const"], 1)
            pool.wait_ge(s["const"], 1)

            def final_norm(m):
                pool.wait_ge(s["ve3_ready"], m + 1)
                pool.tensor_tensor(rs3[:, :], ve3[:, :], mhalf[:, 0:C], ALU.pow).then_inc(s["rs3_ready"], 1)

            def attention(b):
                for n in range(NG * C):
                    kc = n % C
                    for p in range(2):
                        pool.wait_ge(s["exp_ready"], 32 * b + 2 * n + p + 1)
                        pool.sem_inc(s["steps_pool"], 1)
                        blk = prob[:, n % 2, 2 * p:2 * p + 2, P * kc:P * kc + P]
                        pool.affine_select(out=blk, in_=blk, compare_op=ALU.is_ge, fill=0.0, base=0,
                                           pattern=[[0, 2], [1, P]], channel_multiplier=-1).then_inc(s["masked"], 1)
                pool.wait_ge(s["ms2_ready"], b + 1)
                pool.tensor_tensor(r2[:, :], ms2[:, :], mhalf[:, 0:C], ALU.pow).then_inc(s["r2_ready"], 1)
                pool.wait_ge(s["x2_ready"], b + 1)
                pool.tensor_tensor(both_x[:, :, :], X[:, ds(C * b, C), :], x2[:, :, :],
                                   ALU.add).then_inc(s["both_ready"], 1)

            def both(b):
                final_norm(b - 1)
                attention(b)

            loop(pool, attention, both, final_norm)

        @block.tensor
        def _(pe):
            mm, tr = nc.tensor.matmul, nc.tensor.transpose
            pe.wait_ge(s["ld_w"], 16 * 6)
            mm(psA[:, 0, 0:2 * D], wd[:, :], wu[:, :, :], start=True, stop=True).then_inc(s["w_ps"], 1)
            pe.wait_ge(s["w_ready"], 1)

            def project(b):
                pe.wait_ge(s["xr_ready"], b + 1)
                for c in range(C):
                    last = tr(psY[:, 0, P * c:P * c + P], xr[:, c, :], ident[:, :])
                last.then_inc(s["xrT_ps"], 1)
                pe.wait_ge(s["xrT_sb"], b + 1)
                for c in range(C):
                    dst = (psH[:, 0, :], psH[:, 1, :], psY[:, 1, :], psY[:, 0, :])[c]
                    mm(dst[:, 0:3 * D], xrT[:, P * c:P * c + P], wqkv[:, :], start=True,
                       stop=True).then_inc(s["qkv_ps"], 1)
                pe.wait_ge(s["hi_ready"], C * b + C)
                pe.wait_ge(s["lo_ready"], C * b + C)
                for g in range(NG):
                    for c in range(C):
                        last = tr(psA[:, g, P * c:P * c + P],
                                  qs[:, c, 4 * g:4 * g + 4, :].rearrange("p h r -> p (h r)").bitcast(F32), ident[:, :])
                    last.then_inc(s["stack_ps"], 1)
                for g in range(NG):
                    dst = (psH, psY)[g // 2][:, g % 2, :]
                    for c in range(C):
                        last = tr(dst[:, P * c:P * c + P],
                                  ks[:, c, 4 * g:4 * g + 4, :].rearrange("p h r -> p (h r)").bitcast(F32), ident[:, :])
                    last.then_inc(s["stack_ps"], 1)
                pe.wait_ge(s["k_sb"], NG * b + NG)
                pe.wait_ge(s["qpad_in"], 64 * b + 64)

            def score_steps(b, lo, hi):
                for n in range(lo, hi):
                    c, p = divmod(n, MH // 2)
                    if n >= 2:
                        pe.wait_ge(s["max_ready"], 32 * b + n - 1)
                    for j in range(2):
                        h = 2 * p + j
                        dst = psA[:, 2 * (n % 2) + j, :]
                        keys = max(P * (c + 1), 256)
                        mm(dst[:, 0:keys], qpad[:, h, P * c:P * c + P], kT[:, h // 4, 0:keys], start=True, stop=False)
                        last = mm(dst[:, P * c:P * c + P], identb[:, :], maskb[:, :], start=False, stop=True)
                    last.then_inc(s["s_ps"], 1)

            def weigh(b):
                pe.wait_ge(s["shift_ready"], b + 1)
                for c in range(C):
                    last = tr(psA[0:32, 0, P * c:P * c + P],
                              shift[:, c, :, :, :].rearrange("p a j g -> p (a j g)").bitcast(F32), ident[:, :])
                last.then_inc(s["shiftT_ps"], 1)
                pe.wait_ge(s["shift_in"], 128 * b + 128)

                def scores(n):
                    g, kc = divmod(n, C)
                    for p in range(2):
                        m = 2 * n + p
                        if m >= 2:
                            pe.wait_ge(s["exp_ready"], 32 * b + m - 1)
                        q0 = min(P * kc, 256)
                        for j in range(2):
                            h = 4 * g + 2 * p + j
                            last = mm(psA[:, 2 * (m % 2) + j, q0:T], kT[:, g, P * kc:P * kc + P], qpad[:, h, q0:T],
                                      start=True, stop=True)
                        last.then_inc(s["st_ps"], 1)

                scores(0)
                for n in range(NG * C):
                    if n + 1 < NG * C:
                        scores(n + 1)
                    g, kc = divmod(n, C)
                    pe.wait_ge(s["masked"], 32 * b + 2 * n + 2)
                    if kc == 0 and g >= 2:
                        pe.wait_ge(s["oT_sb"], NG * b + g - 1)
                    for a in range(4):
                        last = mm(psH[R * a:R * a + R, g % 2, P * kc:T], va[:, kc, 4 * g + a, :],
                                  prob[:, n % 2, a, P * kc:T], start=(kc == 0), stop=(kc == C - 1),
                                  tile_position=(0, R * a))
                    last.then_inc(s["pv_done"], 1)

            def finish(b):
                pe.wait_ge(s["oT_sb"], NG * b + NG)
                for c in range(C):
                    if c >= 2:
                        pe.wait_ge(s["attn_ready"], C * b + c - 1)
                    for g in range(NG):
                        last = tr(psY[:, c % 2, P * g:P * g + P], oT[:, g, P * c:P * c + P], ident[:, :])
                    last.then_inc(s["o_ps"], 1)
                pe.wait_ge(s["attn_ready"], C * b + C)
                for c in range(C):
                    last = tr(psH[:, 0, P * c:P * c + P], attn[:, c, :], ident[:, :])
                last.then_inc(s["attnT_ps"], 1)
                pe.wait_ge(s["attnT_sb"], b + 1)
                for c in range(C):
                    last = mm(psH[:, 1, D * c:D * c + D], attnT[:, P * c:P * c + P], wo[:, :], start=True, stop=True)
                last.then_inc(s["wo_ps"], 1)
                pe.wait_ge(s["t_ready"], b + 1)
                for c in range(C):
                    last = tr(psY[:, 0, P * c:P * c + P], t[:, c, :], ident[:, :])
                last.then_inc(s["tT_ps"], 1)
                pe.wait_ge(s["tT_sb"], b + 1)
                for c in range(C):
                    last = mm(psY[:, 1, NE * c:NE * c + NE], tT[:, P * c:P * c + P], wgate[:, :], start=True, stop=True)
                last.then_inc(s["lg_ps"], 1)

            def hidden(m, e):
                for k in range(2):
                    if e:
                        pe.wait_ge(s["hid_ready"], 2 * NE * m + 2 * (e - 1) + k + 1)
                    mm(psH[:, k, :], wexp1[:, e, P * k:P * k + P], tT[:, :], start=True,
                       stop=True).then_inc(s["hid_ps"], 1)

            def down(m, e):
                pe.wait_ge(s["hid_ready"], 2 * NE * m + 2 * e + 2)
                if e >= 2:
                    pe.wait_ge(s["y_used"], NE * m + e - 1)
                for c in range(C):
                    for k in range(2):
                        last = mm(psY[:, e % 2, D * c:D * c + D], hid[:, e % 2, k, P * c:P * c + P], wexp2[:, e, k, :],
                                  start=(k == 0), stop=(k == 1))
                last.then_inc(s["y_ps"], 1)

            def first(b):
                project(b)
                score_steps(b, 0, 32)
                weigh(b)
                finish(b)

            def rest(b):
                project(b)
                for e in range(NE):
                    score_steps(b, 4 * e, 4 * e + 4)
                    hidden(b - 1, e)
                    if e:
                        down(b - 1, e - 1)
                down(b - 1, NE - 1)
                pe.wait_ge(s["y_used"], NE * (b - 1) + NE)
                weigh(b)
                finish(b)

            def last_(m):
                pe.wait_ge(s["comb_ready"], m + 1)
                hidden(m, 0)
                for e in range(NE):
                    if e + 1 < NE:
                        hidden(m, e + 1)
                    down(m, e)

            loop(pe, first, rest, last_)

        @block.scalar
        def _(act):
            A = nc.scalar.activation

            def project(b):
                act.wait_ge(s["xrT_ps"], b + 1)
                A(xrT[:, :], psY[:, 0, :], ACT.Copy).then_inc(s["xrT_sb"], 1)
                if isinstance(b, int):
                    act.wait_ge(s["const"], 1)
                for c in range(C):
                    act.wait_ge(s["qkv_ps"], C * b + c + 1)
                    src = (psH[:, 0, :], psH[:, 1, :], psY[:, 1, :], psY[:, 0, :])[c]
                    q, k, v = (src[:, D * i:D * i + D].rearrange("p (h m) -> p h m", m=MD) for i in range(3))
                    A(qs[:, c, :, 0:MD], q, ACT.Copy)
                    A(ks[:, c, :, 0:MD], k, ACT.Copy)
                    A(va[:, c, :, 0:MD], v, ACT.Copy).then_inc(s["hi_ready"], 1)
                for g in range(NG):
                    act.wait_ge(s["stack_ps"], 8 * b + g + 1)
                    A(qT[:, g, :], psA[:, g, :], ACT.Copy).then_inc(s["q_sb"], 1)

            def weigh(b):
                act.wait_ge(s["shiftT_ps"], b + 1)
                A(shiftT[:, :], psA[0:32, 0, :], ACT.Copy).then_inc(s["shiftT_sb"], 1)
                for n in range(NG * C):
                    kc = n % C
                    if n >= 2:
                        act.wait_ge(s["pv_done"], 16 * b + n - 1)
                    for p in range(2):
                        m = 2 * n + p
                        act.wait_ge(s["st_ps"], 32 * b + m + 1)
                        A(prob[:, n % 2, 2 * p:2 * p + 2, P * kc:T], psA[:, 2 * (m % 2):2 * (m % 2) + 2, P * kc:T],
                          ACT.Exp).then_inc(s["exp_ready"], 1)

            def finish(b):
                act.wait_ge(s["attnT_ps"], b + 1)
                A(attnT[:, :], psH[:, 0, :], ACT.Copy).then_inc(s["attnT_sb"], 1)
                act.wait_ge(s["tT_ps"], b + 1)
                A(tT[:, :], psY[:, 0, :], ACT.Copy).then_inc(s["tT_sb"], 1)
                act.wait_ge(s["lg_shift"], b + 1)
                A(ex[:, :, :], lg[:, :, :], ACT.Exp).then_inc(s["lg_exp"], 1)

            def experts(m):
                for e in range(NE):
                    for k in range(2):
                        act.wait_ge(s["hid_ps"], 2 * NE * m + 2 * e + k + 1)
                        if e >= 2 and k == 0:
                            act.wait_ge(s["y_ps"], NE * m + e - 1)
                        A(hid[:, e % 2, k, :], psH[:, k, :], ACT.Silu).then_inc(s["hid_ready"], 1)

            def first(b):
                project(b)
                weigh(b)
                finish(b)

            def rest(b):
                project(b)
                experts(b - 1)
                weigh(b)
                finish(b)

            loop(act, first, rest, experts)

        @block.vector
        def _(dve):
            V = nc.vector
            own = Chain(dve, s["own_dve"])
            dve.wait_ge(s["w_ps"], 1)
            V.tensor_scalar(wqkv[:, D:3 * D], psA[:, 0, 0:2 * D], g1c[:, :], None, ALU.mult)
            V.tensor_scalar(wqkv[:, 0:D], wqkv[:, 0:D], g1c[:, :], MD ** -0.5, ALU.mult,
                            ALU.mult).then_inc(s["w_ready"], 1)
            dve.wait_ge(s["ld_e"], 64)
            V.tensor_scalar(wexp1[:, :, :], wexp1[:, :, :], g2c[:, :], None, ALU.mult)
            own(V.tensor_scalar(wgate[:, :], wgate[:, :], g2c[:, :], None, ALU.mult))
            V.memset(outb[:, 0, 0:1], 0.0).then_inc(s["out_done"], 16)

            def project(b):
                if not isinstance(b, int):
                    dve.wait_ge(s["tT_ps"], b)
                for c in range(C):
                    last = V.tensor_scalar(xr[:, c, :], X[:, ds(C * b + c, 1), :], r1[:, ds(C * b + c, 1)], None,
                                           ALU.mult)
                last.then_inc(s["xr_ready"], 1)
                for c in range(C):
                    dve.wait_ge(s["hi_ready"], C * b + c + 1)
                    src = (psH[:, 0, :], psH[:, 1, :], psY[:, 1, :], psY[:, 0, :])[c]
                    q, k = (src[:, D * i:D * i + D].rearrange("p (h m) -> p h m", m=MD) for i in range(2))
                    V.tensor_copy(qs[:, c, :, MD:2 * MD], qs[:, c, :, 0:MD].bitcast(F32))
                    V.tensor_copy(ks[:, c, :, 2 * MD:3 * MD], ks[:, c, :, 0:MD].bitcast(F32))
                    V.tensor_tensor(qs[:, c, :, 2 * MD:3 * MD], q, qs[:, c, :, 0:MD].bitcast(F32), ALU.subtract)
                    V.tensor_tensor(ks[:, c, :, MD:2 * MD], k, ks[:, c, :, 0:MD].bitcast(F32),
                                    ALU.subtract).then_inc(s["lo_ready"], 1)
                for g in range(NG):
                    dve.wait_ge(s["stack_ps"], 8 * b + NG + g + 1)
                    V.tensor_copy(kT[:, g, :], (psH, psY)[g // 2][:, g % 2, :]).then_inc(s["k_sb"], 1)

            def maxima(b, lo, hi):
                for n in range(lo, hi):
                    c, p = divmod(n, MH // 2)
                    dve.wait_ge(s["s_ps"], 32 * b + n + 1)
                    V.tensor_reduce(negmax[:, c, 2 * p:2 * p + 2], psA[:, 2 * (n % 2):2 * (n % 2) + 2, 0:P * (c + 1)],
                                    AX, ALU.max, negate=True).then_inc(s["max_ready"], 1)

            def shifts(b):
                dve.wait_ge(s["max_ready"], 32 * b + 32)
                for c in range(C):
                    m = negmax[:, c, :].rearrange("p (g a) -> p a g", a=4)
                    last = V.tensor_copy(shift[:, c, :, 0, :], m)
                own(last)
                for c in range(C):
                    m = negmax[:, c, :].rearrange("p (g a) -> p a g", a=4)
                    last = V.tensor_tensor(shift[:, c, :, 1, :], m, shift[:, c, :, 0, :].bitcast(F32), ALU.subtract)
                last.then_inc(s["shift_ready"], 1)

            def finish(b):
                for g in range(NG):
                    dve.wait_ge(s["pv_done"], 16 * b + 4 * g + 4)
                    V.tensor_copy(oT[:, g, :], psH[:, g % 2, :]).then_inc(s["oT_sb"], 1)
                for c in range(C):
                    dve.wait_ge(s["o_ps"], C * b + c + 1)
                    src = psY[:, c % 2, :].rearrange("p (h r) -> p h r", r=R)
                    own(V.reciprocal(rden[:, c, :], src[:, :, MD]))
                    V.tensor_tensor(attn[:, c, :].rearrange("p (h m) -> p h m", m=MD), src[:, :, 0:MD],
                                    rden[:, c, :].unsqueeze(2).broadcast_to([P, MH, MD]),
                                    ALU.mult).then_inc(s["attn_ready"], 1)
                dve.wait_ge(s["wo_ps"], b + 1)
                V.tensor_tensor(x2[:, :, :], X[:, ds(C * b, C), :], psH[:, 1, :].rearrange("p (c d) -> p c d", d=D),
                                ALU.add).then_inc(s["x2_ready"], 1)
                dve.wait_ge(s["x2_ready"], b + 1)
                for c in range(C):
                    last = V.bn_stats(st2[:, c, :], x2[:, c, :])
                own(last)
                dve.sem_inc(s["steps_dve"], 1)
                for c in range(C):
                    last = V.bn_aggr(mv2[:, c, :], st2[:, c, :])
                own(last)
                own(V.tensor_tensor(ms2[:, :], mv2[:, :, 0], mv2[:, :, 0], ALU.mult))
                V.scalar_tensor_tensor(out=ms2[:, :], in0=ms2[:, :], scalar=RMS_EPS, in1=mv2[:, :, 1], op0=ALU.add,
                                       op1=ALU.add).then_inc(s["ms2_ready"], 1)
                dve.wait_ge(s["r2_ready"], b + 1)
                for c in range(C):
                    last = V.tensor_scalar(t[:, c, :], x2[:, c, :], r2[:, c:c + 1], None, ALU.mult)
                last.then_inc(s["t_ready"], 1)
                dve.wait_ge(s["lg_ps"], b + 1)
                src = psY[:, 1, 0:C * NE].rearrange("p (c e) -> p c e", e=NE)
                own(V.tensor_copy(lg[:, :, :], src))
                other = lg[:, :, :].unsqueeze(2).broadcast_to([P, C, NE, NE])
                this = lg[:, :, :].unsqueeze(3).broadcast_to([P, C, NE, NE])
                V.tensor_tensor(before[:, :, :, :], other, this, ALU.is_gt)
                V.tensor_tensor(equal[:, :, :, :], other, this, ALU.is_equal)
                own(V.tensor_reduce(top1[:, :], lg[:, :, :], AX, ALU.max))
                V.tensor_tensor(lg[:, :, :], lg[:, :, :], top1[:, :].unsqueeze(2).broadcast_to([P, C, NE]),
                                ALU.subtract).then_inc(s["lg_shift"], 1)
                own(V.tensor_tensor(equal[:, :, :, :], equal[:, :, :, :],
                                    tri[:, :, :].unsqueeze(1).broadcast_to([P, C, NE, NE]), ALU.mult))
                own(V.tensor_tensor(before[:, :, :, :], before[:, :, :, :], equal[:, :, :, :], ALU.add))
                own(V.tensor_reduce(rank[:, :, :], before[:, :, :, :], AX, ALU.add))
                dve.wait_ge(s["lg_exp"], b + 1)
                own(V.scalar_tensor_tensor(out=rank[:, :, :], in0=rank[:, :, :], scalar=2.0, in1=ex[:, :, :],
                                           op0=ALU.is_lt, op1=ALU.mult))
                own(V.tensor_reduce(wsum[:, :], rank[:, :, :], AX, ALU.add))
                own(V.reciprocal(wrec[:, :], wsum[:, :]))
                V.tensor_tensor(comb[:, :, :], rank[:, :, :], wrec[:, :].unsqueeze(2).broadcast_to([P, C, NE]),
                                ALU.mult).then_inc(s["comb_ready"], 1)

            def gather(m, e):
                if e == 0:
                    dve.wait_ge(s["comb_ready"], m + 1)
                    dve.wait_ge(s["both_ready"], m + 1)
                dve.wait_ge(s["y_ps"], NE * m + e + 1)
                if e:
                    dve.wait_ge(s["y_used"], NE * m + e)
                for c in range(C):
                    last = V.scalar_tensor_tensor(out=acc[:, c, :], in0=psY[:, e % 2, D * c:D * c + D],
                                                  scalar=comb[:, c, e:e + 1], in1=(acc if e else both_x)[:, c, :],
                                                  op0=ALU.mult, op1=ALU.add)
                last.then_inc(s["y_used"], 1)

            def statistics(m):
                dve.wait_ge(s["y_used"], NE * m + NE)
                for c in range(C):
                    last = V.bn_stats(st3[:, c, :], acc[:, c, :])
                own(last)
                dve.sem_inc(s["steps_dve"], 1)
                for c in range(C):
                    last = V.bn_aggr(mv3[:, c, :], st3[:, c, :])
                own(last)
                V.tensor_scalar(ve3[:, :], mv3[:, :, 1], LN_EPS, None, ALU.add).then_inc(s["ve3_ready"], 1)

            def result(m):
                dve.wait_ge(s["rs3_ready"], m + 1)
                dve.wait_ge(s["out_done"], 16 * m + 16)
                for c in range(C):
                    last = V.tensor_scalar(outb[:, c, :], acc[:, c, :], mv3[:, c, 0:1], rs3[:, c:c + 1], ALU.subtract,
                                           ALU.mult)
                last.then_inc(s["out_ready"], 1)

            def first(b):
                project(b)
                maxima(b, 0, 32)
                shifts(b)
                finish(b)

            def rest(b):
                project(b)
                maxima(b, 0, 12)
                for e in range(NE - 2):
                    gather(b - 1, e)
                    if e < 5:
                        maxima(b, 12 + 4 * e, 16 + 4 * e)
                gather(b - 1, NE - 2)
                gather(b - 1, NE - 1)
                shifts(b)
                statistics(b - 1)
                result(b - 1)
                finish(b)

            def last_(m):
                for e in range(NE):
                    gather(m, e)
                statistics(m)
                result(m)

            before_loop = None
            first(0)
            before_loop, own.n = own.n, 0
            with dve.Fori(1, B) as b:
                own.base = before_loop + (b - 1) * PER_TRIP
                rest(b)
            assert own.n == PER_TRIP, own.n
            own.base, own.n = before_loop + (B - 1) * PER_TRIP, 0
            last_(B - 1)


PER_TRIP = 18

INPUTS = ["x", "xT", "wqkvT", "woutT", "b_out", "ln_g", "ln_b", "w1gT", "b1g", "w2gT", "b2g"]
INPUTS2 = ["g1", "Wq", "WdkvT", "Wuk", "Wuv", "Wo", "g2", "gate_w", "w1", "w2"]


def program(nc, ins, out):
    with ExitStack() as ctx:
        def sb(name, shape, dt=F32):
            return ctx.enter_context(nc.sbuf_tensor(name, shape, dt))

        keep = {
            "X": sb("X", [P, NC, D]),
            "qpad": sb("qpad", [P, MH, T], F32R),
            "ident": sb("ident", [P, P]),
            "identb": sb("identb", [P, P], BF16),
            "maskb": sb("maskb", [P, P], BF16),
            "tri": sb("tri", [P, NE, NE]),
            "r1": sb("r1", [P, NC]),
            "mhalf": sb("mhalf", [P, NC]),
        }
        gated_attention(nc, keep, *(ins[k] for k in INPUTS))
        causal_attention_and_experts(nc, keep, *(ins[k] for k in INPUTS2), out)


def kernel(**inputs):
    import concourse.bacc as bacc
    from concourse.bass_utils import run_bass_kernel_spmd

    a = {k.split("_", 1)[1]: np.asarray(v) for k, v in inputs.items()}
    tokens = a["attn_x"]
    laid = {
        "x": tokens.reshape(NC, P, D).transpose(1, 0, 2),
        "xT": tokens.reshape(B * T, D).T,
        "wqkvT": a["attn_w_qkv"].T,
        "woutT": a["attn_w_out"].T,
        "b_out": a["attn_b_out"].reshape(1, D),
        "ln_g": a["attn_ln_g"].reshape(DH, 1),
        "ln_b": a["attn_ln_b"].reshape(DH, 1),
        "w1gT": a["attn_w1"].T,
        "b1g": a["attn_b1"].reshape(GH, 1),
        "w2gT": a["attn_w2"].T,
        "b2g": a["attn_b2"].reshape(1, 1).repeat(B, 0),
        "g1": a["ffn_g1"].reshape(D, 1),
        "Wq": a["ffn_Wq"],
        "WdkvT": a["ffn_Wdkv"].T,
        "Wuk": a["ffn_Wuk"],
        "Wuv": a["ffn_Wuv"],
        "Wo": a["ffn_Wo"],
        "g2": a["ffn_g2"].reshape(D, 1),
        "gate_w": a["ffn_gate_w"],
        "w1": a["ffn_w1"],
        "w2": a["ffn_w2"],
    }
    nc = bacc.Bacc("TRN2", target_bir_lowering=False, num_devices=1)
    arrays, ins = {}, {}
    for name, v in laid.items():
        arrays[f"in_{name}"] = v = np.ascontiguousarray(v)
        ins[name] = nc.dram_tensor(f"in_{name}", v.shape, mybir.dt.from_np(v.dtype), kind="ExternalInput").ap()
    out = nc.dram_tensor("out", tokens.shape, F32, kind="ExternalOutput").ap()
    program(nc, ins, out)
    r = run_bass_kernel_spmd(nc, [arrays], core_ids=[0])
    return r.results[0]["out"]
```

```python
from contextlib import ExitStack

import numpy as np

import concourse.bass as bass
from concourse import mybir

ALU = mybir.AluOpType
ACT = mybir.ActivationFunctionType
AX = mybir.AxisListType.X
F32 = mybir.dt.float32
F32R = mybir.dt.float32r
BF16 = mybir.dt.bfloat16
NEG_MAX = float(np.finfo(np.float32).min)
ds = bass.ds

B, T, D = 8, 512, 128
P = 128
C = T // P
NC = B * C
H, DH = 16, 64
INNER = H * DH
NI = INNER // P
TOPK = 32
HB = P // TOPK
NH = B // HB
GH = 16
GR0 = 32
LN_EPS = 1e-5
RMS_EPS = 1e-6
MH, MD = 16, 8
LAT = 64
NG = MH // 4
R = 32
SHIFT = 3 * MD
NE, EH = 8, 256
BIG = -1e30


class Chain:

    def __init__(self, eng, sem):
        self.eng, self.sem, self.n, self.base = eng, sem, 0, 0

    def __call__(self, ins):
        self.n += 1
        ins.then_inc(self.sem, 1)
        self.eng.wait_ge(self.sem, self.base + self.n)


def head_at(k):
    return 2 * (k % (H // 2)) + k // (H // 2)


def gated_attention(nc, keep, x, xT, wqkvT, woutT, b_out, ln_g, ln_b, w1gT, b1g, w2gT, b2g):
    X, ident, mhalf, r1 = keep["X"], keep["ident"], keep["mhalf"], keep["r1"]
    ctx = ExitStack()
    with ctx:
        def sb(name, shape, dt=F32):
            return ctx.enter_context(nc.sbuf_tensor(name, shape, dt))

        def sem(name):
            return ctx.enter_context(nc.semaphore(name))

        XT = sb("XT", [P, B * T])
        WQKV = sb("WQKV", [P, 3 * INNER])
        WOUT = sb("WOUT", [P, NI, D])
        Fc = sb("Fc", [P, 2, T])
        sq = sb("sq", [P, 2, T])
        var = sb("var", [64, B // 2, T])
        hid = sb("hid", [64, B // 2, T])
        wsum = sb("wsum", [P, DH])
        wmean = sb("wmean", [P, 2])
        Wc = sb("Wc", [P, DH])
        w1raw = sb("w1raw", [P, 64])
        w1g = sb("w1g", [P, 64])
        gcol = sb("gcol", [P, 1])
        bcol = sb("bcol", [P, 1])
        ones64 = sb("ones64", [P, 64])
        b1col = sb("b1col", [64, 1])
        cbias = sb("cbias", [64, 1])
        w2col = sb("w2col", [64, 1])
        w2sel = sb("w2sel", [64, B // 2, B])
        b2col = sb("b2col", [B, 1])
        bout = sb("bout", [1, D])
        ones8 = sb("ones8", [1, B])
        selb = sb("selb", [B, B, P])
        selh = sb("selh", [B, NH, P])
        rcol = sb("rcol", [P, 1])
        iota32 = sb("iota32", [P, TOPK])
        scores = sb("scores", [B, T])
        cur = sb("cur", [B, 2, T])
        top8 = sb("top8", [B, 8])
        gv = sb("gv", [B, T])
        ones512 = sb("ones512", [B, T])
        mask = sb("mask", [B, T])
        pos = sb("pos", [B, T])
        slot = sb("slot", [B, T])
        slotT = sb("slotT", [P, B, C])
        gT = sb("gT", [P, B, C])
        GR = sb("GR", [P, NC, 2 * TOPK + 1])
        SR = sb("SR", [P, NH, T])
        Xg = sb("Xg", [P, B * TOPK])
        Xc = sb("Xc", [P, B * TOPK])
        xm = sb("xm", [P, B])
        QK = sb("QK", [P, 2 * NI, B * TOPK])
        V = sb("V", [P, NH, INNER])
        S0 = sb("S0", [P, H, TOPK])
        mx = sb("mx", [P, 6, H])
        BD = sb("BD", [P, H, P])
        BDT = sb("BDT", [P, H, P])
        OT = sb("OT", [P, NI, P])
        vmT = sb("vmT", [P, NI, B])
        base = sb("base", [B, D])
        base_all = sb("base_all", [P, B, D])
        delta = sb("delta", [P, NH, D])
        st6 = sb("st6", [P, C, 6])
        mv = sb("mv", [P, NC, 2])
        rs = sb("rs", [P, NC])
        ve = sb("ve", [P, NC])
        y = XT[:, :].rearrange("p (i d) -> p i d", d=D)
        bank = [ctx.enter_context(nc.psum_tensor(f"a{i}", [P, 512], F32)) for i in range(8)]

        ld_gate, ld_zero, ld_x, ld_w = sem("ld_gate"), sem("ld_zero"), sem("ld_x"), sem("ld_w")
        ld_xT = [sem(f"ld_xT{j}") for j in range(4)]
        ld_wq = sem("ld_wq")
        zeroed, consts = sem("zeroed"), sem("consts")
        wc_ready, cb_ps = sem("wc_ready"), sem("cb_ps")
        f_ps, f_sb, g_ps, g_used, std_ready, hpre, gelu, sc_ps = (
            sem(n) for n in ("f_ps", "f_sb", "g_ps", "g_used", "std_ready", "hpre", "gelu", "sc_ps"))
        sc_sb, sig, slot_ready, slotT_ps, slotT_sb, sr_ps, sr_sb, gr_ready = (
            sem(n) for n in ("sc_sb", "sig", "slot_ready", "slotT_ps", "slotT_sb", "sr_ps", "sr_sb", "gr_ready"))
        xs_ps, xs_sb, qk_ps, q_sb, k_sb, v_ps, v_sb, vm_ps, vm_sb, base_ps, base_sb = (
            sem(n) for n in ("xs_ps", "xs_sb", "qk_ps", "q_sb", "k_sb", "v_ps", "v_sb", "vm_ps", "vm_sb", "base_ps", "base_sb"))
        s_ps, s_sb, s_shift, s_exp, em, bd_ready, bdT_ps, bdT_sb, o_ps, o_sb, dl_ps, dl_sb = (
            sem(n) for n in ("s_ps", "s_sb", "s_shift", "s_exp", "em", "bd_ready", "bdT_ps", "bdT_sb", "o_ps", "o_sb",
                             "dl_ps", "dl_sb"))
        xb_ready = sem("xb_ready")
        at_ps, y_ready, ve_ready, rstd_ready = (sem(n) for n in ("at_ps", "y_ready", "ve_ready", "rstd_ready"))
        ms_ready, r1_ready = sem("ms_ready"), sem("r1_ready")
        dve_own, pool_own, act_own = sem("dve_own"), sem("pool_own"), sem("act_own")

        block = ctx.enter_context(nc.Block())

        @block.sync
        def _(sp):
            sp.dma_start(WQKV[:, 0:INNER], wqkvT[:, 0:INNER]).then_inc(ld_wq, 16)
            sp.dma_start(gcol[0:DH, :], ln_g).then_inc(ld_gate, 16)
            sp.dma_start(gcol[DH:P, :], ln_g).then_inc(ld_gate, 16)
            sp.dma_start(bcol[0:DH, :], ln_b).then_inc(ld_gate, 16)
            sp.dma_start(bcol[DH:P, :], ln_b).then_inc(ld_gate, 16)
            sp.dma_start(b2col[:, :], b2g).then_inc(ld_gate, 16)
            sp.wait_ge(zeroed, 1)
            for k in range(2):
                sp.dma_start(w1raw[DH * k:DH * k + DH, GR0 * k:GR0 * k + GH], w1gT).then_inc(ld_zero, 16)
                sp.dma_start(b1col[GR0 * k:GR0 * k + GH, :], b1g).then_inc(ld_zero, 16)
                sp.dma_start(w2col[GR0 * k:GR0 * k + GH, :], w2gT).then_inc(ld_zero, 16)
            for j in range(4):
                sp.dma_start(XT[:, 2 * T * j:2 * T * (j + 1)], xT[:, 2 * T * j:2 * T * (j + 1)]).then_inc(ld_xT[j], 16)
            sp.dma_start(X[:, :, :], x).then_inc(ld_x, 16)
            sp.dma_start(WQKV[:, INNER:3 * INNER], wqkvT[:, INNER:3 * INNER]).then_inc(ld_w, 16)
            sp.dma_start(WOUT[:, :, :], woutT.rearrange("(c p) d -> p c d", p=P)).then_inc(ld_w, 16)
            sp.dma_start(bout[:, :], b_out).then_inc(ld_w, 16)

        @block.gpsimd
        def _(pool):
            own = Chain(pool, pool_own)
            own(pool.memset(w1raw[:, :], 0.0))
            own(pool.memset(b1col[:, :], 0.0))
            pool.memset(w2col[:, :], 0.0).then_inc(zeroed, 1)
            pool.wait_ge(zeroed, 1)
            own(pool.memset(ident[:, :], 0.0))
            own(pool.memset(ones64[:, :], 0.0))
            own(pool.memset(w2sel[:, :, :], 0.0))
            own(pool.memset(selb[:, :, :], 0.0))
            own(pool.memset(selh[:, :, :], 1.0))
            own(pool.memset(ones8[:, :], 1.0))
            own(pool.memset(ones512[:, :], 1.0))
            own(pool.memset(mhalf[:, :], -0.5))
            own(pool.memset(keep["tri"][:, :, :], 1.0))
            own(pool.memset(ones64[0:DH, 0:GH], 1.0 / DH))
            own(pool.memset(ones64[DH:P, GR0:GR0 + GH], 1.0 / DH))
            own(pool.affine_select(out=ident[:, :], in_=ident[:, :], compare_op=ALU.not_equal, fill=1.0, base=0,
                               pattern=[[-1, P]], channel_multiplier=1))
            own(pool.affine_select(out=selb[:, :, :], in_=selb[:, :, :], compare_op=ALU.not_equal, fill=1.0, base=0,
                               pattern=[[-1, B], [0, P]], channel_multiplier=1))
            own(pool.affine_select(out=selh[:, :, :], in_=selh[:, :, :], compare_op=ALU.is_ge, fill=0.0, base=0,
                                   pattern=[[1, NH * P]], channel_multiplier=-TOPK))
            own(pool.affine_select(out=selh[:, :, :], in_=selh[:, :, :], compare_op=ALU.is_ge, fill=0.0,
                               base=TOPK - 1, pattern=[[-1, NH * P]], channel_multiplier=TOPK))
            own(pool.iota(iota32[:, :], pattern=[[1, TOPK]], base=0, channel_multiplier=0,
                      allow_small_or_imprecise_dtypes=True))
            for a in range(HB):
                own(pool.iota(rcol[TOPK * a:TOPK * (a + 1), :], pattern=[[0, 1]], base=0, channel_multiplier=1,
                          allow_small_or_imprecise_dtypes=True))
            own(pool.affine_select(out=keep["tri"][:, :, :], in_=keep["tri"][:, :, :], compare_op=ALU.is_gt, fill=0.0,
                               base=0, pattern=[[1, NE], [-1, NE]], channel_multiplier=0))
            pool.memset(BD[:, :, :], 0.0).then_inc(consts, 1)
            pool.wait_ge(consts, 1)
            own(pool.memset(keep["identb"][:, :], 0.0))
            own(pool.memset(keep["maskb"][:, :], 0.0))
            own(pool.memset(keep["qpad"][:, :, :].bitcast(F32), 0.0))
            own(pool.affine_select(out=keep["identb"][:, :], in_=keep["identb"][:, :], compare_op=ALU.not_equal,
                               fill=1.0, base=0, pattern=[[-1, P]], channel_multiplier=1))
            own(pool.affine_select(out=keep["maskb"][:, :], in_=keep["maskb"][:, :], compare_op=ALU.is_ge,
                               fill=BIG, base=0, pattern=[[-1, P]], channel_multiplier=1))
            pool.wait_ge(ld_x, 16)
            pool.wait_ge(base_sb, 2)
            for b in range(B):
                ts = slice(C * b, C * b + C)
                pool.tensor_tensor(y[:, ts, :], X[:, ts, :], base_all[:, b, :].unsqueeze(1).broadcast_to([P, C, D]),
                                   ALU.add).then_inc(xb_ready, 1)
            for b in range(B):
                cs = slice(C * b, C * b + C)
                pool.wait_ge(ve_ready, b + 1)
                pool.tensor_tensor(rs[:, cs], ve[:, cs], mhalf[:, cs], ALU.pow).then_inc(rstd_ready, 1)
            pool.wait_ge(ms_ready, 1)
            pool.tensor_tensor(r1[:, :], ve[:, :], mhalf[:, :], ALU.pow).then_inc(r1_ready, 1)

        @block.tensor
        def _(pe):
            mm = nc.tensor.matmul
            pe.wait_ge(ld_gate, 16 * 5)
            pe.wait_ge(ld_zero, 16 * 6)
            mm(bank[7][0:64, 0:1], w1raw[:, :], bcol[:, :], start=True, stop=True).then_inc(cb_ps, 1)
            pe.wait_ge(wc_ready, 1)
            pe.wait_ge(consts, 1)

            def features(j):
                pe.wait_ge(ld_xT[j], 16)
                if j >= 2:
                    pe.wait_ge(f_sb, 2 * (j - 1))
                for k in range(2):
                    b = 2 * j + k
                    last = mm(bank[j % 2][DH * k:DH * k + DH, :], Wc[:, :], XT[:, T * b:T * b + T],
                              start=True, stop=True)
                last.then_inc(f_ps, 1)

            features(0)
            for j in range(B // 2):
                if j + 1 < B // 2:
                    features(j + 1)
                pe.wait_ge(f_sb, 2 * j + 2)
                mm(bank[2 + j][0:64, :], w1g[:, :], Fc[:, j % 2, :], start=True, stop=True)
                if j == 1:
                    pe.wait_ge(wc_ready, 2)
                if j >= 2:
                    pe.wait_ge(g_used, j - 1)
                mm(bank[6 + j % 2][0:64, :], ones64[:, :], sq[:, j % 2, :], start=True, stop=True).then_inc(g_ps, 1)
            for j in range(B // 2):
                pe.wait_ge(gelu, j + 1)
                last = mm(bank[0][0:B, :], w2sel[:, j, :], hid[:, j, :], start=(j == 0), stop=(j == B // 2 - 1))
            last.then_inc(sc_ps, 1)

            pe.wait_ge(slot_ready, 1)
            pe.wait_ge(sig, 1)
            for c in range(C):
                nc.tensor.transpose(bank[1][:, B * c:B * c + B], slot[:, P * c:P * c + P], ident[0:B, 0:B])
                last = nc.tensor.transpose(bank[1][:, 64 + B * c:64 + B * c + B], gv[:, P * c:P * c + P],
                                           ident[0:B, 0:B])
            last.then_inc(slotT_ps, 1)
            for n in range(NH):
                last = mm(bank[2 + n][:, :], selh[:, n, :], slot[:, :], start=True, stop=True)
            last.then_inc(sr_ps, 1)

            pe.wait_ge(ld_x, 16)
            pe.wait_ge(gr_ready, 1)
            for b in range(B):
                o = (2 * TOPK + 1) * (b % HB)
                for c in range(C):
                    last = mm(bank[4 + b // HB][:, o:o + 2 * TOPK + 1], X[:, C * b + c, :], GR[:, C * b + c, :],
                              start=(c == 0), stop=(c == C - 1))
            last.then_inc(xs_ps, 1)

            pe.wait_ge(xs_sb, 1)
            pe.wait_ge(ld_w, 48)
            pe.wait_ge(sr_sb, 1)
            for i in range(NI):
                if i >= 4:
                    pe.wait_ge(q_sb, i - 3)
                for k in range(2):
                    n = 2 * i + k
                    last = mm(bank[i % 4][:, 256 * k:256 * k + 256], WQKV[:, P * n:P * n + P], Xg[:, :],
                              start=True, stop=True)
                last.then_inc(qk_ps, 1)
            for n in range(NH):
                for k in range(2):
                    if n == 1:
                        pe.wait_ge(v_sb, k + 1)
                    mm(bank[6 + k][:, :], Xc[:, P * n:P * n + P],
                       WQKV[:, 2 * INNER + 512 * k:2 * INNER + 512 * k + 512], start=True, stop=True).then_inc(v_ps, 1)
            for i in range(NI):
                last = mm(bank[4][:, B * i:B * i + B], WQKV[:, 2 * INNER + P * i:2 * INNER + P * i + P], xm[:, :],
                          start=True, stop=True)
            last.then_inc(vm_ps, 1)
            pe.wait_ge(vm_sb, 1)
            for i in range(NI):
                mm(bank[5][0:B, 0:D], vmT[:, i, :], WOUT[:, i, :], start=(i == 0), stop=False)
            mm(bank[5][0:B, 0:D], ones8[:, :], bout[:, :], start=False, stop=True).then_inc(base_ps, 1)
            pe.wait_ge(base_sb, 1)
            for b in range(B):
                last = mm(bank[4 + b // 4][:, D * (b % 4):D * (b % 4) + D], selb[:, b, :], base[:, :],
                          start=True, stop=True)
            last.then_inc(base_ps, 1)

            pe.wait_ge(q_sb, NI // 2)
            pe.wait_ge(k_sb, NI // 2)
            pe.wait_ge(v_sb, 4)
            pe.wait_ge(base_sb, 2)
            for n in range(NH):
                for q in range(4):
                    if n:
                        pe.wait_ge(bdT_sb, 4)
                    for k in range(4):
                        h = head_at(4 * q + k)
                        rows = slice(DH * (h % 2), DH * (h % 2) + DH)
                        last = mm(bank[q][:, P * k:P * k + P], QK[rows, h // 2, P * n:P * n + P],
                                  QK[rows, NI + h // 2, P * n:P * n + P], start=True, stop=True)
                last.then_inc(s_ps, 1)
                pe.wait_ge(bd_ready, n + 1)
                for q in range(4):
                    for k in range(4):
                        last = nc.tensor.transpose(bank[q][:, P * k:P * k + P], BD[:, 4 * q + k, :], ident[:, :])
                    last.then_inc(bdT_ps, 1)
                pe.wait_ge(bdT_sb, 4 * n + 4)
                if n:
                    pe.wait_ge(o_sb, 2)
                for k in range(H):
                    h = head_at(k)
                    i = h // 2
                    rows = slice(DH * (h % 2), DH * (h % 2) + DH)
                    last = mm(bank[4 + i // 4][rows, P * (i % 4):P * (i % 4) + P], V[:, n, DH * h:DH * h + DH],
                              BDT[:, k, :], start=True, stop=True)
                last.then_inc(o_ps, 1)
                pe.wait_ge(o_sb, 2 * n + 2)
                for i in range(NI):
                    last = mm(bank[6][:, D * n:D * n + D], OT[:, i, :], WOUT[:, i, :], start=(i == 0),
                              stop=(i == NI - 1))
                last.then_inc(dl_ps, 1)
            pe.wait_ge(dl_sb, 2)
            for b in range(B):
                n, a = divmod(b, HB)
                rows = slice(TOPK * a, TOPK * a + TOPK)
                if b >= 4:
                    pe.wait_ge(y_ready, b - 3)
                for c in range(C):
                    last = mm(bank[b % 4][:, D * c:D * c + D], SR[rows, n, P * c:P * c + P], delta[rows, n, :],
                              start=True, stop=True, tile_position=(TOPK * a, 0))
                last.then_inc(at_ps, 1)

        @block.scalar
        def _(act):
            A = nc.scalar.activation
            own = Chain(act, act_own)
            for j in range(B // 2):
                act.wait_ge(f_ps, j + 1)
                if j >= 2:
                    act.wait_ge(g_ps, j - 1)
                A(Fc[:, j % 2, :], bank[j % 2][:, :], ACT.Copy).then_inc(f_sb, 1)
                A(sq[:, j % 2, :], bank[j % 2][:, :], ACT.Square).then_inc(f_sb, 1)
            act.wait_ge(g_used, 4)
            A(var[:, :, :], var[:, :, :], ACT.Sqrt).then_inc(std_ready, 1)
            for j in range(B // 2):
                act.wait_ge(hpre, j + 1)
                A(hid[:, j, :], hid[:, j, :], ACT.Gelu, bias=cbias[:, :]).then_inc(gelu, 1)
            act.wait_ge(sc_sb, 1)
            A(gv[:, :], scores[:, :], ACT.Sigmoid).then_inc(sig, 1)
            act.wait_ge(xs_ps, 1)
            for i in range(NI // 2, NI):
                act.wait_ge(qk_ps, i + 1)
                A(QK[:, 2 * i:2 * i + 2, :], bank[i % 4][:, :].rearrange("p (k t) -> p k t", k=2),
                  ACT.Copy).then_inc(k_sb, 1)
            for n in range(NH):
                for k in range(2):
                    act.wait_ge(v_ps, 2 * n + k + 1)
                    A(V[:, n, 512 * k:512 * k + 512], bank[6 + k][:, :], ACT.Copy).then_inc(v_sb, 1)
            for n in range(NH):
                act.wait_ge(s_shift, 2 * n + 1)
                A(mx[:, 1, :], mx[:, 0, :], ACT.Exp, scale=-1.0).then_inc(em, 1)
                act.wait_ge(s_shift, 2 * n + 2)
                A(S0[:, :, :], S0[:, :, :], ACT.Exp).then_inc(s_exp, 1)
                for q in range(4):
                    act.wait_ge(bdT_ps, 4 * n + q + 1)
                    if n and q == 0:
                        act.wait_ge(o_ps, 1)
                    A(BDT[:, 4 * q:4 * q + 4, :], bank[q][:, :].rearrange("p (k t) -> p k t", k=4),
                      ACT.Copy).then_inc(bdT_sb, 1)
                act.wait_ge(o_ps, n + 1)
                if n:
                    act.wait_ge(dl_ps, 1)
                for i in range(2):
                    A(OT[:, 4 * i:4 * i + 4, :], bank[4 + i][:, :].rearrange("p (k t) -> p k t", k=4),
                      ACT.Copy).then_inc(o_sb, 1)

        @block.vector
        def _(dve):
            V_ = nc.vector
            own = Chain(dve, dve_own)
            dve.wait_ge(ld_wq, 16)
            own(V_.tensor_reduce(wsum[:, :], WQKV[:, 0:INNER].rearrange("p (h e) -> p e h", h=H), AX, ALU.add))
            own(V_.tensor_reduce(wmean[:, 0:1], wsum[:, :], AX, ALU.add))
            own(V_.tensor_scalar(wmean[:, 1:2], wmean[:, 0:1], -1.0 / DH, None, ALU.mult))
            V_.tensor_scalar(Wc[:, :], wsum[:, :], wmean[:, 1:2], 1.0 / H, ALU.add, ALU.mult)
            dve.wait_ge(ld_gate, 16 * 5)
            dve.wait_ge(ld_zero, 16 * 6)
            dve.wait_ge(consts, 1)
            V_.tensor_scalar(w1g[:, :], w1raw[:, :], gcol[:, :], None, ALU.mult)
            V_.tensor_copy(w2sel[0:32, :, :].rearrange("p j b -> p (j b)")[:, 0:31:10],
                           w2col[0:32, :].broadcast_to([32, 4]))
            V_.tensor_copy(w2sel[32:64, :, :].rearrange("p j b -> p (j b)")[:, 1:32:10],
                           w2col[32:64, :].broadcast_to([32, 4])).then_inc(wc_ready, 1)
            dve.wait_ge(cb_ps, 1)
            V_.tensor_tensor(cbias[:, :], bank[7][0:64, 0:1], b1col[:, :], ALU.add).then_inc(wc_ready, 1)
            for j in range(B // 2):
                dve.wait_ge(g_ps, j + 1)
                V_.tensor_scalar(var[:, j, :], bank[6 + j % 2][0:64, :], LN_EPS, None, ALU.add).then_inc(g_used, 1)
            dve.wait_ge(std_ready, 1)
            own(V_.reciprocal(var[:, :, :], var[:, :, :]))
            for j in range(B // 2):
                V_.tensor_tensor(hid[:, j, :], bank[2 + j][0:64, :], var[:, j, :], ALU.mult).then_inc(hpre, 1)
            dve.wait_ge(sc_ps, 1)
            ins = V_.tensor_scalar(scores[:, :], bank[0][0:B, :], b2col[:, :], None, ALU.add)
            ins.then_inc(sc_sb, 1)
            dve.wait_ge(sc_sb, 1)
            src = scores[:, :]
            for i in range(TOPK // 8):
                own(V_.max(top8[:, :], src))
                own(V_.match_replace(cur[:, i % 2, :], top8[:, :], src, NEG_MAX))
                src = cur[:, i % 2, :]
            own(V_.tensor_tensor(mask[:, :], scores[:, :], src, ALU.is_gt))
            own(V_.tensor_tensor_scan(pos[:, :], ones512[:, :], mask[:, :], 0.0, ALU.mult, ALU.add))
            own(V_.tensor_tensor(pos[:, :], pos[:, :], mask[:, :], ALU.mult))
            V_.tensor_scalar(slot[:, :], pos[:, :], -1.0, None, ALU.add).then_inc(slot_ready, 1)
            dve.wait_ge(slotT_ps, 1)
            V_.tensor_copy(slotT[:, :, :], bank[1][:, 0:B * C].rearrange("p (c b) -> p b c", b=B))
            V_.tensor_copy(gT[:, :, :], bank[1][:, 64:64 + B * C].rearrange("p (c b) -> p b c", b=B)
                           ).then_inc(slotT_sb, 1)
            dve.wait_ge(slotT_sb, 1)
            s3 = slotT[:, :, :].rearrange("p b c -> p (b c)").unsqueeze(2).broadcast_to([P, NC, TOPK])
            g3 = gT[:, :, :].rearrange("p b c -> p (b c)").unsqueeze(2).broadcast_to([P, NC, TOPK])
            i3 = iota32[:, :].unsqueeze(1).broadcast_to([P, NC, TOPK])
            own(V_.tensor_tensor(GR[:, :, TOPK:2 * TOPK], s3, i3, ALU.is_equal))
            own(V_.tensor_tensor(GR[:, :, 0:TOPK], GR[:, :, TOPK:2 * TOPK], g3, ALU.mult))
            V_.tensor_scalar(GR[:, :, TOPK:2 * TOPK], GR[:, :, TOPK:2 * TOPK], -1.0 / T, None, ALU.add)
            V_.memset(GR[:, :, 2 * TOPK:], 1.0 / T).then_inc(gr_ready, 1)
            dve.wait_ge(sr_ps, 1)
            for n in range(NH):
                last = V_.tensor_scalar(SR[:, n, :], bank[2 + n][:, :], rcol[:, :], None, ALU.is_equal)
            last.then_inc(sr_sb, 1)
            dve.wait_ge(xs_ps, 1)
            for n in range(NH):
                v = bank[4 + n][:, 0:HB * (2 * TOPK + 1)].rearrange("p (b k) -> p b k", b=HB)
                o = slice(P * n, P * n + P)
                V_.tensor_copy(Xg[:, o].rearrange("p (b k) -> p b k", b=HB), v[:, :, 0:TOPK])
                V_.tensor_copy(Xc[:, o].rearrange("p (b k) -> p b k", b=HB), v[:, :, TOPK:2 * TOPK])
                last = V_.tensor_copy(xm[:, HB * n:HB * n + HB], v[:, :, 2 * TOPK])
            last.then_inc(xs_sb, 1)
            for i in range(NI // 2):
                dve.wait_ge(qk_ps, i + 1)
                V_.tensor_scalar(QK[:, 2 * i:2 * i + 2, :], bank[i % 4][:, :].rearrange("p (k t) -> p k t", k=2),
                                 DH ** -0.5, None, ALU.mult).then_inc(q_sb, 1)
            dve.wait_ge(vm_ps, 1)
            V_.tensor_copy(vmT[:, :, :], bank[4][:, 0:NI * B].rearrange("p (i b) -> p i b", b=B)).then_inc(vm_sb, 1)
            dve.wait_ge(base_ps, 1)
            V_.tensor_copy(base[:, :], bank[5][0:B, 0:D]).then_inc(base_sb, 1)
            dve.wait_ge(base_ps, 2)
            for n in range(2):
                last = V_.tensor_copy(base_all[:, 4 * n:4 * n + 4, :],
                                      bank[4 + n][:, :].rearrange("p (b d) -> p b d", b=4))
            last.then_inc(base_sb, 1)
            m, e_, s, r, u, neg = (mx[:, k, :] for k in range(6))
            for n in range(NH):
                dve.wait_ge(s_ps, n + 1)
                for q in range(4):
                    for a in range(HB):
                        rows = slice(TOPK * a, TOPK * a + TOPK)
                        last = V_.tensor_copy(S0[rows, 4 * q:4 * q + 4, :],
                                              bank[q][rows, :].rearrange("p (k t) -> p k t", k=4)[:, :, rows])
                own(last)
                own(V_.tensor_reduce(m, S0[:, :, :], AX, ALU.max))
                V_.tensor_scalar(m, m, 0.0, None, ALU.max).then_inc(s_shift, 1)
                dve.wait_ge(s_shift, 2 * n + 1)
                V_.tensor_tensor(S0[:, :, :], S0[:, :, :], m.unsqueeze(2).broadcast_to([P, H, TOPK]),
                                 ALU.subtract).then_inc(s_shift, 1)
                dve.wait_ge(em, n + 1)
                dve.wait_ge(s_exp, n + 1)
                own(V_.tensor_reduce(s, S0[:, :, :], AX, ALU.add))
                own(V_.scalar_tensor_tensor(out=s, in0=e_, scalar=float(T - TOPK), in1=s, op0=ALU.mult, op1=ALU.add))
                own(V_.reciprocal(r, s))
                V_.tensor_tensor(u, e_, r, ALU.mult)
                own(V_.tensor_tensor(S0[:, :, :], S0[:, :, :], r.unsqueeze(2).broadcast_to([P, H, TOPK]), ALU.mult))
                if n:
                    dve.wait_ge(bdT_ps, 4)
                for a in range(HB):
                    rows = slice(TOPK * a, TOPK * a + TOPK)
                    last = V_.tensor_tensor(BD[rows, :, rows], S0[rows, :, :],
                                            u[rows].unsqueeze(2).broadcast_to([TOPK, H, TOPK]), ALU.subtract)
                last.then_inc(bd_ready, 1)
                dve.wait_ge(dl_ps, n + 1)
                V_.tensor_copy(delta[:, n, :], bank[6][:, D * n:D * n + D]).then_inc(dl_sb, 1)

            def normalise(b):
                dve.wait_ge(rstd_ready, b + 1)
                for c in range(C):
                    i = C * b + c
                    last = V_.tensor_scalar(X[:, i, :], y[:, i, :], mv[:, i, 0:1], rs[:, i:i + 1],
                                            ALU.subtract, ALU.mult)
                return last

            for b in range(B):
                dve.wait_ge(at_ps, b + 1)
                dve.wait_ge(xb_ready, b + 1)
                V_.tensor_tensor(y[:, C * b:C * b + C, :], y[:, C * b:C * b + C, :],
                                 bank[b % 4][:, :].rearrange("p (c d) -> p c d", c=C), ALU.add).then_inc(y_ready, 1)
                dve.wait_ge(y_ready, b + 1)
                for c in range(C):
                    last = V_.bn_stats(st6[:, c, :], y[:, C * b + c, :])
                own(last)
                for c in range(C):
                    last = V_.bn_aggr(mv[:, C * b + c, :], st6[:, c, :])
                own(last)
                V_.tensor_scalar(ve[:, C * b:C * b + C], mv[:, C * b:C * b + C, 1], LN_EPS, None,
                                 ALU.add).then_inc(ve_ready, 1)
                if b:
                    normalise(b - 1)
            own(normalise(B - 1))
            own(V_.tensor_tensor(rs[:, :], rs[:, :], rs[:, :], ALU.mult))
            own(V_.tensor_tensor(rs[:, :], rs[:, :], mv[:, :, 1], ALU.mult))
            V_.tensor_scalar(ve[:, :], rs[:, :], RMS_EPS, None, ALU.add).then_inc(ms_ready, 1)
            dve.wait_ge(r1_ready, 1)


SCORE_STEPS, WEIGHT_STEPS = 12, 12
SCORES = ([(c, h, 2) for c in (0, 1) for h in (0, 2)] + [(c, h, 1) for c in (2, 3) for h in range(4)])
WEIGHTS = ([(c, h, 1) for c in (0, 1) for h in range(4)] + [(c, h, 2) for c in (2, 3) for h in (0, 2)])
WEIGHED = [4, 8, 10, 12]
ADD_LAG = 4
FIRST_UNIT, UNITS_PER_SLOT = 17, 0.74
SPARE = ("turn", "attnT", "project", "tokensT", "logits", "shiftT", "keys", "queries", "nextT", "qkv")


def order_of_trip():
    steps = []
    at = {
        0: [("here", "shift", 1)],
        1: [("here", "keys", 3)],
        2: [("here", "queries", 3), ("here", "place", 3)],
        3: [("here", "shiftT", 1), ("end", "add", NE - 1)],
        4: [("rest", "turn", 0), ("end", "norm", 0)],
        5: [("rest", "turn", 1), ("ahead", "next", 0)],
        6: [("rest", "turn", 2)],
        7: [("rest", "turn", 3), ("end", "norm root", 0)],
        8: [("ahead", "nextT", 0)],
        9: [("rest", "attnT", 0), ("end", "result", 0)],
        10: [("ahead", "qkv", 0), ("ahead", "parts", 0)],
        11: [("rest", "project", 0), ("rest", "statistics", 0)],
        12: [("rest", "root", 0), ("here", "shift", 2), ("ahead", "qkv", 1), ("ahead", "parts", 1)],
        13: [("ahead", "qkv", 2), ("ahead", "parts", 2)],
        14: [("rest", "scale", 0), ("rest", "residuals", 0)],
        15: [("here", "shiftT", 2)],
        16: [("rest", "tokensT", 0), ("rest", "split", 0)],
        17: [("ahead", "qkv", 3), ("ahead", "parts", 3)],
        18: [("rest", "logits", 0), ("rest", "rank", 0), ("ahead", "values", 0)],
        19: [("ahead", "keys", 4)],
        20: [("ahead", "queries", 4), ("ahead", "place", 4)],
        21: [("rest", "combine", 0)],
        24: [("here", "shift", 3)],
        25: [("ahead", "keys", 5)],
        26: [("ahead", "queries", 5), ("ahead", "place", 5)],
        27: [("here", "shiftT", 3)],
        30: [("ahead", "values", 1)],
        36: [("ahead", "shift", 4)],
        37: [("ahead", "keys", 6)],
        38: [("ahead", "queries", 6), ("ahead", "place", 6)],
        39: [("ahead", "shiftT", 4)],
        42: [("ahead", "values", 2)],
    }
    units = [("hidden", 0)]
    for e in range(NE):
        units += [("hidden", k) for k in (2 * e + 1, 2 * e + 2) if k < 2 * NE - 1]
        units += [("hidden", 2 * NE - 1)] * (e == NE - 2) + [("down", e)]
    lagging = []

    def unit():
        if units:
            what = units.pop(0)
            steps.append(("rest",) + what)
            lagging.append([what, 0])
        for item in list(lagging):
            item[1] += 1
            if item[1] == 2:
                steps.append(("rest", {"hidden": "gate", "down": "sum"}[item[0][0]], item[0][1]))
                if item[0][0] == "hidden":
                    lagging.remove(item)
            elif item[1] == ADD_LAG:
                if item[0][1] < NE - 1:
                    steps.append(("rest", "add", item[0][1]))
                lagging.remove(item)

    owed = 0.0
    for slot in range(NG * WEIGHT_STEPS):
        n = slot + 2 * SCORE_STEPS
        steps.append(("here", "weight", slot))
        part = "here" if n < NG * SCORE_STEPS else "ahead"
        steps.append((part, "score", n))
        if slot % SCORE_STEPS == 0 and slot:
            before = "here" if n - 1 < NG * SCORE_STEPS else "ahead"
            steps.append((before, "maximum", n - 1))
        elif slot % SCORE_STEPS:
            steps.append((part, "maximum", n - 1))
        g, k = divmod(slot, WEIGHT_STEPS)
        for c in range(C):
            if (k - 1) % WEIGHT_STEPS == WEIGHED[c] % WEIGHT_STEPS and slot > 1:
                done = C * g + c - (C if k == 1 else 0)
                steps.append(("here", "value", done))
                if done % C == C - 1:
                    steps.append(("here", "heads", done // C))
        steps += at.get(slot, [])
        if slot >= FIRST_UNIT:
            owed += UNITS_PER_SLOT
            while owed >= 1:
                unit()
                owed -= 1
    steps.append(("ahead", "maximum", 6 * SCORE_STEPS - 1))
    unit()
    steps += [("here", "value", NG * C - 1), ("here", "heads", NG - 1), ("ahead", "values", 3)]
    while units or lagging:
        unit()
    return steps


def causal_attention_and_experts(nc, keep, g1, Wq, WdkvT, Wuk, Wuv, Wo, g2, gate_w, w1, w2, out):
    X, ident, identb, maskb = keep["X"], keep["ident"], keep["identb"], keep["maskb"]
    qpad, r1, mhalf, tri = keep["qpad"], keep["r1"], keep["mhalf"], keep["tri"]
    ctx = ExitStack()
    with ctx:
        def sb(name, shape, dt=F32):
            return ctx.enter_context(nc.sbuf_tensor(name, shape, dt))

        def sem(name):
            return ctx.enter_context(nc.semaphore(name))

        w1h = sb("w1h", [P, NE, EH], F32R)
        w1l = sb("w1l", [P, NE, EH], F32R)
        wexp2 = sb("wexp2", [P, NE, 2, D])
        wgate = sb("wgate", [P, NE])
        wqkv = sb("wqkv", [P, 3 * D])
        wo = sb("wo", [P, D])
        wd = sb("wd", [LAT, D])
        wu = sb("wu", [LAT, 2, D])
        g1c, g2c = sb("g1c", [P, 1]), sb("g2c", [P, 1])
        xr = sb("xr", [P, C, D])
        xrT = sb("xrT", [P, T])
        qs = sb("qs", [P, C, MH, R], F32R)
        ks = sb("ks", [P, C, MH, R], F32R)
        qT = sb("qT", [P, NG, T], F32R)
        kT = sb("kT", [P, NG, T], F32R)
        va = sb("va", [P, C, MH, R])
        negmax = sb("negmax", [P, 2, C, 4])
        shift = sb("shift", [P, C, 4, 2], F32R)
        shiftT = sb("shiftT", [4 * 2, 2, T], F32R)
        prob = sb("prob", [P, 2, 4, T])
        oT = sb("oT", [P, NG, T])
        rden = sb("rden", [P, C, MH])
        attn = sb("attn", [P, C, D])
        attnT = sb("attnT", [P, T])
        x2 = sb("x2", [P, C, D])
        prod = sb("prod", [P, 2, C, D])
        t = sb("t", [P, C, D])
        tT = sb("tT", [P, T])
        st2, mv2, ms2, r2 = sb("st2", [P, C, 6]), sb("mv2", [P, C, 2]), sb("ms2", [P, C]), sb("r2", [P, C])
        st3, mv3, ve3, rs3 = sb("st3", [P, C, 6]), sb("mv3", [P, C, 2]), sb("ve3", [P, C]), sb("rs3", [P, C])
        lg, ex = sb("lg", [P, C, NE]), sb("ex", [P, C, NE])
        before, equal = sb("before", [P, C, NE, NE]), sb("equal", [P, C, NE, NE])
        rank, top1 = sb("rank", [P, C, NE]), sb("top1", [P, C])
        wsum, wrec = sb("wsum2", [P, C]), sb("wrec", [P, C])
        comb = sb("comb", [P, C, NE])
        hid = sb("hid2", [P, 2, 2, T])
        tanh = sb("tanh", [P, 2, T])
        vstage = sb("vstage", [P, C, D])
        tTh, tTl = sb("tTh", [P, T], F32R), sb("tTl", [P, T], F32R)
        acc = sb("acc", [P, C, D])
        outb = sb("outb", [P, C, D])
        w1raw = prob[:, 0, :, :].rearrange("p a t -> p (a t)").rearrange("p (e h) -> p e h", e=NE)
        psS = ctx.enter_context(nc.psum_tensor("psS", [P, 2, 512], F32))
        psW = ctx.enter_context(nc.psum_tensor("psW", [P, 2, 512], F32))
        psV = ctx.enter_context(nc.psum_tensor("psV", [P, 512], F32))
        psHid = ctx.enter_context(nc.psum_tensor("psHid", [P, 512], F32))
        psY = ctx.enter_context(nc.psum_tensor("psY", [P, 512], F32))
        spare = ctx.enter_context(nc.psum_tensor("spare", [P, 512], F32))

        names = """ld_w ld_e const w_ps w_ready xr_ready spare_full spare_read v_placed qpad_in s_ps max_ready
            shift_ready shift_in st_ps exp_ready masked pv_done oT_sb high_ready prod_ready prod_used both_ready ms2_ready r2_ready t_ready
            tT_split lg_shift lg_exp comb_ready hid_ps tanh_ready hid_ready y_ps y_used ve3_ready rs3_ready
            out_ready out_done own_pool own_dve steps_dve steps_pool""".split()
        s = {n: sem(n) for n in names}
        full = order_of_trip()
        kinds = [[step[1:] for step in full if step[0] in parts] for parts in
                 (("ahead",), ("here", "ahead"), ("here", "rest", "ahead"), ("here", "rest", "end", "ahead"),
                  ("here", "rest", "end"), ("rest", "end"), ("end",))]
        uses = [sum(step[0] in SPARE for step in steps) for steps in kinds]

        def run(eng, trip, chain=None, meanwhile=None):
            used = 0
            for b in range(-1, 2):
                if b == 0 and meanwhile:
                    meanwhile()
                trip(kinds[b + 1], b, used)
                used += uses[b + 1]
            if chain:
                before, chain.n = chain.base + chain.n, 0
            with eng.Fori(2, B - 1) as b:
                if chain:
                    chain.base = before + (b - 2) * OWN_PER_TRIP
                trip(kinds[3], b, used + (b - 2) * uses[3])
            used += (B - 3) * uses[3]
            if chain:
                assert chain.n == OWN_PER_TRIP, chain.n
                chain.base, chain.n = before + (B - 3) * OWN_PER_TRIP, 0
            for b in range(B - 1, B + 2):
                trip(kinds[b - B + 5], b, used)
                used += uses[b - B + 5]

        def counter(steps, used):
            place = {step: used + i + 1 for i, step in enumerate(t for t in steps if t[0] in SPARE)}
            return lambda what, n=0: place[what, n]

        def wait(eng, name, count):
            if not isinstance(count, int) or count > 0:
                eng.wait_ge(s[name], count)

        out_v = out.rearrange("b (c p) d -> p (b c) d", p=P)
        block = ctx.enter_context(nc.Block())

        @block.sync
        def _(sp):
            sp.dma_start(wd[:, :], WdkvT).then_inc(s["ld_w"], 16)
            sp.dma_start(wu[:, 0, :], Wuk).then_inc(s["ld_w"], 16)
            sp.dma_start(wu[:, 1, :], Wuv).then_inc(s["ld_w"], 16)
            sp.dma_start(g1c[:, :], g1).then_inc(s["ld_w"], 16)
            sp.dma_start(wqkv[:, 0:D], Wq).then_inc(s["ld_w"], 16)
            sp.dma_start(wo[:, :], Wo).then_inc(s["ld_w"], 16)
            sp.dma_start(g2c[:, :], g2).then_inc(s["ld_e"], 16)
            sp.dma_start(wgate[:, :], gate_w).then_inc(s["ld_e"], 16)
            sp.dma_start(w1raw, w1.rearrange("e d h -> d e h")).then_inc(s["ld_e"], 16)
            sp.dma_start(wexp2[:, :, :, :], w2.rearrange("e (k p) d -> p e k d", p=P)).then_inc(s["ld_e"], 16)

            def trip(steps, b, used):
                use = counter(steps, used)
                for what, n in steps:
                    if what == "place":
                        sp.wait_ge(s["spare_read"], use("queries", n))
                        wait(sp, "st_ps", WEIGHT_STEPS * (NG * b + n - 3))
                        for a in range(4):
                            rows = slice(R * a, R * a + R)
                            sp.dma_start(qpad[rows, 4 * (n % NG) + a, :].bitcast(F32),
                                         qT[rows, n % NG, :].bitcast(F32)).then_inc(s["qpad_in"], 16)
                    elif what == "shiftT":
                        sp.wait_ge(s["spare_read"], use("shiftT", n))
                        wait(sp, "s_ps", SCORE_STEPS * (NG * b + n + 1))
                        for a in range(4):
                            row = R * a + SHIFT
                            sp.dma_start(qpad[row:row + 2, 4 * (n % NG) + a, :].bitcast(F32),
                                         shiftT[2 * a:2 * a + 2, n % 2, :].bitcast(F32)).then_inc(s["shift_in"], 16)
                    elif what == "result":
                        sp.wait_ge(s["out_ready"], b - 1)
                        sp.dma_start(out_v[:, ds(C * (b - 2), C), :], outb[:, :, :]).then_inc(s["out_done"], 16)

            run(sp, trip)
            sp.wait_ge(s["out_done"], 16 * B + 16)

        @block.gpsimd
        def _(pool):
            own = Chain(pool, s["own_pool"])
            own(pool.memset(va[:, :, :, :], 0.0))
            own(pool.memset(va[:, :, :, MD:MD + 1], 1.0))
            own(pool.memset(qs[:, :, :, :].bitcast(F32), 0.0))
            own(pool.memset(ks[:, :, :, :].bitcast(F32), 0.0))
            pool.memset(ks[:, :, :, SHIFT:SHIFT + 2].bitcast(F32), 1.0).then_inc(s["const"], 1)
            pool.wait_ge(s["const"], 1)

            def trip(steps, b, used):
                use = counter(steps, used)
                m = b - 1
                for what, n in steps:
                    if what == "values":
                        pool.wait_ge(s["spare_read"], use("qkv", C - 1))
                        wait(pool, "pv_done", NG * C * b + C * n + C)
                        if not isinstance(b, int):
                            pool.sem_inc(s["steps_pool"], 1)
                        for c in range(C):
                            last = pool.tensor_copy(va[:, c, 4 * n:4 * n + 4, 0:MD],
                                                    vstage[:, c, 4 * MD * n:4 * MD * n + 4 * MD].rearrange(
                                                        "p (h m) -> p h m", m=MD))
                        last.then_inc(s["v_placed"], 1)
                    elif what == "root":
                        pool.wait_ge(s["ms2_ready"], m + 1)
                        pool.tensor_tensor(r2[:, :], ms2[:, :], mhalf[:, 0:C], ALU.pow).then_inc(s["r2_ready"], 1)
                    elif what == "residuals":
                        pool.wait_ge(s["spare_read"], use("project"))
                        wait(pool, "out_ready", m)
                        pool.tensor_tensor(acc[:, :, :], X[:, ds(C * m, C), :], x2[:, :, :],
                                           ALU.add).then_inc(s["both_ready"], 1)
                    elif what == "value":
                        g, kc = divmod(n, C)
                        pool.wait_ge(s["exp_ready"], WEIGHT_STEPS * (NG * b + g) + WEIGHED[kc])
                        if not isinstance(b, int):
                            pool.sem_inc(s["steps_pool"], 1)
                        blk = prob[:, n % 2, :, P * kc:P * kc + P]
                        pool.affine_select(out=blk, in_=blk, compare_op=ALU.is_ge, fill=0.0, base=0,
                                           pattern=[[0, 4], [1, P]], channel_multiplier=-1).then_inc(s["masked"], 1)
                    elif what == "add":
                        of = m if n < NE - 1 else m - 1
                        if n == 0:
                            pool.wait_ge(s["both_ready"], of + 1)
                        else:
                            pool.wait_ge(s["prod_used"], NE * of + n)
                        pool.wait_ge(s["y_used"], NE * of + n + 1)
                        pool.tensor_tensor(acc[:, :, :], acc[:, :, :], prod[:, n % 2, :, :],
                                           ALU.add).then_inc(s["prod_used"], 1)
                    elif what == "norm root":
                        pool.wait_ge(s["ve3_ready"], m)
                        pool.tensor_tensor(rs3[:, :], ve3[:, :], mhalf[:, 0:C], ALU.pow).then_inc(s["rs3_ready"], 1)

            run(pool, trip)

        @block.tensor
        def _(pe):
            mm, tr = nc.tensor.matmul, nc.tensor.transpose
            pe.wait_ge(s["ld_w"], 16 * 6)
            mm(psS[:, 0, 0:2 * D], wd[:, :], wu[:, :, :], start=True, stop=True).then_inc(s["w_ps"], 1)
            pe.wait_ge(s["w_ready"], 1)

            def trip(steps, b, used):
                use = counter(steps, used)
                m = b - 1
                for what, n in steps:
                    if what in SPARE:
                        wait(pe, "spare_read", use(what, n) - 1)
                    if what == "nextT":
                        pe.wait_ge(s["xr_ready"], b + 2)
                        for c in range(C):
                            last = tr(spare[:, P * c:P * c + P], xr[:, c, :], ident[:, :])
                        last.then_inc(s["spare_full"], 1)
                    elif what == "qkv":
                        mm(spare[:, 0:3 * D], xrT[:, P * n:P * n + P], wqkv[:, :], start=True,
                           stop=True).then_inc(s["spare_full"], 1)
                    elif what in ("keys", "queries"):
                        stack = ks if what == "keys" else qs
                        h = 4 * (n % NG)
                        for c in range(C):
                            last = tr(spare[:, P * c:P * c + P],
                                      stack[:, c, h:h + 4, :].rearrange("p h r -> p (h r)").bitcast(F32), ident[:, :])
                        last.then_inc(s["spare_full"], 1)
                    elif what == "turn":
                        if n == 0:
                            pe.wait_ge(s["oT_sb"], NG * m + NG)
                        for g in range(NG):
                            last = tr(spare[:, P * g:P * g + P], oT[:, g, P * n:P * n + P], ident[:, :])
                        last.then_inc(s["spare_full"], 1)
                    elif what == "attnT":
                        for c in range(C):
                            last = tr(spare[:, P * c:P * c + P], attn[:, c, :], ident[:, :])
                        last.then_inc(s["spare_full"], 1)
                    elif what == "project":
                        for c in range(C):
                            last = mm(spare[:, D * c:D * c + D], attnT[:, P * c:P * c + P], wo[:, :], start=True,
                                      stop=True)
                        last.then_inc(s["spare_full"], 1)
                    elif what == "tokensT":
                        pe.wait_ge(s["t_ready"], m + 1)
                        for c in range(C):
                            last = tr(spare[:, P * c:P * c + P], t[:, c, :], ident[:, :])
                        last.then_inc(s["spare_full"], 1)
                    elif what == "logits":
                        for c in range(C):
                            last = mm(spare[:, NE * c:NE * c + NE], tT[:, P * c:P * c + P], wgate[:, :], start=True,
                                      stop=True)
                        last.then_inc(s["spare_full"], 1)
                    elif what == "hidden":
                        e, k = divmod(n, 2)
                        if n == 0:
                            pe.wait_ge(s["tT_split"], m + 1)
                        else:
                            pe.wait_ge(s["hid_ready"], 2 * NE * m + n)
                        for i, (w, v) in enumerate(((w1h, tTh), (w1h, tTl), (w1l, tTh))):
                            last = mm(psHid[:, :], w[:, e, P * k:P * k + P], v[:, :], start=(i == 0), stop=(i == 2))
                        last.then_inc(s["hid_ps"], 1)
                    elif what == "down":
                        pe.wait_ge(s["hid_ready"], 2 * NE * m + 2 * n + 2)
                        if n:
                            pe.wait_ge(s["y_used"], NE * m + n)
                        for c in range(C):
                            for k in range(2):
                                last = mm(psY[:, D * c:D * c + D], hid[:, n % 2, k, P * c:P * c + P],
                                          wexp2[:, n, k, :], start=(k == 0), stop=(k == 1))
                        last.then_inc(s["y_ps"], 1)
                    elif what == "score":
                        u, i = divmod(n, SCORE_STEPS)
                        g = u % NG
                        c, first, heads = SCORES[i]
                        if i == 0:
                            pe.wait_ge(s["qpad_in"], 64 * (NG * b + u + 1))
                        wait(pe, "max_ready", NG * SCORE_STEPS * b + n - 1)
                        for j in range(heads):
                            dst = psS[:, n % 2, 256 * j:512]
                            keys = max(P * (c + 1), 256)
                            mm(dst[:, 0:keys], qpad[:, 4 * g + first + j, P * c:P * c + P], kT[:, g, 0:keys],
                               start=True, stop=False)
                            last = mm(dst[:, P * c:P * c + P], identb[:, :], maskb[:, :], start=False, stop=True)
                        last.then_inc(s["s_ps"], 1)
                    elif what == "shiftT":
                        pe.wait_ge(s["shift_ready"], NG * b + n + 1)
                        for c in range(C):
                            last = tr(spare[0:8, P * c:P * c + P],
                                      shift[:, c, :, :].rearrange("p a j -> p (a j)").bitcast(F32), ident[:, :])
                        last.then_inc(s["spare_full"], 1)
                    elif what == "weight":
                        g, i = divmod(n, WEIGHT_STEPS)
                        kc, first, heads = WEIGHTS[i]
                        if i == 0:
                            pe.wait_ge(s["shift_in"], 64 * (NG * b + g + 1))
                        wait(pe, "exp_ready", NG * WEIGHT_STEPS * b + n - 1)
                        q0 = min(P * kc, 256)
                        for j in range(heads):
                            last = mm(psW[:, n % 2, 256 * j:256 * j + T - q0], kT[:, g, P * kc:P * kc + P],
                                      qpad[:, 4 * g + first + j, q0:T], start=True, stop=True)
                        last.then_inc(s["st_ps"], 1)
                    elif what == "value":
                        g, kc = divmod(n, C)
                        pe.wait_ge(s["masked"], NG * C * b + n + 1)
                        if kc == 0:
                            pe.wait_ge(s["v_placed"], NG * b + g + 1)
                            wait(pe, "oT_sb", NG * b + g)
                        for a in range(4):
                            last = mm(psV[R * a:R * a + R, P * kc:T], va[:, kc, 4 * g + a, :],
                                      prob[:, n % 2, a, P * kc:T], start=(kc == 0), stop=(kc == C - 1),
                                      tile_position=(0, R * a))
                        last.then_inc(s["pv_done"], 1)

            run(pe, trip)

        @block.scalar
        def _(act):
            A = nc.scalar.activation

            def trip(steps, b, used):
                use = counter(steps, used)
                m = b - 1
                for what, n in steps:
                    if what in ("nextT", "attnT", "tokensT", "keys", "queries", "shiftT"):
                        act.wait_ge(s["spare_full"], use(what, n))
                    if what == "nextT":
                        A(xrT[:, :], spare[:, :], ACT.Copy).then_inc(s["spare_read"], 1)
                    elif what == "parts":
                        act.wait_ge(s["spare_full"], use("qkv", n))
                        q, k = (spare[:, D * i:D * i + D].rearrange("p (h m) -> p h m", m=MD).unsqueeze(
                            2).broadcast_to([P, MH, 2, MD]) for i in range(2))
                        A(qs[:, n, :, 0:2 * MD].rearrange("p h (j m) -> p h j m", j=2), q, ACT.Copy)
                        A(ks[:, n, :, :].rearrange("p h (j m) -> p h j m", j=2)[:, :, :, 0:MD], k, ACT.Copy)
                        if n == 0:
                            wait(act, "v_placed", NG * (b + 1))
                        A(vstage[:, n, :], spare[:, 2 * D:3 * D], ACT.Copy).then_inc(s["high_ready"], 1)
                    elif what == "attnT":
                        A(attnT[:, :], spare[:, :], ACT.Copy).then_inc(s["spare_read"], 1)
                    elif what == "keys":
                        wait(act, "st_ps", WEIGHT_STEPS * (NG * b + n - 3))
                        A(kT[:, n % NG, :], spare[:, :], ACT.Copy).then_inc(s["spare_read"], 1)
                    elif what == "queries":
                        wait(act, "qpad_in", 64 * (NG * b + n - 3))
                        A(qT[:, n % NG, :], spare[:, :], ACT.Copy).then_inc(s["spare_read"], 1)
                    elif what == "shiftT":
                        wait(act, "shift_in", 64 * (NG * b + n - 1))
                        A(shiftT[:, n % 2, :], spare[0:8, :], ACT.Copy).then_inc(s["spare_read"], 1)
                    elif what == "tokensT":
                        A(tTh[:, :], spare[:, :], ACT.Copy)
                        A(tT[:, :], spare[:, :], ACT.Copy).then_inc(s["spare_read"], 1)
                    elif what == "combine":
                        act.wait_ge(s["lg_shift"], m + 1)
                        A(ex[:, :, :], lg[:, :, :], ACT.Exp).then_inc(s["lg_exp"], 1)
                    elif what == "hidden":
                        act.wait_ge(s["hid_ps"], 2 * NE * m + n + 1)
                        A(tanh[:, n % 2, :], psHid[:, :], ACT.Tanh, scale=0.5).then_inc(s["tanh_ready"], 1)
                    elif what == "heads":
                        act.wait_ge(s["pv_done"], NG * C * b + C * n + C)
                        if n == 0 and ("turn", 0) in steps:
                            act.wait_ge(s["spare_full"], use("turn", C - 1))
                        A(oT[:, n, :], psV[:, :], ACT.Copy).then_inc(s["oT_sb"], 1)
                    elif what == "weight":
                        g, i = divmod(n, WEIGHT_STEPS)
                        kc, first, heads = WEIGHTS[i]
                        if n == 0 and isinstance(b, int) and b == 0:
                            act.wait_ge(s["w_ready"], 2)
                        if first == 0:
                            wait(act, "pv_done", NG * C * b + C * g + kc - 1)
                        act.wait_ge(s["st_ps"], NG * WEIGHT_STEPS * b + n + 1)
                        skip = P * kc - min(P * kc, 256)
                        width = T - P * kc
                        src = psW[:, n % 2, :].rearrange("p (j t) -> p j t", j=heads)[:, :, skip:skip + width]
                        A(prob[:, kc % 2, first:first + heads, P * kc:T], src, ACT.Exp).then_inc(s["exp_ready"], 1)

            run(act, trip)

        @block.vector
        def _(dve):
            V = nc.vector
            own = Chain(dve, s["own_dve"])

            def trip(steps, b, used):
                use = counter(steps, used)
                m = b - 1
                for what, n in steps:
                    if what == "next":
                        for c in range(C):
                            last = V.tensor_scalar(xr[:, c, :], X[:, ds(C * (b + 1) + c, 1), :],
                                                   r1[:, ds(C * (b + 1) + c, 1)], None, ALU.mult)
                        last.then_inc(s["xr_ready"], 1)
                    elif what == "parts":
                        dve.wait_ge(s["high_ready"], C * (b + 1) + n + 1)
                        q, k = (spare[:, D * i:D * i + D].rearrange("p (h m) -> p h m", m=MD) for i in range(2))
                        V.tensor_tensor(qs[:, n, :, 2 * MD:3 * MD], q, qs[:, n, :, 0:MD].bitcast(F32), ALU.subtract)
                        V.tensor_tensor(ks[:, n, :, MD:2 * MD], k, ks[:, n, :, 0:MD].bitcast(F32),
                                        ALU.subtract).then_inc(s["spare_read"], 1)
                    elif what == "maximum":
                        u, i = divmod(n, SCORE_STEPS)
                        c, first, heads = SCORES[i]
                        dve.wait_ge(s["s_ps"], NG * SCORE_STEPS * b + n + 1)
                        src = psS[:, n % 2, :].rearrange("p (j t) -> p j t", j=heads)[:, :, 0:P * (c + 1)]
                        V.tensor_reduce(negmax[:, u % 2, c, first:first + heads], src, AX, ALU.max,
                                        negate=True).then_inc(s["max_ready"], 1)
                    elif what == "shift":
                        dve.wait_ge(s["max_ready"], SCORE_STEPS * (NG * b + n + 1))
                        own(V.tensor_copy(shift[:, :, :, 0], negmax[:, n % 2, :, :]))
                        V.tensor_tensor(shift[:, :, :, 1], negmax[:, n % 2, :, :], shift[:, :, :, 0].bitcast(F32),
                                        ALU.subtract).then_inc(s["shift_ready"], 1)
                    elif what == "turn":
                        dve.wait_ge(s["spare_full"], use("turn", n))
                        src = spare[:, :].rearrange("p (h r) -> p h r", r=R)
                        own(V.reciprocal(rden[:, n, :], src[:, :, MD]))
                        V.tensor_tensor(attn[:, n, :].rearrange("p (h m) -> p h m", m=MD), src[:, :, 0:MD],
                                        rden[:, n, :].unsqueeze(2).broadcast_to([P, MH, MD]),
                                        ALU.mult).then_inc(s["spare_read"], 1)
                    elif what == "statistics":
                        dve.wait_ge(s["spare_full"], use("project"))
                        V.tensor_tensor(x2[:, :, :], X[:, ds(C * m, C), :],
                                        spare[:, :].rearrange("p (c d) -> p c d", d=D),
                                        ALU.add).then_inc(s["spare_read"], 1)
                        dve.wait_ge(s["spare_read"], use("project"))
                        for c in range(C):
                            last = V.bn_stats(st2[:, c, :], x2[:, c, :])
                        own(last)
                        dve.sem_inc(s["steps_dve"], 1)
                        for c in range(C):
                            last = V.bn_aggr(mv2[:, c, :], st2[:, c, :])
                        own(last)
                        own(V.tensor_tensor(ms2[:, :], mv2[:, :, 0], mv2[:, :, 0], ALU.mult))
                        V.scalar_tensor_tensor(out=ms2[:, :], in0=ms2[:, :], scalar=RMS_EPS, in1=mv2[:, :, 1],
                                               op0=ALU.add, op1=ALU.add).then_inc(s["ms2_ready"], 1)
                    elif what == "scale":
                        dve.wait_ge(s["r2_ready"], m + 1)
                        for c in range(C):
                            last = V.tensor_scalar(t[:, c, :], x2[:, c, :], r2[:, c:c + 1], None, ALU.mult)
                        last.then_inc(s["t_ready"], 1)
                    elif what == "split":
                        dve.wait_ge(s["spare_read"], use("tokensT"))
                        V.tensor_tensor(tTl[:, :], tT[:, :], tTh[:, :].bitcast(F32),
                                        ALU.subtract).then_inc(s["tT_split"], 1)
                    elif what == "rank":
                        dve.wait_ge(s["spare_full"], use("logits"))
                        V.tensor_copy(lg[:, :, :], spare[:, 0:C * NE].rearrange("p (c e) -> p c e", e=NE)
                                      ).then_inc(s["spare_read"], 1)
                        dve.wait_ge(s["spare_read"], use("logits"))
                        other = lg[:, :, :].unsqueeze(2).broadcast_to([P, C, NE, NE])
                        this = lg[:, :, :].unsqueeze(3).broadcast_to([P, C, NE, NE])
                        V.tensor_tensor(before[:, :, :, :], other, this, ALU.is_gt)
                        V.tensor_tensor(equal[:, :, :, :], other, this, ALU.is_equal)
                        own(V.tensor_reduce(top1[:, :], lg[:, :, :], AX, ALU.max))
                        V.tensor_tensor(lg[:, :, :], lg[:, :, :], top1[:, :].unsqueeze(2).broadcast_to([P, C, NE]),
                                        ALU.subtract).then_inc(s["lg_shift"], 1)
                        own(V.tensor_tensor(equal[:, :, :, :], equal[:, :, :, :],
                                            tri[:, :, :].unsqueeze(1).broadcast_to([P, C, NE, NE]), ALU.mult))
                        own(V.tensor_tensor(before[:, :, :, :], before[:, :, :, :], equal[:, :, :, :], ALU.add))
                        own(V.tensor_reduce(rank[:, :, :], before[:, :, :, :], AX, ALU.add))
                    elif what == "combine":
                        dve.wait_ge(s["lg_exp"], m + 1)
                        own(V.scalar_tensor_tensor(out=rank[:, :, :], in0=rank[:, :, :], scalar=2.0, in1=ex[:, :, :],
                                                   op0=ALU.is_lt, op1=ALU.mult))
                        own(V.tensor_reduce(wsum[:, :], rank[:, :, :], AX, ALU.add))
                        own(V.reciprocal(wrec[:, :], wsum[:, :]))
                        V.tensor_tensor(comb[:, :, :], rank[:, :, :],
                                        wrec[:, :].unsqueeze(2).broadcast_to([P, C, NE]),
                                        ALU.mult).then_inc(s["comb_ready"], 1)
                    elif what == "gate":
                        e, k = divmod(n, 2)
                        dve.wait_ge(s["tanh_ready"], 2 * NE * m + n + 1)
                        if e >= 2 and k == 0:
                            dve.wait_ge(s["y_ps"], NE * m + e - 1)
                        V.scalar_tensor_tensor(out=hid[:, e % 2, k, :], in0=tanh[:, n % 2, :], scalar=1.0,
                                               in1=psHid[:, :], op0=ALU.add, op1=ALU.mult).then_inc(s["hid_ready"], 1)
                    elif what == "sum":
                        if n == 0:
                            dve.wait_ge(s["comb_ready"], m + 1)
                        wait(dve, "prod_used", NE * m + n - 1)
                        dve.wait_ge(s["y_ps"], NE * m + n + 1)
                        V.tensor_tensor(prod[:, n % 2, :, :], psY[:, :].rearrange("p (c d) -> p c d", d=D),
                                        comb[:, :, n:n + 1].broadcast_to([P, C, D]), ALU.mult).then_inc(s["y_used"], 1)
                    elif what == "norm":
                        dve.wait_ge(s["prod_used"], NE * m)
                        for c in range(C):
                            last = V.bn_stats(st3[:, c, :], acc[:, c, :])
                        own(last)
                        dve.sem_inc(s["steps_dve"], 1)
                        for c in range(C):
                            last = V.bn_aggr(mv3[:, c, :], st3[:, c, :])
                        own(last)
                        V.tensor_scalar(ve3[:, :], mv3[:, :, 1], LN_EPS, None, ALU.add).then_inc(s["ve3_ready"], 1)
                    elif what == "result":
                        dve.wait_ge(s["rs3_ready"], m)
                        dve.wait_ge(s["out_done"], 16 * m)
                        for c in range(C):
                            last = V.tensor_scalar(outb[:, c, :], acc[:, c, :], mv3[:, c, 0:1], rs3[:, c:c + 1],
                                                   ALU.subtract, ALU.mult)
                        last.then_inc(s["out_ready"], 1)

            dve.wait_ge(s["w_ps"], 1)
            V.tensor_scalar(wqkv[:, D:3 * D], psS[:, 0, 0:2 * D], g1c[:, :], None, ALU.mult)
            V.tensor_scalar(wqkv[:, 0:D], wqkv[:, 0:D], g1c[:, :], MD ** -0.5, ALU.mult,
                            ALU.mult).then_inc(s["w_ready"], 1)
            dve.wait_ge(s["const"], 1)
            def expert_weights():
                dve.wait_ge(s["ld_e"], 64)
                V.tensor_scalar(w1raw, w1raw, g2c[:, :], None, ALU.mult)
                V.tensor_scalar(wexp2[:, :, :, :], wexp2[:, :, :, :], 0.5, None, ALU.mult)
                V.memset(outb[:, 0, 0:1], 0.0).then_inc(s["out_done"], 16)
                own(V.tensor_scalar(wgate[:, :], wgate[:, :], g2c[:, :], None, ALU.mult))
                own(V.tensor_copy(w1h[:, :, :], w1raw))
                V.tensor_tensor(w1l[:, :, :], w1raw, w1h[:, :, :].bitcast(F32), ALU.subtract).then_inc(s["w_ready"], 1)

            run(dve, trip, own, expert_weights)


OWN_PER_TRIP = 20


PER_TRIP = 0

INPUTS = ["x", "xT", "wqkvT", "woutT", "b_out", "ln_g", "ln_b", "w1gT", "b1g", "w2gT", "b2g"]
INPUTS2 = ["g1", "Wq", "WdkvT", "Wuk", "Wuv", "Wo", "g2", "gate_w", "w1", "w2"]


def program(nc, ins, out):
    with ExitStack() as ctx:
        def sb(name, shape, dt=F32):
            return ctx.enter_context(nc.sbuf_tensor(name, shape, dt))

        keep = {
            "X": sb("X", [P, NC, D]),
            "qpad": sb("qpad", [P, MH, T], F32R),
            "ident": sb("ident", [P, P]),
            "identb": sb("identb", [P, P], BF16),
            "maskb": sb("maskb", [P, P], BF16),
            "tri": sb("tri", [P, NE, NE]),
            "r1": sb("r1", [P, NC]),
            "mhalf": sb("mhalf", [P, NC]),
        }
        gated_attention(nc, keep, *(ins[k] for k in INPUTS))
        causal_attention_and_experts(nc, keep, *(ins[k] for k in INPUTS2), out)


def kernel(**inputs):
    import concourse.bacc as bacc
    from concourse.bass_utils import run_bass_kernel_spmd

    a = {k.split("_", 1)[1]: np.asarray(v) for k, v in inputs.items()}
    tokens = a["attn_x"]
    laid = {
        "x": tokens.reshape(NC, P, D).transpose(1, 0, 2),
        "xT": tokens.reshape(B * T, D).T,
        "wqkvT": a["attn_w_qkv"].T,
        "woutT": a["attn_w_out"].T,
        "b_out": a["attn_b_out"].reshape(1, D),
        "ln_g": a["attn_ln_g"].reshape(DH, 1),
        "ln_b": a["attn_ln_b"].reshape(DH, 1),
        "w1gT": a["attn_w1"].T,
        "b1g": a["attn_b1"].reshape(GH, 1),
        "w2gT": a["attn_w2"].T,
        "b2g": a["attn_b2"].reshape(1, 1).repeat(B, 0),
        "g1": a["ffn_g1"].reshape(D, 1),
        "Wq": a["ffn_Wq"],
        "WdkvT": a["ffn_Wdkv"].T,
        "Wuk": a["ffn_Wuk"],
        "Wuv": a["ffn_Wuv"],
        "Wo": a["ffn_Wo"],
        "g2": a["ffn_g2"].reshape(D, 1),
        "gate_w": a["ffn_gate_w"],
        "w1": a["ffn_w1"],
        "w2": a["ffn_w2"],
    }
    nc = bacc.Bacc("TRN2", target_bir_lowering=False, num_devices=1)
    arrays, ins = {}, {}
    for name, v in laid.items():
        arrays[f"in_{name}"] = v = np.ascontiguousarray(v)
        ins[name] = nc.dram_tensor(f"in_{name}", v.shape, mybir.dt.from_np(v.dtype), kind="ExternalInput").ap()
    out = nc.dram_tensor("out", tokens.shape, F32, kind="ExternalOutput").ap()
    program(nc, ins, out)
    r = run_bass_kernel_spmd(nc, [arrays], core_ids=[0])
    return r.results[0]["out"]
```

```python
from contextlib import ExitStack

import numpy as np

import concourse.bass as bass
from concourse import mybir

ALU = mybir.AluOpType
ACT = mybir.ActivationFunctionType
AX = mybir.AxisListType.X
F32 = mybir.dt.float32
F32R = mybir.dt.float32r
BF16 = mybir.dt.bfloat16
NEG_MAX = float(np.finfo(np.float32).min)
ds = bass.ds

B, T, D = 8, 512, 128
P = 128
C = T // P
NC = B * C
H, DH = 16, 64
INNER = H * DH
NI = INNER // P
TOPK = 32
HB = P // TOPK
NH = B // HB
GH = 16
GR0 = 32
LN_EPS = 1e-5
RMS_EPS = 1e-6
MH, MD = 16, 8
LAT = 64
NG = MH // 4
R = 32
SHIFT = 3 * MD
NE, EH = 8, 256
BIG = -1e30


class Chain:

    def __init__(self, eng, sem):
        self.eng, self.sem, self.n, self.base = eng, sem, 0, 0

    def __call__(self, ins):
        self.n += 1
        ins.then_inc(self.sem, 1)
        self.eng.wait_ge(self.sem, self.base + self.n)


def head_at(k):
    return 2 * (k % (H // 2)) + k // (H // 2)


def gated_attention(nc, keep, x, xT, wqkvT, woutT, b_out, ln_g, ln_b, w1gT, b1g, w2gT, b2g):
    X, ident, mhalf, r1 = keep["X"], keep["ident"], keep["mhalf"], keep["r1"]
    ctx = ExitStack()
    with ctx:
        def sb(name, shape, dt=F32):
            return ctx.enter_context(nc.sbuf_tensor(name, shape, dt))

        def sem(name):
            return ctx.enter_context(nc.semaphore(name))

        XT = sb("XT", [P, B * T])
        WQKV = sb("WQKV", [P, 3 * INNER])
        WOUT = sb("WOUT", [P, NI, D])
        Fc = sb("Fc", [P, 2, T])
        sq = sb("sq", [P, 2, T])
        var = sb("var", [P, NH, T])
        hid = sb("hid", [P, NH, T])
        wsum = sb("wsum", [P, DH])
        wmean = sb("wmean", [P, 2])
        Wc = sb("Wc", [P, DH])
        w1raw = sb("w1raw", [P, 64])
        w1g = sb("w1g", [P, 64])
        gcol = sb("gcol", [P, 1])
        bcol = sb("bcol", [P, 1])
        ones64 = sb("ones64", [P, 64])
        b1col = sb("b1col", [P, 1])
        cbias = sb("cbias", [P, 1])
        w2col = sb("w2col", [P, 1])
        w2sel = sb("w2sel", [P, NH, B])
        b2col = sb("b2col", [B, 1])
        bout = sb("bout", [1, D])
        ones8 = sb("ones8", [1, B])
        selb = sb("selb", [B, B, P])
        selh = sb("selh", [B, NH, P])
        rcol = sb("rcol", [P, 1])
        iota32 = sb("iota32", [P, TOPK])
        scores = sb("scores", [B, T])
        cur = sb("cur", [B, 2, T])
        top8 = sb("top8", [B, 8])
        gv = sb("gv", [B, T])
        ones512 = sb("ones512", [B, T])
        mask = sb("mask", [B, T])
        pos = sb("pos", [B, T])
        slot = sb("slot", [B, T])
        slotT = sb("slotT", [P, B, C])
        gT = sb("gT", [P, B, C])
        GR = sb("GR", [P, NC, 2 * TOPK + 1])
        SR = sb("SR", [P, NH, T])
        Xg = sb("Xg", [P, B * TOPK])
        Xc = sb("Xc", [P, B * TOPK])
        xm = sb("xm", [P, B])
        QK = sb("QK", [P, 2 * NI, B * TOPK])
        V = sb("V", [P, NH, INNER])
        S0 = sb("S0", [P, NH, H, TOPK])
        mx = sb("mx", [P, NH, 6, H])
        BD = sb("BD", [P, H, P])
        BDT = sb("BDT", [P, H, P])
        OT = sb("OT", [P, NI, P])
        vmT = sb("vmT", [P, NI, B])
        base = sb("base", [B, D])
        base_all = sb("base_all", [P, B, D])
        delta = sb("delta", [P, NH, D])
        st6 = sb("st6", [P, C, 6])
        mv = sb("mv", [P, NC, 2])
        rs = sb("rs", [P, NC])
        ve = sb("ve", [P, NC])
        off = sb("off", [P, NC])
        sqr = sb("sqr", [P, NC])
        y = XT[:, :].rearrange("p (i d) -> p i d", d=D)
        bank = [ctx.enter_context(nc.psum_tensor(f"a{i}", [P, 512], F32)) for i in range(8)]

        ld_gate, ld_zero, ld_x, ld_w = sem("ld_gate"), sem("ld_zero"), sem("ld_x"), sem("ld_w")
        ld_xT = [sem(f"ld_xT{j}") for j in range(4)]
        ld_wq = sem("ld_wq")
        zeroed, consts = sem("zeroed"), sem("consts")
        wc_ready, cb_ps = sem("wc_ready"), sem("cb_ps")
        f_ps, f_sb, g_ps, g_used, std_ready, hpre, gelu, sc_ps = (
            sem(n) for n in ("f_ps", "f_sb", "g_ps", "g_used", "std_ready", "hpre", "gelu", "sc_ps"))
        sc_sb, sig, slot_ready, slotT_ps, slotT_sb, sr_ps, sr_sb, gr_ready = (
            sem(n) for n in ("sc_sb", "sig", "slot_ready", "slotT_ps", "slotT_sb", "sr_ps", "sr_sb", "gr_ready"))
        xs_ps, xs_sb, qk_ps, q_sb, k_sb, v_ps, v_sb, vm_ps, vm_sb, base_ps, base_sb = (
            sem(n) for n in ("xs_ps", "xs_sb", "qk_ps", "q_sb", "k_sb", "v_ps", "v_sb", "vm_ps", "vm_sb", "base_ps", "base_sb"))
        s_ps, s_sb, s_shift, s_exp, em, bd_ready, bdT_ps, bdT_sb, o_ps, o_sb, dl_ps, dl_sb = (
            sem(n) for n in ("s_ps", "s_sb", "s_shift", "s_exp", "em", "bd_ready", "bdT_ps", "bdT_sb", "o_ps", "o_sb",
                             "dl_ps", "dl_sb"))
        xb_ready = sem("xb_ready")
        ld_next = sem("ld_next")
        off_ready, x_ready = sem("off_ready"), sem("x_ready")
        at_ps, y_ready, ve_ready, rstd_ready = (sem(n) for n in ("at_ps", "y_ready", "ve_ready", "rstd_ready"))
        ms_ready, r1_ready = sem("ms_ready"), sem("r1_ready")
        dve_own, pool_own, act_own = sem("dve_own"), sem("pool_own"), sem("act_own")

        block = ctx.enter_context(nc.Block())

        @block.sync
        def _(sp):
            sp.dma_start(WQKV[:, 0:INNER], wqkvT[:, 0:INNER]).then_inc(ld_wq, 16)
            sp.dma_start(gcol[0:DH, :], ln_g).then_inc(ld_gate, 16)
            sp.dma_start(gcol[DH:P, :], ln_g).then_inc(ld_gate, 16)
            sp.dma_start(bcol[0:DH, :], ln_b).then_inc(ld_gate, 16)
            sp.dma_start(bcol[DH:P, :], ln_b).then_inc(ld_gate, 16)
            sp.dma_start(b2col[:, :], b2g).then_inc(ld_gate, 16)
            sp.wait_ge(zeroed, 1)
            for k in range(2):
                sp.dma_start(w1raw[DH * k:DH * k + DH, GR0 * k:GR0 * k + GH], w1gT).then_inc(ld_zero, 16)
                for r in range(2):
                    rows = slice(64 * r + GR0 * k, 64 * r + GR0 * k + GH)
                    sp.dma_start(b1col[rows, :], b1g).then_inc(ld_zero, 16)
                    sp.dma_start(w2col[rows, :], w2gT).then_inc(ld_zero, 16)
            for j in range(4):
                sp.dma_start(XT[:, 2 * T * j:2 * T * (j + 1)], xT[:, 2 * T * j:2 * T * (j + 1)]).then_inc(ld_xT[j], 16)
            sp.dma_start(X[:, :, :], x).then_inc(ld_x, 16)
            sp.dma_start(WQKV[:, INNER:3 * INNER], wqkvT[:, INNER:3 * INNER]).then_inc(ld_w, 16)
            sp.dma_start(WOUT[:, :, :], woutT.rearrange("(c p) d -> p c d", p=P)).then_inc(ld_w, 16)
            sp.dma_start(bout[:, :], b_out).then_inc(ld_w, 16)
            for tile, src in keep["loads"]:
                sp.dma_start(tile, src).then_inc(ld_next, 16)
            sp.wait_ge(ld_next, 16 * len(keep["loads"]))

        @block.gpsimd
        def _(pool):
            own = Chain(pool, pool_own)
            own(pool.memset(w1raw[:, :], 0.0))
            own(pool.memset(b1col[:, :], 0.0))
            pool.memset(w2col[:, :], 0.0).then_inc(zeroed, 1)
            pool.wait_ge(zeroed, 1)
            own(pool.memset(ident[:, :], 0.0))
            own(pool.memset(ones64[:, :], 0.0))
            own(pool.memset(w2sel[:, :, :], 0.0))
            own(pool.memset(selb[:, :, :], 0.0))
            own(pool.memset(selh[:, :, :], 1.0))
            own(pool.memset(ones8[:, :], 1.0))
            own(pool.memset(ones512[:, :], 1.0))
            own(pool.memset(mhalf[:, :], -0.5))
            own(pool.memset(keep["tri"][:, :, :], 1.0))
            own(pool.memset(ones64[0:DH, 0:GH], 1.0 / DH))
            own(pool.memset(ones64[DH:P, GR0:GR0 + GH], 1.0 / DH))
            own(pool.affine_select(out=ident[:, :], in_=ident[:, :], compare_op=ALU.not_equal, fill=1.0, base=0,
                               pattern=[[-1, P]], channel_multiplier=1))
            own(pool.affine_select(out=selb[:, :, :], in_=selb[:, :, :], compare_op=ALU.not_equal, fill=1.0, base=0,
                               pattern=[[-1, B], [0, P]], channel_multiplier=1))
            own(pool.affine_select(out=selh[:, :, :], in_=selh[:, :, :], compare_op=ALU.is_ge, fill=0.0, base=0,
                                   pattern=[[1, NH * P]], channel_multiplier=-TOPK))
            own(pool.affine_select(out=selh[:, :, :], in_=selh[:, :, :], compare_op=ALU.is_ge, fill=0.0,
                               base=TOPK - 1, pattern=[[-1, NH * P]], channel_multiplier=TOPK))
            own(pool.iota(iota32[:, :], pattern=[[1, TOPK]], base=0, channel_multiplier=0,
                      allow_small_or_imprecise_dtypes=True))
            for a in range(HB):
                own(pool.iota(rcol[TOPK * a:TOPK * (a + 1), :], pattern=[[0, 1]], base=0, channel_multiplier=1,
                          allow_small_or_imprecise_dtypes=True))
            own(pool.affine_select(out=keep["tri"][:, :, :], in_=keep["tri"][:, :, :], compare_op=ALU.is_gt, fill=0.0,
                               base=0, pattern=[[1, NE], [-1, NE]], channel_multiplier=0))
            pool.memset(BD[:, :, :], 0.0).then_inc(consts, 1)
            pool.wait_ge(consts, 1)
            own(pool.memset(keep["identb"][:, :], 0.0))
            own(pool.memset(keep["maskb"][:, :], 0.0))
            own(pool.memset(keep["qpad"][:, :, :].bitcast(F32), 0.0))
            own(pool.affine_select(out=keep["identb"][:, :], in_=keep["identb"][:, :], compare_op=ALU.not_equal,
                               fill=1.0, base=0, pattern=[[-1, P]], channel_multiplier=1))
            own(pool.affine_select(out=keep["maskb"][:, :], in_=keep["maskb"][:, :], compare_op=ALU.is_ge,
                               fill=BIG, base=0, pattern=[[-1, P]], channel_multiplier=1))
            pool.wait_ge(ld_x, 16)
            pool.wait_ge(base_sb, 2)
            for b in range(B):
                ts = slice(C * b, C * b + C)
                pool.tensor_tensor(y[:, ts, :], X[:, ts, :], base_all[:, b, :].unsqueeze(1).broadcast_to([P, C, D]),
                                   ALU.add).then_inc(xb_ready, 1)
            def mean_square_root(b):
                pool.wait_ge(ms_ready, b + 1)
                cs = slice(C * b, C * b + C)
                pool.tensor_tensor(r1[:, cs], ve[:, cs], mhalf[:, cs], ALU.pow).then_inc(r1_ready, 1)

            for b in range(B):
                cs = slice(C * b, C * b + C)
                pool.wait_ge(ve_ready, b + 1)
                pool.tensor_tensor(rs[:, cs], ve[:, cs], mhalf[:, cs], ALU.pow).then_inc(rstd_ready, 1)
                if b:
                    mean_square_root(b - 1)
            mean_square_root(B - 1)

        @block.tensor
        def _(pe):
            mm = nc.tensor.matmul
            pe.wait_ge(ld_gate, 16 * 5)
            pe.wait_ge(ld_zero, 16 * 10)
            for r in range(2):
                last = mm(bank[7][64 * r:64 * r + 64, 0:1], w1raw[:, :], bcol[:, :], start=True, stop=True)
            last.then_inc(cb_ps, 1)
            pe.wait_ge(wc_ready, 1)
            pe.wait_ge(consts, 1)

            def features(j):
                pe.wait_ge(ld_xT[j], 16)
                if j >= 2:
                    pe.wait_ge(f_sb, 2 * (j - 1))
                for k in range(2):
                    b = 2 * j + k
                    last = mm(bank[j % 2][DH * k:DH * k + DH, :], Wc[:, :], XT[:, T * b:T * b + T],
                              start=True, stop=True)
                last.then_inc(f_ps, 1)

            features(0)
            for j in range(B // 2):
                if j + 1 < B // 2:
                    features(j + 1)
                pe.wait_ge(f_sb, 2 * j + 2)
                i, rows = j // 2, slice(64 * (j % 2), 64 * (j % 2) + 64)
                mm(bank[2 + i][rows, :], w1g[:, :], Fc[:, j % 2, :], start=True, stop=True)
                if j == 2:
                    pe.wait_ge(wc_ready, 2)
                mm(bank[6 + i][rows, :], ones64[:, :], sq[:, j % 2, :], start=True, stop=True).then_inc(g_ps, 1)
            for i in range(NH):
                pe.wait_ge(gelu, i + 1)
                last = mm(bank[0][0:B, :], w2sel[:, i, :], hid[:, i, :], start=(i == 0), stop=(i == NH - 1))
            last.then_inc(sc_ps, 1)

            pe.wait_ge(slot_ready, 1)
            pe.wait_ge(sig, 1)
            for c in range(C):
                nc.tensor.transpose(bank[1][:, B * c:B * c + B], slot[:, P * c:P * c + P], ident[0:B, 0:B])
                last = nc.tensor.transpose(bank[1][:, 64 + B * c:64 + B * c + B], gv[:, P * c:P * c + P],
                                           ident[0:B, 0:B])
            last.then_inc(slotT_ps, 1)
            for n in range(NH):
                last = mm(bank[2 + n][:, :], selh[:, n, :], slot[:, :], start=True, stop=True)
            last.then_inc(sr_ps, 1)

            pe.wait_ge(ld_x, 16)
            pe.wait_ge(gr_ready, 1)
            for b in range(B):
                o = (2 * TOPK + 1) * (b % HB)
                for c in range(C):
                    last = mm(bank[4 + b // HB][:, o:o + 2 * TOPK + 1], X[:, C * b + c, :], GR[:, C * b + c, :],
                              start=(c == 0), stop=(c == C - 1))
            last.then_inc(xs_ps, 1)

            pe.wait_ge(xs_sb, 1)
            pe.wait_ge(ld_w, 48)
            pe.wait_ge(sr_sb, 1)
            for i in range(NI):
                if i >= 4:
                    pe.wait_ge(q_sb, i - 3)
                for k in range(2):
                    n = 2 * i + k
                    last = mm(bank[i % 4][:, 256 * k:256 * k + 256], WQKV[:, P * n:P * n + P], Xg[:, :],
                              start=True, stop=True)
                last.then_inc(qk_ps, 1)
            for n in range(NH):
                for k in range(2):
                    if n == 1:
                        pe.wait_ge(v_sb, k + 1)
                    mm(bank[6 + k][:, :], Xc[:, P * n:P * n + P],
                       WQKV[:, 2 * INNER + 512 * k:2 * INNER + 512 * k + 512], start=True, stop=True).then_inc(v_ps, 1)
            for i in range(NI):
                last = mm(bank[4][:, B * i:B * i + B], WQKV[:, 2 * INNER + P * i:2 * INNER + P * i + P], xm[:, :],
                          start=True, stop=True)
            last.then_inc(vm_ps, 1)
            pe.wait_ge(vm_sb, 1)
            for i in range(NI):
                mm(bank[5][0:B, 0:D], vmT[:, i, :], WOUT[:, i, :], start=(i == 0), stop=False)
            mm(bank[5][0:B, 0:D], ones8[:, :], bout[:, :], start=False, stop=True).then_inc(base_ps, 1)
            pe.wait_ge(base_sb, 1)
            for b in range(B):
                last = mm(bank[4 + b // 4][:, D * (b % 4):D * (b % 4) + D], selb[:, b, :], base[:, :],
                          start=True, stop=True)
            last.then_inc(base_ps, 1)

            pe.wait_ge(q_sb, NI // 2)
            pe.wait_ge(k_sb, NI // 2)
            pe.wait_ge(v_sb, 4)
            pe.wait_ge(base_sb, 2)
            for n in range(NH):
                for q in range(4):
                    for k in range(4):
                        h = head_at(4 * q + k)
                        rows = slice(DH * (h % 2), DH * (h % 2) + DH)
                        last = mm(bank[4 * n + q][:, P * k:P * k + P], QK[rows, h // 2, P * n:P * n + P],
                                  QK[rows, NI + h // 2, P * n:P * n + P], start=True, stop=True)
                last.then_inc(s_ps, 1)
            for n in range(NH):
                pe.wait_ge(bd_ready, n + 1)
                for q in range(4):
                    for k in range(4):
                        last = nc.tensor.transpose(bank[4 * n + q][:, P * k:P * k + P], BD[:, 4 * q + k, :],
                                                   ident[:, :])
                    last.then_inc(bdT_ps, 1)
                pe.wait_ge(bdT_sb, 4 * n + 4)
                for k in range(H):
                    h = head_at(k)
                    i = h // 2
                    rows = slice(DH * (h % 2), DH * (h % 2) + DH)
                    last = mm(bank[4 * n + i // 4][rows, P * (i % 4):P * (i % 4) + P], V[:, n, DH * h:DH * h + DH],
                              BDT[:, k, :], start=True, stop=True)
                last.then_inc(o_ps, 1)
                pe.wait_ge(o_sb, 2 * n + 2)
                for i in range(NI):
                    last = mm(bank[4 * n + 2][:, 0:D], OT[:, i, :], WOUT[:, i, :], start=(i == 0),
                              stop=(i == NI - 1))
                last.then_inc(dl_ps, 1)
            pe.wait_ge(dl_sb, 2)
            for b in range(B):
                n, a = divmod(b, HB)
                rows = slice(TOPK * a, TOPK * a + TOPK)
                if b >= 4:
                    pe.wait_ge(y_ready, b - 3)
                for c in range(C):
                    last = mm(bank[b % 4][:, D * c:D * c + D], SR[rows, n, P * c:P * c + P], delta[rows, n, :],
                              start=True, stop=True, tile_position=(TOPK * a, 0))
                last.then_inc(at_ps, 1)

        @block.scalar
        def _(act):
            A = nc.scalar.activation
            own = Chain(act, act_own)
            for j in range(B // 2):
                act.wait_ge(f_ps, j + 1)
                if j >= 2:
                    act.wait_ge(g_ps, j - 1)
                A(Fc[:, j % 2, :], bank[j % 2][:, :], ACT.Copy).then_inc(f_sb, 1)
                A(sq[:, j % 2, :], bank[j % 2][:, :], ACT.Square).then_inc(f_sb, 1)
            for i in range(NH):
                act.wait_ge(g_used, i + 1)
                A(var[:, i, :], var[:, i, :], ACT.Sqrt).then_inc(std_ready, 1)
            for i in range(NH):
                act.wait_ge(hpre, i + 1)
                A(hid[:, i, :], hid[:, i, :], ACT.Gelu, bias=cbias[:, :]).then_inc(gelu, 1)
            act.wait_ge(sc_sb, 1)
            A(gv[:, :], scores[:, :], ACT.Sigmoid).then_inc(sig, 1)
            act.wait_ge(xs_ps, 1)
            for i in range(NI // 2, NI):
                act.wait_ge(qk_ps, i + 1)
                A(QK[:, 2 * i:2 * i + 2, :], bank[i % 4][:, :].rearrange("p (k t) -> p k t", k=2),
                  ACT.Copy).then_inc(k_sb, 1)
            for n in range(NH):
                for k in range(2):
                    act.wait_ge(v_ps, 2 * n + k + 1)
                    A(V[:, n, 512 * k:512 * k + 512], bank[6 + k][:, :], ACT.Copy).then_inc(v_sb, 1)
            def exponentials(n):
                act.wait_ge(s_shift, 2 * n + 1)
                A(mx[:, n, 1, :], mx[:, n, 0, :], ACT.Exp, scale=-1.0).then_inc(em, 1)
                act.wait_ge(s_shift, 2 * n + 2)
                A(S0[:, n, :, :], S0[:, n, :, :], ACT.Exp).then_inc(s_exp, 1)

            exponentials(0)
            for n in range(NH):
                for q in range(4):
                    act.wait_ge(bdT_ps, 4 * n + q + 1)
                    if n and q == 0:
                        act.wait_ge(o_ps, 1)
                    A(BDT[:, 4 * q:4 * q + 4, :], bank[4 * n + q][:, :].rearrange("p (k t) -> p k t", k=4),
                      ACT.Copy).then_inc(bdT_sb, 1)
                if n == 0:
                    exponentials(1)
                act.wait_ge(o_ps, n + 1)
                if n:
                    act.wait_ge(dl_ps, 1)
                for i in range(2):
                    A(OT[:, 4 * i:4 * i + 4, :], bank[4 * n + i][:, :].rearrange("p (k t) -> p k t", k=4),
                      ACT.Copy).then_inc(o_sb, 1)
            for b in range(B):
                act.wait_ge(off_ready, b + 1)
                for c in range(C):
                    i = C * b + c
                    last = A(X[:, i, :], y[:, i, :], ACT.Identity, scale=rs[:, i:i + 1], bias=off[:, i:i + 1])
                last.then_inc(x_ready, 1)

        @block.vector
        def _(dve):
            V_ = nc.vector
            own = Chain(dve, dve_own)
            dve.wait_ge(ld_wq, 16)
            own(V_.tensor_reduce(wsum[:, :], WQKV[:, 0:INNER].rearrange("p (h e) -> p e h", h=H), AX, ALU.add))
            own(V_.tensor_reduce(wmean[:, 0:1], wsum[:, :], AX, ALU.add))
            own(V_.tensor_scalar(wmean[:, 1:2], wmean[:, 0:1], -1.0 / DH, None, ALU.mult))
            V_.tensor_scalar(Wc[:, :], wsum[:, :], wmean[:, 1:2], 1.0 / H, ALU.add, ALU.mult)
            dve.wait_ge(ld_gate, 16 * 5)
            dve.wait_ge(ld_zero, 16 * 10)
            dve.wait_ge(consts, 1)
            V_.tensor_scalar(w1g[:, :], w1raw[:, :], gcol[:, :], None, ALU.mult)
            for q in range(4):
                rows = slice(32 * q, 32 * q + 32)
                step = B // 2 + B
                last = V_.tensor_copy(w2sel[rows, :, :].rearrange("p i b -> p (i b)")[:, q:q + step + 1:step],
                                      w2col[rows, :].broadcast_to([32, NH]))
            last.then_inc(wc_ready, 1)
            dve.wait_ge(cb_ps, 1)
            V_.tensor_tensor(cbias[:, :], bank[7][:, 0:1], b1col[:, :], ALU.add).then_inc(wc_ready, 1)
            for i in range(NH):
                dve.wait_ge(g_ps, 2 * i + 2)
                V_.tensor_scalar(var[:, i, :], bank[6 + i][:, :], LN_EPS, None, ALU.add).then_inc(g_used, 1)
            for i in range(NH):
                dve.wait_ge(std_ready, i + 1)
                own(V_.reciprocal(var[:, i, :], var[:, i, :]))
                V_.tensor_tensor(hid[:, i, :], bank[2 + i][:, :], var[:, i, :], ALU.mult).then_inc(hpre, 1)
            dve.wait_ge(sc_ps, 1)
            ins = V_.tensor_scalar(scores[:, :], bank[0][0:B, :], b2col[:, :], None, ALU.add)
            ins.then_inc(sc_sb, 1)
            dve.wait_ge(sc_sb, 1)
            src = scores[:, :]
            for i in range(TOPK // 8):
                own(V_.max(top8[:, :], src))
                own(V_.match_replace(cur[:, i % 2, :], top8[:, :], src, NEG_MAX))
                src = cur[:, i % 2, :]
            own(V_.tensor_tensor(mask[:, :], scores[:, :], src, ALU.is_gt))
            own(V_.tensor_tensor_scan(pos[:, :], ones512[:, :], mask[:, :], 0.0, ALU.mult, ALU.add))
            own(V_.tensor_tensor(pos[:, :], pos[:, :], mask[:, :], ALU.mult))
            V_.tensor_scalar(slot[:, :], pos[:, :], -1.0, None, ALU.add).then_inc(slot_ready, 1)
            dve.wait_ge(slotT_ps, 1)
            V_.tensor_copy(slotT[:, :, :], bank[1][:, 0:B * C].rearrange("p (c b) -> p b c", b=B))
            V_.tensor_copy(gT[:, :, :], bank[1][:, 64:64 + B * C].rearrange("p (c b) -> p b c", b=B)
                           ).then_inc(slotT_sb, 1)
            dve.wait_ge(slotT_sb, 1)
            s3 = slotT[:, :, :].rearrange("p b c -> p (b c)").unsqueeze(2).broadcast_to([P, NC, TOPK])
            g3 = gT[:, :, :].rearrange("p b c -> p (b c)").unsqueeze(2).broadcast_to([P, NC, TOPK])
            i3 = iota32[:, :].unsqueeze(1).broadcast_to([P, NC, TOPK])
            own(V_.tensor_tensor(GR[:, :, TOPK:2 * TOPK], s3, i3, ALU.is_equal))
            own(V_.tensor_tensor(GR[:, :, 0:TOPK], GR[:, :, TOPK:2 * TOPK], g3, ALU.mult))
            V_.tensor_scalar(GR[:, :, TOPK:2 * TOPK], GR[:, :, TOPK:2 * TOPK], -1.0 / T, None, ALU.add)
            V_.memset(GR[:, :, 2 * TOPK:], 1.0 / T).then_inc(gr_ready, 1)
            dve.wait_ge(sr_ps, 1)
            for n in range(NH):
                last = V_.tensor_scalar(SR[:, n, :], bank[2 + n][:, :], rcol[:, :], None, ALU.is_equal)
            last.then_inc(sr_sb, 1)
            dve.wait_ge(xs_ps, 1)
            for n in range(NH):
                v = bank[4 + n][:, 0:HB * (2 * TOPK + 1)].rearrange("p (b k) -> p b k", b=HB)
                o = slice(P * n, P * n + P)
                V_.tensor_copy(Xg[:, o].rearrange("p (b k) -> p b k", b=HB), v[:, :, 0:TOPK])
                V_.tensor_copy(Xc[:, o].rearrange("p (b k) -> p b k", b=HB), v[:, :, TOPK:2 * TOPK])
                last = V_.tensor_copy(xm[:, HB * n:HB * n + HB], v[:, :, 2 * TOPK])
            last.then_inc(xs_sb, 1)
            for i in range(NI // 2):
                dve.wait_ge(qk_ps, i + 1)
                V_.tensor_scalar(QK[:, 2 * i:2 * i + 2, :], bank[i % 4][:, :].rearrange("p (k t) -> p k t", k=2),
                                 DH ** -0.5, None, ALU.mult).then_inc(q_sb, 1)
            dve.wait_ge(vm_ps, 1)
            V_.tensor_copy(vmT[:, :, :], bank[4][:, 0:NI * B].rearrange("p (i b) -> p i b", b=B)).then_inc(vm_sb, 1)
            dve.wait_ge(base_ps, 1)
            V_.tensor_copy(base[:, :], bank[5][0:B, 0:D]).then_inc(base_sb, 1)
            dve.wait_ge(base_ps, 2)
            for n in range(2):
                last = V_.tensor_copy(base_all[:, 4 * n:4 * n + 4, :],
                                      bank[4 + n][:, :].rearrange("p (b d) -> p b d", b=4))
            last.then_inc(base_sb, 1)
            for n in range(NH):
                m, e_, s, r, u, _ = (mx[:, n, k, :] for k in range(6))
                dve.wait_ge(s_ps, n + 1)
                for q in range(4):
                    for a in range(HB):
                        rows = slice(TOPK * a, TOPK * a + TOPK)
                        last = V_.tensor_copy(S0[rows, n, 4 * q:4 * q + 4, :],
                                              bank[4 * n + q][rows, :].rearrange("p (k t) -> p k t", k=4)[:, :, rows])
                own(last)
                own(V_.tensor_reduce(m, S0[:, n, :, :], AX, ALU.max))
                V_.tensor_scalar(m, m, 0.0, None, ALU.max).then_inc(s_shift, 1)
                dve.wait_ge(s_shift, 2 * n + 1)
                V_.tensor_tensor(S0[:, n, :, :], S0[:, n, :, :], m.unsqueeze(2).broadcast_to([P, H, TOPK]),
                                 ALU.subtract).then_inc(s_shift, 1)
                dve.wait_ge(em, n + 1)
                dve.wait_ge(s_exp, n + 1)
                own(V_.tensor_reduce(s, S0[:, n, :, :], AX, ALU.add))
                own(V_.scalar_tensor_tensor(out=s, in0=e_, scalar=float(T - TOPK), in1=s, op0=ALU.mult, op1=ALU.add))
                own(V_.reciprocal(r, s))
                V_.tensor_tensor(u, e_, r, ALU.mult)
                own(V_.tensor_tensor(S0[:, n, :, :], S0[:, n, :, :], r.unsqueeze(2).broadcast_to([P, H, TOPK]),
                                     ALU.mult))
                if n:
                    dve.wait_ge(bdT_ps, 4)
                for a in range(HB):
                    rows = slice(TOPK * a, TOPK * a + TOPK)
                    last = V_.tensor_tensor(BD[rows, :, rows], S0[rows, n, :, :],
                                            u[rows].unsqueeze(2).broadcast_to([TOPK, H, TOPK]), ALU.subtract)
                last.then_inc(bd_ready, 1)
            for n in range(NH):
                dve.wait_ge(dl_ps, n + 1)
                V_.tensor_copy(delta[:, n, :], bank[4 * n + 2][:, 0:D]).then_inc(dl_sb, 1)

            def offset(b):
                dve.wait_ge(rstd_ready, b + 1)
                cs = slice(C * b, C * b + C)
                V_.scalar_tensor_tensor(out=off[:, cs], in0=mv[:, cs, 0], scalar=-1.0, in1=rs[:, cs],
                                        op0=ALU.mult, op1=ALU.mult).then_inc(off_ready, 1)
                own(V_.tensor_tensor(sqr[:, cs], rs[:, cs], rs[:, cs], ALU.mult))
                own(V_.tensor_tensor(sqr[:, cs], sqr[:, cs], mv[:, cs, 1], ALU.mult))
                V_.tensor_scalar(ve[:, cs], sqr[:, cs], RMS_EPS, None, ALU.add).then_inc(ms_ready, 1)

            for b in range(B):
                dve.wait_ge(at_ps, b + 1)
                dve.wait_ge(xb_ready, b + 1)
                V_.tensor_tensor(y[:, C * b:C * b + C, :], y[:, C * b:C * b + C, :],
                                 bank[b % 4][:, :].rearrange("p (c d) -> p c d", c=C), ALU.add).then_inc(y_ready, 1)
                dve.wait_ge(y_ready, b + 1)
                for c in range(C):
                    last = V_.bn_stats(st6[:, c, :], y[:, C * b + c, :])
                own(last)
                for c in range(C):
                    last = V_.bn_aggr(mv[:, C * b + c, :], st6[:, c, :])
                own(last)
                V_.tensor_scalar(ve[:, C * b:C * b + C], mv[:, C * b:C * b + C, 1], LN_EPS, None,
                                 ALU.add).then_inc(ve_ready, 1)
                if b:
                    offset(b - 1)
            offset(B - 1)
            dve.wait_ge(r1_ready, B)


SCORE_STEPS, WEIGHT_STEPS = 12, 12
SCORES = ([(c, h, 2) for c in (0, 1) for h in (0, 2)] + [(c, h, 1) for c in (2, 3) for h in range(4)])
WEIGHTS = ([(c, h, 1) for c in (0, 1) for h in range(4)] + [(c, h, 2) for c in (2, 3) for h in (0, 2)])
WEIGHED = [4, 8, 10, 12]
ADD_LAG = 4
UNIT_SLOTS = [17, 19, 21, 22, 23, 25, 26, 27, 29, 30, 31, 33, 33, 35, 37, 38, 40, 41, 42, 43, 45, 46, 46, 47]
SPARE = ("turn", "attnT", "project", "tokensT", "logits", "shiftT", "keys", "queries", "nextT", "qkv")


def order_of_trip(alone=False):
    steps = []
    at = {
        0: [("here", "shift", 1), ("here", "keys", 3)],
        2: [("here", "queries", 3), ("here", "place", 3)],
        3: [("here", "shiftT", 1), ("end", "add", NE - 1), ("end", "norm", 0)],
        4: [("rest", "turn", 0), ("rest", "turn", 1)],
        6: [("ahead", "next", 0), ("rest", "turn", 2)],
        7: [("rest", "turn", 3), ("end", "norm root", 0)],
        8: [("ahead", "nextT", 0)],
        9: [("rest", "attnT", 0), ("first", "prepare", 0)],
        10: [("end", "result", 0), ("ahead", "qkv", 0), ("ahead", "parts", 0)],
        11: [("rest", "project", 0)],
        12: [("rest", "statistics", 0), ("rest", "moments", 0), ("ahead", "qkv", 1), ("ahead", "parts", 1)],
        13: [("here", "shift", 2), ("ahead", "qkv", 2), ("rest", "root", 0), ("ahead", "parts", 2)],
        14: [("rest", "scale", 0), ("here", "shiftT", 2)],
        15: [("rest", "tokensT", 0), ("rest", "residuals", 0)],
        16: [("rest", "split", 0)],
        17: [("ahead", "qkv", 3), ("ahead", "parts", 3), ("ahead", "values", 0)],
        18: [("first", "prepare", 1), ("rest", "logits", 0)],
        19: [("rest", "rank", 0), ("ahead", "keys", 4), ("rest", "compare", 0)],
        20: [("ahead", "queries", 4), ("ahead", "place", 4)],
        21: [("rest", "count", 0), ("rest", "combine", 0)],
        24: [("here", "shift", 3)],
        25: [("ahead", "keys", 5), ("first", "prepare", 2)],
        26: [("ahead", "queries", 5), ("ahead", "place", 5)],
        28: [("here", "shiftT", 3)],
        29: [("ahead", "values", 1)],
        36: [("ahead", "shift", 4)],
        37: [("ahead", "keys", 6)],
        38: [("ahead", "queries", 6), ("ahead", "place", 6), ("first", "prepare", 3)],
        41: [("ahead", "shiftT", 4)],
        42: [("ahead", "values", 2)],
    }
    units = []
    for e in range(NE):
        upto = min(2 * NE, 2 * e + (4 if alone or e == NE - 2 else 3))
        units += [("hidden", k) for k in range(sum(u[0] == "hidden" for u in units), upto)] + [("down", e)]
    lagging = []

    def unit():
        if units:
            what = units.pop(0)
            steps.append(("rest",) + what)
            lagging.append([what, 0])
        for item in list(lagging):
            item[1] += 1
            if item[1] == 2:
                steps.append(("rest", {"hidden": "gate", "down": "sum"}[item[0][0]], item[0][1]))
                if item[0][0] == "hidden":
                    lagging.remove(item)
            elif item[1] == ADD_LAG:
                if item[0][1] < NE - 1:
                    steps.append(("rest", "add", item[0][1]))
                lagging.remove(item)

    for slot in range(NG * WEIGHT_STEPS):
        n = slot + 2 * SCORE_STEPS
        steps.append(("here", "weight", slot))
        part = "here" if n < NG * SCORE_STEPS else "ahead"
        steps.append((part, "score", n))
        if slot % SCORE_STEPS == 0 and slot:
            before = "here" if n - 1 < NG * SCORE_STEPS else "ahead"
            steps.append((before, "maximum", n - 1))
        elif slot % SCORE_STEPS:
            steps.append((part, "maximum", n - 1))
        g, k = divmod(slot, WEIGHT_STEPS)
        for c in range(C):
            if (k - 1) % WEIGHT_STEPS == WEIGHED[c] % WEIGHT_STEPS and slot > 1:
                done = C * g + c - (C if k == 1 else 0)
                steps.append(("here", "value", done))
                if done % C == C - 1:
                    steps.append(("here", "heads", done // C))
        for item in [item for item in lagging if item[0][0] == "hidden"]:
            steps.append(("rest", "gate", item[0][1]))
            lagging.remove(item)
        steps += at.get(slot, [])
        for _ in range(UNIT_SLOTS.count(slot)):
            unit()
    steps.append(("ahead", "maximum", 6 * SCORE_STEPS - 1))
    unit()
    steps += [("here", "value", NG * C - 1), ("here", "heads", NG - 1), ("ahead", "values", 3)]
    while units or lagging:
        unit()
    return steps


def causal_attention_and_experts(nc, keep, g2, gate_w, w1, w2, out):
    X, ident, identb, maskb = keep["X"], keep["ident"], keep["identb"], keep["maskb"]
    qpad, r1, mhalf, tri = keep["qpad"], keep["r1"], keep["mhalf"], keep["tri"]
    wqkv, wo, wd, wu, g1c = (keep[n] for n in ("wqkv", "wo", "wd", "wu", "g1c"))
    ctx = ExitStack()
    with ctx:
        def sb(name, shape, dt=F32):
            return ctx.enter_context(nc.sbuf_tensor(name, shape, dt))

        def sem(name):
            return ctx.enter_context(nc.semaphore(name))

        w1h = sb("w1h", [P, NE, EH], F32R)
        w1l = sb("w1l", [P, NE, EH], F32R)
        wexp2 = sb("wexp2", [P, NE, 2, D])
        wgate = sb("wgate", [P, NE])
        g2c = sb("g2c", [P, 1])
        xr = sb("xr", [P, C, D])
        xrT = sb("xrT", [P, T])
        qs = sb("qs", [P, C, MH, R], F32R)
        ks = sb("ks", [P, C, MH, R], F32R)
        qT = sb("qT", [P, NG, T], F32R)
        kT = sb("kT", [P, NG, T], F32R)
        va = sb("va", [P, C, MH, R])
        negmax = sb("negmax", [P, 2, C, 4])
        shift = sb("shift", [P, C, 4, 2], F32R)
        shiftT = sb("shiftT", [4 * 2, 2, T], F32R)
        prob = sb("prob", [P, 2, 4, T])
        oT = sb("oT", [P, NG, T])
        rden = sb("rden", [P, C, MH])
        attn = sb("attn", [P, C, D])
        attnT = sb("attnT", [P, T])
        x2 = sb("x2", [P, C, D])
        prod = sb("prod", [P, 2, C, D])
        t = sb("t", [P, C, D])
        tT = sb("tT", [P, T])
        st2, mv2, ms2, r2 = sb("st2", [P, C, 6]), sb("mv2", [P, C, 2]), sb("ms2", [P, C]), sb("r2", [P, C])
        st3, mv3, ve3, rs3 = sb("st3", [P, C, 6]), sb("mv3", [P, C, 2]), sb("ve3", [P, C]), sb("rs3", [P, C])
        lg, lgx, ex = sb("lg", [P, C, NE]), sb("lgx", [P, C, NE]), sb("ex", [P, C, NE])
        before, equal = sb("before", [P, C, NE, NE]), sb("equal", [P, C, NE, NE])
        rank, top1 = sb("rank", [P, C, NE]), sb("top1", [P, C])
        wsum, wrec = sb("wsum2", [P, C]), sb("wrec", [P, C])
        comb = sb("comb", [P, C, NE])
        hid = sb("hid2", [P, 2, 2, T])
        tanh = sb("tanh", [P, 2, T])
        vstage = sb("vstage", [P, C, D])
        tTh, tTl = sb("tTh", [P, T], F32R), sb("tTl", [P, T], F32R)
        acc = sb("acc", [P, C, D])
        outb = sb("outb", [P, C, D])
        w1raw = hid[:, :, :, :].rearrange("p a k t -> p (a k t)").rearrange("p (e h) -> p e h", e=NE)
        psS = ctx.enter_context(nc.psum_tensor("psS", [P, 2, 512], F32))
        psW = ctx.enter_context(nc.psum_tensor("psW", [P, 2, 512], F32))
        psV = ctx.enter_context(nc.psum_tensor("psV", [P, 512], F32))
        psHid = ctx.enter_context(nc.psum_tensor("psHid", [P, 512], F32))
        psY = ctx.enter_context(nc.psum_tensor("psY", [P, 512], F32))
        spare = ctx.enter_context(nc.psum_tensor("spare", [P, 512], F32))

        names = """ld_e const w_ps w_ready xr_ready spare_full spare_read v_placed qpad_in s_ps max_ready
            shift_ready shift_in st_ps exp_ready masked pv_done oT_sb high_ready prod_used both_ready ms2_ready
            r2_ready t_ready tT_split lg_shift lg_exp comb_ready hid_ps tanh_ready hid_ready y_ps y_used ve3_ready rs3_ready
            out_ready out_done own_pool own_dve steps_dve steps_pool""".split()
        s = {n: sem(n) for n in names}
        full = order_of_trip()
        kinds = [[step[1:] for step in full if step[0] in parts] for parts in
                 (("ahead",), ("here", "ahead", "first"), ("here", "rest", "ahead"), ("here", "rest", "end", "ahead"),
                  ("here", "rest", "end"), ("rest", "end"), ("end",))]
        kinds[5] = [step[1:] for step in order_of_trip(alone=True) if step[0] in ("rest", "end")]
        uses = [sum(step[0] in SPARE for step in steps) for steps in kinds]

        def run(eng, trip, chain=None, meanwhile=None):
            used = 0
            for b in range(-1, 2):
                if b == 0 and meanwhile:
                    meanwhile()
                trip(kinds[b + 1], b, used)
                used += uses[b + 1]
            if chain:
                before, chain.n = chain.base + chain.n, 0
            with eng.Fori(2, B - 1) as b:
                if chain:
                    chain.base = before + (b - 2) * OWN_PER_TRIP
                trip(kinds[3], b, used + (b - 2) * uses[3])
            used += (B - 3) * uses[3]
            if chain:
                assert chain.n == OWN_PER_TRIP, chain.n
                chain.base, chain.n = before + (B - 3) * OWN_PER_TRIP, 0
            for b in range(B - 1, B + 2):
                trip(kinds[b - B + 5], b, used)
                used += uses[b - B + 5]

        def counter(steps, used):
            place = {step: used + i + 1 for i, step in enumerate(t for t in steps if t[0] in SPARE)}
            return lambda what, n=0: place[what, n]

        def projection_bank(steps, n):
            return spare if ("weight", 0) in steps else (spare, psV, psHid, psY)[n]

        def hidden_bank(steps, n):
            return (psHid[:, :], 1) if ("weight", 0) in steps else (
                (psHid[:, :], psW[:, 0, :], psW[:, 1, :], psS[:, 0, :])[n % 4], 4)

        def wait(eng, name, count):
            if not isinstance(count, int) or count > 0:
                eng.wait_ge(s[name], count)

        out_v = out.rearrange("b (c p) d -> p (b c) d", p=P)
        block = ctx.enter_context(nc.Block())

        @block.sync
        def _(sp):
            def expert_weights():
                sp.dma_start(g2c[:, :], g2).then_inc(s["ld_e"], 16)
                sp.dma_start(wgate[:, :], gate_w).then_inc(s["ld_e"], 16)
                sp.dma_start(w1raw, w1.rearrange("e d h -> d e h")).then_inc(s["ld_e"], 16)
                sp.dma_start(wexp2[:, :, :, :], w2.rearrange("e (k p) d -> p e k d", p=P)).then_inc(s["ld_e"], 16)

            def trip(steps, b, used):
                use = counter(steps, used)
                for what, n in steps:
                    if what == "place":
                        sp.wait_ge(s["spare_read"], use("queries", n))
                        wait(sp, "st_ps", WEIGHT_STEPS * (NG * b + n - 3))
                        for a in range(4):
                            rows = slice(R * a, R * a + R)
                            sp.dma_start(qpad[rows, 4 * (n % NG) + a, :].bitcast(F32),
                                         qT[rows, n % NG, :].bitcast(F32)).then_inc(s["qpad_in"], 16)
                    elif what == "shiftT":
                        sp.wait_ge(s["spare_read"], use("shiftT", n))
                        wait(sp, "s_ps", SCORE_STEPS * (NG * b + n + 1))
                        for a in range(4):
                            row = R * a + SHIFT
                            sp.dma_start(qpad[row:row + 2, 4 * (n % NG) + a, :].bitcast(F32),
                                         shiftT[2 * a:2 * a + 2, n % 2, :].bitcast(F32)).then_inc(s["shift_in"], 16)
                    elif what == "result":
                        sp.wait_ge(s["out_ready"], b - 1)
                        sp.dma_start(out_v[:, ds(C * (b - 2), C), :], outb[:, :, :]).then_inc(s["out_done"], 16)

            run(sp, trip, meanwhile=expert_weights)
            sp.wait_ge(s["out_done"], 16 * B + 16)

        @block.gpsimd
        def _(pool):
            own = Chain(pool, s["own_pool"])
            own(pool.memset(va[:, :, :, :], 0.0))
            own(pool.memset(va[:, :, :, MD:MD + 1], 1.0))

            def trip(steps, b, used):
                use = counter(steps, used)
                m = b - 1
                for what, n in steps:
                    if what == "values":
                        pool.wait_ge(s["spare_read"], use("qkv", C - 1))
                        wait(pool, "pv_done", NG * C * b + C * n + C)
                        if not isinstance(b, int):
                            pool.sem_inc(s["steps_pool"], 1)
                        for c in range(C):
                            last = pool.tensor_copy(va[:, c, 4 * n:4 * n + 4, 0:MD],
                                                    vstage[:, c, 4 * MD * n:4 * MD * n + 4 * MD].rearrange(
                                                        "p (h m) -> p h m", m=MD))
                        last.then_inc(s["v_placed"], 1)
                    elif what == "root":
                        pool.wait_ge(s["ms2_ready"], m + 1)
                        pool.tensor_tensor(r2[:, :], ms2[:, :], mhalf[:, 0:C], ALU.pow).then_inc(s["r2_ready"], 1)
                    elif what == "residuals":
                        pool.wait_ge(s["spare_read"], use("project"))
                        wait(pool, "out_ready", m)
                        pool.tensor_tensor(acc[:, :, :], X[:, ds(C * m, C), :], x2[:, :, :],
                                           ALU.add).then_inc(s["both_ready"], 1)
                    elif what == "value":
                        g, kc = divmod(n, C)
                        pool.wait_ge(s["exp_ready"], WEIGHT_STEPS * (NG * b + g) + WEIGHED[kc])
                        if not isinstance(b, int):
                            pool.sem_inc(s["steps_pool"], 1)
                        blk = prob[:, n % 2, :, P * kc:P * kc + P]
                        pool.affine_select(out=blk, in_=blk, compare_op=ALU.is_ge, fill=0.0, base=0,
                                           pattern=[[0, 4], [1, P]], channel_multiplier=-1).then_inc(s["masked"], 1)
                    elif what == "add":
                        of = m if n < NE - 1 else m - 1
                        if n == 0:
                            pool.wait_ge(s["both_ready"], of + 1)
                        else:
                            pool.wait_ge(s["prod_used"], NE * of + n)
                        pool.wait_ge(s["y_used"], NE * of + n + 1)
                        pool.tensor_tensor(acc[:, :, :], acc[:, :, :], prod[:, n % 2, :, :],
                                           ALU.add).then_inc(s["prod_used"], 1)
                    elif what == "norm root":
                        pool.wait_ge(s["ve3_ready"], m)
                        pool.tensor_tensor(rs3[:, :], ve3[:, :], mhalf[:, 0:C], ALU.pow).then_inc(s["rs3_ready"], 1)

            run(pool, trip)

        @block.tensor
        def _(pe):
            mm, tr = nc.tensor.matmul, nc.tensor.transpose
            mm(psS[:, 0, 0:2 * D], wd[:, :], wu[:, :, :], start=True, stop=True).then_inc(s["w_ps"], 1)
            pe.wait_ge(s["w_ready"], 1)

            def trip(steps, b, used):
                use = counter(steps, used)
                m = b - 1
                for what, n in steps:
                    if what == "qkv" and ("weight", 0) not in steps:
                        wait(pe, "spare_read", use("nextT"))
                    elif what in SPARE:
                        wait(pe, "spare_read", use(what, n) - 1)
                    if what == "nextT":
                        pe.wait_ge(s["xr_ready"], b + 2)
                        for c in range(C):
                            last = tr(spare[:, P * c:P * c + P], xr[:, c, :], ident[:, :])
                        last.then_inc(s["spare_full"], 1)
                    elif what == "qkv":
                        mm(projection_bank(steps, n)[:, 0:3 * D], xrT[:, P * n:P * n + P], wqkv[:, :], start=True,
                           stop=True).then_inc(s["spare_full"], 1)
                    elif what in ("keys", "queries"):
                        stack = ks if what == "keys" else qs
                        h = 4 * (n % NG)
                        for c in range(C):
                            last = tr(spare[:, P * c:P * c + P],
                                      stack[:, c, h:h + 4, :].rearrange("p h r -> p (h r)").bitcast(F32), ident[:, :])
                        last.then_inc(s["spare_full"], 1)
                    elif what == "turn":
                        if n == 0:
                            pe.wait_ge(s["oT_sb"], NG * m + NG)
                        for g in range(NG):
                            last = tr(spare[:, P * g:P * g + P], oT[:, g, P * n:P * n + P], ident[:, :])
                        last.then_inc(s["spare_full"], 1)
                    elif what == "attnT":
                        for c in range(C):
                            last = tr(spare[:, P * c:P * c + P], attn[:, c, :], ident[:, :])
                        last.then_inc(s["spare_full"], 1)
                    elif what == "project":
                        for c in range(C):
                            last = mm(spare[:, D * c:D * c + D], attnT[:, P * c:P * c + P], wo[:, :], start=True,
                                      stop=True)
                        last.then_inc(s["spare_full"], 1)
                    elif what == "tokensT":
                        pe.wait_ge(s["t_ready"], m + 1)
                        for c in range(C):
                            last = tr(spare[:, P * c:P * c + P], t[:, c, :], ident[:, :])
                        last.then_inc(s["spare_full"], 1)
                    elif what == "logits":
                        if isinstance(b, int) and b == 1:
                            pe.wait_ge(s["w_ready"], 2)
                        for c in range(C):
                            last = mm(spare[:, NE * c:NE * c + NE], tT[:, P * c:P * c + P], wgate[:, :], start=True,
                                      stop=True)
                        last.then_inc(s["spare_full"], 1)
                    elif what == "hidden":
                        e, k = divmod(n, 2)
                        dst, back = hidden_bank(steps, n)
                        if n == 0:
                            pe.wait_ge(s["tT_split"], m + 1)
                        else:
                            wait(pe, "hid_ready", 2 * NE * m + n + 1 - back)
                        for i, (w, v) in enumerate(((w1h, tTh), (w1h, tTl), (w1l, tTh))):
                            last = mm(dst, w[:, e, P * k:P * k + P], v[:, :], start=(i == 0), stop=(i == 2))
                        last.then_inc(s["hid_ps"], 1)
                    elif what == "down":
                        pe.wait_ge(s["hid_ready"], 2 * NE * m + 2 * n + 2)
                        if n:
                            pe.wait_ge(s["y_used"], NE * m + n)
                        for c in range(C):
                            for k in range(2):
                                last = mm(psY[:, D * c:D * c + D], hid[:, n % 2, k, P * c:P * c + P],
                                          wexp2[:, n, k, :], start=(k == 0), stop=(k == 1))
                        last.then_inc(s["y_ps"], 1)
                    elif what == "score":
                        u, i = divmod(n, SCORE_STEPS)
                        g = u % NG
                        c, first, heads = SCORES[i]
                        if i == 0:
                            pe.wait_ge(s["qpad_in"], 64 * (NG * b + u + 1))
                        wait(pe, "max_ready", NG * SCORE_STEPS * b + n - 1)
                        for j in range(heads):
                            dst = psS[:, n % 2, 256 * j:512]
                            keys = max(P * (c + 1), 256)
                            mm(dst[:, 0:keys], qpad[:, 4 * g + first + j, P * c:P * c + P], kT[:, g, 0:keys],
                               start=True, stop=False)
                            last = mm(dst[:, P * c:P * c + P], identb[:, :], maskb[:, :], start=False, stop=True)
                        last.then_inc(s["s_ps"], 1)
                    elif what == "shiftT":
                        pe.wait_ge(s["shift_ready"], NG * b + n + 1)
                        for c in range(C):
                            last = tr(spare[0:8, P * c:P * c + P],
                                      shift[:, c, :, :].rearrange("p a j -> p (a j)").bitcast(F32), ident[:, :])
                        last.then_inc(s["spare_full"], 1)
                    elif what == "weight":
                        g, i = divmod(n, WEIGHT_STEPS)
                        kc, first, heads = WEIGHTS[i]
                        if i == 0:
                            pe.wait_ge(s["shift_in"], 64 * (NG * b + g + 1))
                        wait(pe, "exp_ready", NG * WEIGHT_STEPS * b + n - 1)
                        q0 = min(P * kc, 256)
                        for j in range(heads):
                            last = mm(psW[:, n % 2, 256 * j:256 * j + T - q0], kT[:, g, P * kc:P * kc + P],
                                      qpad[:, 4 * g + first + j, q0:T], start=True, stop=True)
                        last.then_inc(s["st_ps"], 1)
                    elif what == "value":
                        g, kc = divmod(n, C)
                        pe.wait_ge(s["masked"], NG * C * b + n + 1)
                        if kc == 0:
                            pe.wait_ge(s["v_placed"], NG * b + g + 1)
                            wait(pe, "oT_sb", NG * b + g)
                        for a in range(4):
                            last = mm(psV[R * a:R * a + R, P * kc:T], va[:, kc, 4 * g + a, :],
                                      prob[:, n % 2, a, P * kc:T], start=(kc == 0), stop=(kc == C - 1),
                                      tile_position=(0, R * a))
                        last.then_inc(s["pv_done"], 1)

            run(pe, trip)

        @block.scalar
        def _(act):
            A = nc.scalar.activation

            def trip(steps, b, used):
                use = counter(steps, used)
                m = b - 1
                for what, n in steps:
                    if what in ("nextT", "attnT", "tokensT", "keys", "queries", "shiftT"):
                        act.wait_ge(s["spare_full"], use(what, n))
                    if what == "nextT":
                        A(xrT[:, :], spare[:, :], ACT.Copy).then_inc(s["spare_read"], 1)
                    elif what == "parts":
                        act.wait_ge(s["spare_full"], use("qkv", n))
                        if isinstance(b, int) and b < 0 and n == 0:
                            act.wait_ge(s["const"], 1)
                        src = projection_bank(steps, n)
                        q, k = (src[:, D * i:D * i + D].rearrange("p (h m) -> p h m", m=MD).unsqueeze(
                            2).broadcast_to([P, MH, 2, MD]) for i in range(2))
                        A(qs[:, n, :, 0:2 * MD].rearrange("p h (j m) -> p h j m", j=2), q, ACT.Copy)
                        A(ks[:, n, :, :].rearrange("p h (j m) -> p h j m", j=2)[:, :, :, 0:MD], k, ACT.Copy)
                        if n == 0:
                            wait(act, "v_placed", NG * (b + 1))
                        A(vstage[:, n, :], src[:, 2 * D:3 * D], ACT.Copy).then_inc(s["high_ready"], 1)
                    elif what == "attnT":
                        A(attnT[:, :], spare[:, :], ACT.Copy).then_inc(s["spare_read"], 1)
                    elif what == "keys":
                        wait(act, "st_ps", WEIGHT_STEPS * (NG * b + n - 3))
                        A(kT[:, n % NG, :], spare[:, :], ACT.Copy).then_inc(s["spare_read"], 1)
                    elif what == "queries":
                        wait(act, "qpad_in", 64 * (NG * b + n - 3))
                        A(qT[:, n % NG, :], spare[:, :], ACT.Copy).then_inc(s["spare_read"], 1)
                    elif what == "shiftT":
                        wait(act, "shift_in", 64 * (NG * b + n - 1))
                        A(shiftT[:, n % 2, :], spare[0:8, :], ACT.Copy).then_inc(s["spare_read"], 1)
                    elif what == "tokensT":
                        A(tTh[:, :], spare[:, :], ACT.Copy)
                        A(tT[:, :], spare[:, :], ACT.Copy).then_inc(s["spare_read"], 1)
                    elif what == "combine":
                        act.wait_ge(s["lg_shift"], m + 1)
                        A(ex[:, :, :], lgx[:, :, :], ACT.Exp).then_inc(s["lg_exp"], 1)
                    elif what == "hidden":
                        wait(act, "hid_ready", 2 * NE * m + n - 1)
                        act.wait_ge(s["hid_ps"], 2 * NE * m + n + 1)
                        A(tanh[:, n % 2, :], hidden_bank(steps, n)[0], ACT.Tanh, scale=0.5).then_inc(s["tanh_ready"], 1)
                    elif what == "heads":
                        act.wait_ge(s["pv_done"], NG * C * b + C * n + C)
                        if n == 0 and ("turn", 0) in steps:
                            act.wait_ge(s["spare_full"], use("turn", C - 1))
                        A(oT[:, n, :], psV[:, :], ACT.Copy).then_inc(s["oT_sb"], 1)
                    elif what == "weight":
                        g, i = divmod(n, WEIGHT_STEPS)
                        kc, first, heads = WEIGHTS[i]
                        if first == 0:
                            wait(act, "pv_done", NG * C * b + C * g + kc - 1)
                        act.wait_ge(s["st_ps"], NG * WEIGHT_STEPS * b + n + 1)
                        skip = P * kc - min(P * kc, 256)
                        width = T - P * kc
                        src = psW[:, n % 2, :].rearrange("p (j t) -> p j t", j=heads)[:, :, skip:skip + width]
                        A(prob[:, kc % 2, first:first + heads, P * kc:T], src, ACT.Exp).then_inc(s["exp_ready"], 1)

            run(act, trip)

        @block.vector
        def _(dve):
            V = nc.vector
            own = Chain(dve, s["own_dve"])

            def trip(steps, b, used):
                use = counter(steps, used)
                m = b - 1
                for what, n in steps:
                    if what == "next":
                        for c in range(C):
                            last = V.tensor_scalar(xr[:, c, :], X[:, ds(C * (b + 1) + c, 1), :],
                                                   r1[:, ds(C * (b + 1) + c, 1)], None, ALU.mult)
                        last.then_inc(s["xr_ready"], 1)
                    elif what == "parts":
                        dve.wait_ge(s["high_ready"], C * (b + 1) + n + 1)
                        src = projection_bank(steps, n)
                        q, k = (src[:, D * i:D * i + D].rearrange("p (h m) -> p h m", m=MD) for i in range(2))
                        V.tensor_tensor(qs[:, n, :, 2 * MD:3 * MD], q, qs[:, n, :, 0:MD].bitcast(F32), ALU.subtract)
                        V.tensor_tensor(ks[:, n, :, MD:2 * MD], k, ks[:, n, :, 0:MD].bitcast(F32),
                                        ALU.subtract).then_inc(s["spare_read"], 1)
                    elif what == "prepare":
                        if n == 0:
                            dve.wait_ge(s["ld_e"], 64)
                            V.tensor_scalar(wgate[:, :], wgate[:, :], g2c[:, :], None, ALU.mult)
                            own(V.tensor_scalar(w1raw, w1raw, g2c[:, :], None, ALU.mult))
                        elif n == 1:
                            V.tensor_scalar(wexp2[:, :, :, :], wexp2[:, :, :, :], 0.5, None, ALU.mult)
                        elif n == 2:
                            own(V.tensor_copy(w1h[:, :, :], w1raw))
                        else:
                            V.tensor_tensor(w1l[:, :, :], w1raw, w1h[:, :, :].bitcast(F32),
                                            ALU.subtract).then_inc(s["w_ready"], 1)
                    elif what == "maximum":
                        u, i = divmod(n, SCORE_STEPS)
                        c, first, heads = SCORES[i]
                        dve.wait_ge(s["s_ps"], NG * SCORE_STEPS * b + n + 1)
                        src = psS[:, n % 2, :].rearrange("p (j t) -> p j t", j=heads)[:, :, 0:P * (c + 1)]
                        V.tensor_reduce(negmax[:, u % 2, c, first:first + heads], src, AX, ALU.max,
                                        negate=True).then_inc(s["max_ready"], 1)
                    elif what == "shift":
                        dve.wait_ge(s["max_ready"], SCORE_STEPS * (NG * b + n + 1))
                        own(V.tensor_copy(shift[:, :, :, 0], negmax[:, n % 2, :, :]))
                        V.tensor_tensor(shift[:, :, :, 1], negmax[:, n % 2, :, :], shift[:, :, :, 0].bitcast(F32),
                                        ALU.subtract).then_inc(s["shift_ready"], 1)
                    elif what == "turn":
                        dve.wait_ge(s["spare_full"], use("turn", n))
                        src = spare[:, :].rearrange("p (h r) -> p h r", r=R)
                        own(V.reciprocal(rden[:, n, :], src[:, :, MD]))
                        V.tensor_tensor(attn[:, n, :].rearrange("p (h m) -> p h m", m=MD), src[:, :, 0:MD],
                                        rden[:, n, :].unsqueeze(2).broadcast_to([P, MH, MD]),
                                        ALU.mult).then_inc(s["spare_read"], 1)
                    elif what == "statistics":
                        dve.wait_ge(s["spare_full"], use("project"))
                        V.tensor_tensor(x2[:, :, :], X[:, ds(C * m, C), :],
                                        spare[:, :].rearrange("p (c d) -> p c d", d=D),
                                        ALU.add).then_inc(s["spare_read"], 1)
                        dve.wait_ge(s["spare_read"], use("project"))
                        for c in range(C):
                            last = V.bn_stats(st2[:, c, :], x2[:, c, :])
                        own(last)
                    elif what == "moments":
                        dve.sem_inc(s["steps_dve"], 1)
                        for c in range(C):
                            last = V.bn_aggr(mv2[:, c, :], st2[:, c, :])
                        own(last)
                        own(V.tensor_tensor(ms2[:, :], mv2[:, :, 0], mv2[:, :, 0], ALU.mult))
                        V.scalar_tensor_tensor(out=ms2[:, :], in0=ms2[:, :], scalar=RMS_EPS, in1=mv2[:, :, 1],
                                               op0=ALU.add, op1=ALU.add).then_inc(s["ms2_ready"], 1)
                    elif what == "scale":
                        dve.wait_ge(s["r2_ready"], m + 1)
                        for c in range(C):
                            last = V.tensor_scalar(t[:, c, :], x2[:, c, :], r2[:, c:c + 1], None, ALU.mult)
                        last.then_inc(s["t_ready"], 1)
                    elif what == "split":
                        dve.wait_ge(s["spare_read"], use("tokensT"))
                        V.tensor_tensor(tTl[:, :], tT[:, :], tTh[:, :].bitcast(F32),
                                        ALU.subtract).then_inc(s["tT_split"], 1)
                    elif what == "rank":
                        dve.wait_ge(s["spare_full"], use("logits"))
                        V.tensor_copy(lg[:, :, :], spare[:, 0:C * NE].rearrange("p (c e) -> p c e", e=NE)
                                      ).then_inc(s["spare_read"], 1)
                        dve.wait_ge(s["spare_read"], use("logits"))
                        own(V.tensor_reduce(top1[:, :], lg[:, :, :], AX, ALU.max))
                        V.tensor_tensor(lgx[:, :, :], lg[:, :, :], top1[:, :].unsqueeze(2).broadcast_to([P, C, NE]),
                                        ALU.subtract).then_inc(s["lg_shift"], 1)
                    elif what == "compare":
                        other = lg[:, :, :].unsqueeze(2).broadcast_to([P, C, NE, NE])
                        this = lg[:, :, :].unsqueeze(3).broadcast_to([P, C, NE, NE])
                        V.tensor_tensor(before[:, :, :, :], other, this, ALU.is_gt)
                        own(V.tensor_tensor(equal[:, :, :, :], other, this, ALU.is_equal))
                        own(V.tensor_tensor(equal[:, :, :, :], equal[:, :, :, :],
                                            tri[:, :, :].unsqueeze(1).broadcast_to([P, C, NE, NE]), ALU.mult))
                    elif what == "count":
                        own(V.tensor_tensor(before[:, :, :, :], before[:, :, :, :], equal[:, :, :, :], ALU.add))
                        own(V.tensor_reduce(rank[:, :, :], before[:, :, :, :], AX, ALU.add))
                    elif what == "combine":
                        dve.wait_ge(s["lg_exp"], m + 1)
                        own(V.scalar_tensor_tensor(out=rank[:, :, :], in0=rank[:, :, :], scalar=2.0, in1=ex[:, :, :],
                                                   op0=ALU.is_lt, op1=ALU.mult))
                        own(V.tensor_reduce(wsum[:, :], rank[:, :, :], AX, ALU.add))
                        own(V.reciprocal(wrec[:, :], wsum[:, :]))
                        V.tensor_tensor(comb[:, :, :], rank[:, :, :],
                                        wrec[:, :].unsqueeze(2).broadcast_to([P, C, NE]),
                                        ALU.mult).then_inc(s["comb_ready"], 1)
                    elif what == "gate":
                        e, k = divmod(n, 2)
                        dve.wait_ge(s["tanh_ready"], 2 * NE * m + n + 1)
                        if e >= 2 and k == 0:
                            dve.wait_ge(s["y_ps"], NE * m + e - 1)
                        V.scalar_tensor_tensor(out=hid[:, e % 2, k, :], in0=tanh[:, n % 2, :], scalar=1.0,
                                               in1=hidden_bank(steps, n)[0], op0=ALU.add, op1=ALU.mult).then_inc(s["hid_ready"], 1)
                    elif what == "sum":
                        if n == 0:
                            dve.wait_ge(s["comb_ready"], m + 1)
                        wait(dve, "prod_used", NE * m + n - 1)
                        dve.wait_ge(s["y_ps"], NE * m + n + 1)
                        V.tensor_tensor(prod[:, n % 2, :, :], psY[:, :].rearrange("p (c d) -> p c d", d=D),
                                        comb[:, :, n:n + 1].broadcast_to([P, C, D]), ALU.mult).then_inc(s["y_used"], 1)
                    elif what == "norm":
                        dve.wait_ge(s["prod_used"], NE * m)
                        for c in range(C):
                            last = V.bn_stats(st3[:, c, :], acc[:, c, :])
                        own(last)
                        dve.sem_inc(s["steps_dve"], 1)
                        for c in range(C):
                            last = V.bn_aggr(mv3[:, c, :], st3[:, c, :])
                        own(last)
                        V.tensor_scalar(ve3[:, :], mv3[:, :, 1], LN_EPS, None, ALU.add).then_inc(s["ve3_ready"], 1)
                    elif what == "result":
                        dve.wait_ge(s["rs3_ready"], m)
                        dve.wait_ge(s["out_done"], 16 * m)
                        for c in range(C):
                            last = V.tensor_scalar(outb[:, c, :], acc[:, c, :], mv3[:, c, 0:1], rs3[:, c:c + 1],
                                                   ALU.subtract, ALU.mult)
                        last.then_inc(s["out_ready"], 1)

            own(V.memset(ks[:, :, :, :].bitcast(F32), 0.0))
            V.memset(ks[:, :, :, SHIFT:SHIFT + 2].bitcast(F32), 1.0)
            dve.wait_ge(s["w_ps"], 1)
            V.tensor_scalar(wqkv[:, D:3 * D], psS[:, 0, 0:2 * D], g1c[:, :], None, ALU.mult)
            V.tensor_scalar(wqkv[:, 0:D], wqkv[:, 0:D], g1c[:, :], MD ** -0.5, ALU.mult,
                            ALU.mult).then_inc(s["w_ready"], 1)
            V.memset(qs[:, :, :, :].bitcast(F32), 0.0).then_inc(s["const"], 1)
            dve.wait_ge(s["const"], 1)
            V.memset(outb[:, 0, 0:1], 0.0).then_inc(s["out_done"], 16)
            run(dve, trip, own)


OWN_PER_TRIP = 21


PER_TRIP = 0

INPUTS = ["x", "xT", "wqkvT", "woutT", "b_out", "ln_g", "ln_b", "w1gT", "b1g", "w2gT", "b2g"]
INPUTS2 = ["g2", "gate_w", "w1", "w2"]


def program(nc, ins, out):
    with ExitStack() as ctx:
        def sb(name, shape, dt=F32):
            return ctx.enter_context(nc.sbuf_tensor(name, shape, dt))

        keep = {
            "X": sb("X", [P, NC, D]),
            "qpad": sb("qpad", [P, MH, T], F32R),
            "ident": sb("ident", [P, P]),
            "identb": sb("identb", [P, P], BF16),
            "maskb": sb("maskb", [P, P], BF16),
            "tri": sb("tri", [P, NE, NE]),
            "r1": sb("r1", [P, NC]),
            "mhalf": sb("mhalf", [P, NC]),
        }
        keep.update(wqkv=sb("wqkv", [P, 3 * D]), wo=sb("wo", [P, D]), wd=sb("wd", [LAT, D]),
                    wu=sb("wu", [LAT, 2, D]), g1c=sb("g1c", [P, 1]))
        keep["loads"] = [(keep["wd"][:, :], ins["WdkvT"]), (keep["wu"][:, 0, :], ins["Wuk"]),
                         (keep["wu"][:, 1, :], ins["Wuv"]), (keep["g1c"][:, :], ins["g1"]),
                         (keep["wqkv"][:, 0:D], ins["Wq"]), (keep["wo"][:, :], ins["Wo"])]
        gated_attention(nc, keep, *(ins[k] for k in INPUTS))
        causal_attention_and_experts(nc, keep, *(ins[k] for k in INPUTS2), out)


def kernel(**inputs):
    import concourse.bacc as bacc
    from concourse.bass_utils import run_bass_kernel_spmd

    a = {k.split("_", 1)[1]: np.asarray(v) for k, v in inputs.items()}
    tokens = a["attn_x"]
    laid = {
        "x": tokens.reshape(NC, P, D).transpose(1, 0, 2),
        "xT": tokens.reshape(B * T, D).T,
        "wqkvT": a["attn_w_qkv"].T,
        "woutT": a["attn_w_out"].T,
        "b_out": a["attn_b_out"].reshape(1, D),
        "ln_g": a["attn_ln_g"].reshape(DH, 1),
        "ln_b": a["attn_ln_b"].reshape(DH, 1),
        "w1gT": a["attn_w1"].T,
        "b1g": a["attn_b1"].reshape(GH, 1),
        "w2gT": a["attn_w2"].T,
        "b2g": a["attn_b2"].reshape(1, 1).repeat(B, 0),
        "g1": a["ffn_g1"].reshape(D, 1),
        "Wq": a["ffn_Wq"],
        "WdkvT": a["ffn_Wdkv"].T,
        "Wuk": a["ffn_Wuk"],
        "Wuv": a["ffn_Wuv"],
        "Wo": a["ffn_Wo"],
        "g2": a["ffn_g2"].reshape(D, 1),
        "gate_w": a["ffn_gate_w"],
        "w1": a["ffn_w1"],
        "w2": a["ffn_w2"],
    }
    nc = bacc.Bacc("TRN2", target_bir_lowering=False, num_devices=1)
    arrays, ins = {}, {}
    for name, v in laid.items():
        arrays[f"in_{name}"] = v = np.ascontiguousarray(v)
        ins[name] = nc.dram_tensor(f"in_{name}", v.shape, mybir.dt.from_np(v.dtype), kind="ExternalInput").ap()
    out = nc.dram_tensor("out", tokens.shape, F32, kind="ExternalOutput").ap()
    program(nc, ins, out)
    r = run_bass_kernel_spmd(nc, [arrays], core_ids=[0])
    return r.results[0]["out"]
```
